# Optimizing a Trainium2 kernel written in Bass

```python
import numpy as np
import jax
import jax.numpy as jnp

def _softmax(x, axis=-1):
    return jax.nn.softmax(x, axis=axis)

def _gelu(x):
    return jax.nn.gelu(x, approximate=True)

def _silu(x):
    return jax.nn.silu(x)

def _sigmoid(x):
    return jax.nn.sigmoid(x)

def _layernorm(x, axis=-1, eps=1e-05):
    m = jnp.mean(x, axis=axis, keepdims=True)
    v = jnp.var(x, axis=axis, keepdims=True)
    return (x - m) / jnp.sqrt(v + eps)

def _scatter_add(tgt, idx, src, axis=0):
    return tgt.at[idx].add(src)

def _segment_sum(src, seg, n):
    return jax.ops.segment_sum(src, seg, n)
kernel_name = 'mk_gnn_preln_d4_gnn_r8_889290'

def setup_inputs(seed: int=0):
    np.random.seed(seed)
    _w = jnp.asarray

    def _rec_inputs():
        import jax
        import jax.numpy as jnp
        _gk = jax.random.key(seed)
        x = 0.4998 + 0.2887 * jax.random.normal(jax.random.fold_in(_gk, 1), (12500, 16), jnp.float32)
        _s = jax.random.randint(jax.random.fold_in(_gk, 2), (200000,), 0, 12500, jnp.int32)
        _d = jax.random.randint(jax.random.fold_in(_gk, 3), (200000,), 0, 12500, jnp.int32)
        _loop = jnp.arange(12500, dtype=jnp.int32)
        src = jnp.concatenate([_s, _d, _loop])
        dst = jnp.concatenate([_d, _s, _loop])
        _o = jnp.argsort(dst, stable=True)
        src = src[_o]
        dst = dst[_o]
        edge_attr_13 = 2.91757e-06 + 0.999892 * jax.random.normal(jax.random.fold_in(_gk, 12), (412500, 13), jnp.float32)
        edge_type_8 = jax.random.randint(jax.random.fold_in(_gk, 14), (412500,), 0, 8, jnp.int32)
        edge_weight = jax.random.uniform(jax.random.fold_in(_gk, 15), (412500,), jnp.float32, 0.0, 1)
        return (x, src, dst, edge_attr_13, edge_type_8, edge_weight)
    x, src, dst, edge_attr_13, edge_type_8, edge_weight = _rec_inputs()

    def _L0_gnn_setup():
        import jax, jax.numpy as jnp
        import numpy as np
        N_NODES = 12500
        N_EDGES = 400000
        DIM = 16
        B, K, C, D, E, H = (0.1, 5.0, 1.0, 5.0, 0.9, 0.1)
        E_ = E
        key = jax.random.key(seed)
        k1, k2, k3, k4 = jax.random.split(key, 4)
        x = jax.random.uniform(k1, (N_NODES, DIM), dtype=jnp.float32)
        edge_src = jax.random.randint(k2, (N_EDGES,), 0, N_NODES, dtype=jnp.int32)
        edge_dst = jax.random.randint(k3, (N_EDGES,), 0, N_NODES, dtype=jnp.int32)
        edge_vals = jax.random.uniform(k4, (N_EDGES,), dtype=jnp.float32)
        return {'x': x, 'edge_src': edge_src, 'edge_dst': edge_dst, 'edge_vals': edge_vals}
    _L0_gnn_all = _L0_gnn_setup()
    _L0_gnn_in = {k: v for k, v in _L0_gnn_all.items() if k in ()}
    del _L0_gnn_all

    def _L1_gnn_setup():
        import jax, jax.numpy as jnp
        import numpy as np
        NUM_ENTITIES = 12500
        NUM_RELATIONS = 8
        NUM_CLASSES = 16
        HIDDEN = 16
        NUM_EDGES = 400000

        def rgcn_conv(x, src, dst, edge_type, W, root, bias):
            num_nodes = x.shape[0]
            x_src = x[src]
            msg = jnp.zeros((src.shape[0], W.shape[2]), x.dtype)
            for r in range(NUM_RELATIONS):
                msg = msg + jnp.where((edge_type == r)[:, None], x_src @ W[r], jnp.zeros((), x.dtype))
            cnt = jnp.zeros((num_nodes, NUM_RELATIONS), x.dtype).at[dst, edge_type].add(1.0)
            norm = 1.0 / jnp.maximum(cnt[dst, edge_type], 1.0)
            agg = jax.ops.segment_sum(msg * norm[:, None], dst, num_segments=num_nodes)
            return agg + x @ root + bias
        key = jax.random.key(seed)
        ks = jax.random.split(key, 9)
        s = 1.0 / np.sqrt(HIDDEN)
        edge_index = jax.random.randint(ks[0], (2, NUM_EDGES), 0, NUM_ENTITIES, dtype=jnp.int32)
        edge_type = jax.random.randint(ks[1], (NUM_EDGES,), 0, NUM_RELATIONS, dtype=jnp.int32)
        return {'embed': jax.random.normal(ks[2], (NUM_ENTITIES, HIDDEN), jnp.float32), 'W1': jax.random.normal(ks[3], (NUM_RELATIONS, HIDDEN, HIDDEN), jnp.float32) * s, 'root1': jax.random.normal(ks[4], (HIDDEN, HIDDEN), jnp.float32) * s, 'b1': jnp.zeros((HIDDEN,), jnp.float32), 'W2': jax.random.normal(ks[5], (NUM_RELATIONS, HIDDEN, NUM_CLASSES), jnp.float32) * s, 'root2': jax.random.normal(ks[6], (HIDDEN, NUM_CLASSES), jnp.float32) * s, 'b2': jnp.zeros((NUM_CLASSES,), jnp.float32), 'edge_index': edge_index, 'edge_type': edge_type}
    _L1_gnn_all = _L1_gnn_setup()
    _L1_gnn_in = {k: v for k, v in _L1_gnn_all.items() if k in ('W1', 'root1', 'b1', 'W2', 'root2', 'b2')}
    del _L1_gnn_all

    def _L2_gnn_setup():
        import jax, jax.numpy as jnp
        import numpy as np
        N = 6250
        E = 100000
        NC = 16
        FDIM = 13
        HID = 32
        NREPEATS = 2

        def _gru_cell(x, h, w_ih, w_hh, b_ih, b_hh):
            gi = x @ w_ih.T + b_ih
            gh = h @ w_hh.T + b_hh
            i_r, i_z, i_n = jnp.split(gi, 3, axis=1)
            h_r, h_z, h_n = jnp.split(gh, 3, axis=1)
            r = jax.nn.sigmoid(i_r + h_r)
            z = jax.nn.sigmoid(i_z + h_z)
            n = jnp.tanh(i_n + r * h_n)
            return (1.0 - z) * n + z * h
        key = jax.random.key(seed)
        ks = jax.random.split(key, 10)
        hx = jax.random.normal(ks[0], (N, NC), dtype=jnp.float32)
        edgefeats = jax.random.normal(ks[1], (E, FDIM), dtype=jnp.float32)
        edge_src = jax.random.randint(ks[2], (E,), 0, N, dtype=jnp.int32)
        edge_dst = jax.random.randint(ks[3], (E,), 0, N, dtype=jnp.int32)
        fnet_w1 = jax.random.normal(ks[4], (FDIM, HID), dtype=jnp.float32) * (1.0 / np.sqrt(FDIM))
        fnet_b1 = jnp.zeros((HID,), dtype=jnp.float32)
        fnet_w2 = jax.random.normal(ks[5], (HID, NC * NC), dtype=jnp.float32) * (0.1 / np.sqrt(HID))
        fnet_b2 = jnp.zeros((NC * NC,), dtype=jnp.float32)
        gru_w_ih = jax.random.normal(ks[6], (3 * NC, NC), dtype=jnp.float32) * (1.0 / np.sqrt(NC))
        gru_w_hh = jax.random.normal(ks[7], (3 * NC, NC), dtype=jnp.float32) * (1.0 / np.sqrt(NC))
        gru_b_ih = jnp.zeros((3 * NC,), dtype=jnp.float32)
        gru_b_hh = jnp.zeros((3 * NC,), dtype=jnp.float32)
        return {'hx': hx, 'edgefeats': edgefeats, 'edge_src': edge_src, 'edge_dst': edge_dst, 'fnet_w1': fnet_w1, 'fnet_b1': fnet_b1, 'fnet_w2': fnet_w2, 'fnet_b2': fnet_b2, 'gru_w_ih': gru_w_ih, 'gru_w_hh': gru_w_hh, 'gru_b_ih': gru_b_ih, 'gru_b_hh': gru_b_hh}
    _L2_gnn_all = _L2_gnn_setup()
    _L2_gnn_in = {k: v for k, v in _L2_gnn_all.items() if k in ('fnet_w1', 'fnet_b1', 'fnet_w2', 'fnet_b2', 'gru_w_ih', 'gru_w_hh', 'gru_b_ih', 'gru_b_hh')}
    del _L2_gnn_all

    def _L3_gnn_setup():
        import jax, jax.numpy as jnp
        import numpy as np
        N_NODES = 12500
        key = jax.random.key(seed)
        k1, k2, k3 = jax.random.split(key, 3)
        features = jax.random.normal(k1, (N_NODES, 16), dtype=jnp.float32)
        src = jax.random.randint(k2, (625000,), 0, N_NODES, dtype=jnp.int64)
        dst = jax.random.randint(k3, (625000,), 0, N_NODES, dtype=jnp.int64)
        return {'features': features, 'src': src, 'dst': dst}
    _L3_gnn_all = _L3_gnn_setup()
    _L3_gnn_in = {k: v for k, v in _L3_gnn_all.items() if k in ()}
    del _L3_gnn_all
    return {'x': x, 'src': src, 'dst': dst, 'edge_attr_13': edge_attr_13, 'edge_type_8': edge_type_8, 'edge_weight': edge_weight, 'L1_gnn_W1': _L1_gnn_in['W1'], 'L1_gnn_root1': _L1_gnn_in['root1'], 'L1_gnn_b1': _L1_gnn_in['b1'], 'L1_gnn_W2': _L1_gnn_in['W2'], 'L1_gnn_root2': _L1_gnn_in['root2'], 'L1_gnn_b2': _L1_gnn_in['b2'], 'L2_gnn_fnet_w1': _L2_gnn_in['fnet_w1'], 'L2_gnn_fnet_b1': _L2_gnn_in['fnet_b1'], 'L2_gnn_fnet_w2': _L2_gnn_in['fnet_w2'], 'L2_gnn_fnet_b2': _L2_gnn_in['fnet_b2'], 'L2_gnn_gru_w_ih': _L2_gnn_in['gru_w_ih'], 'L2_gnn_gru_w_hh': _L2_gnn_in['gru_w_hh'], 'L2_gnn_gru_b_ih': _L2_gnn_in['gru_b_ih'], 'L2_gnn_gru_b_hh': _L2_gnn_in['gru_b_hh']}

def reference(x, src, dst, edge_attr_13, edge_type_8, edge_weight, L1_gnn_W1, L1_gnn_root1, L1_gnn_b1, L1_gnn_W2, L1_gnn_root2, L1_gnn_b2, L2_gnn_fnet_w1, L2_gnn_fnet_b1, L2_gnn_fnet_w2, L2_gnn_fnet_b2, L2_gnn_gru_w_ih, L2_gnn_gru_w_hh, L2_gnn_gru_b_ih, L2_gnn_gru_b_hh):
    import jax
    import jax.numpy as jnp

    def _L0_gnn_ref(x, edge_src, edge_dst, edge_vals):
        import jax, jax.numpy as jnp
        import numpy as np
        N_NODES = 12500
        N_EDGES = 400000
        DIM = 16
        B, K, C, D, E, H = (0.1, 5.0, 1.0, 5.0, 0.9, 0.1)
        E_ = E
        n = x.shape[0]
        f = B + x * (1.0 - x / K) * (x / C - 1.0)
        xi = x[edge_src]
        xj = x[edge_dst]
        msg = edge_vals[:, None] * xi * xj / (D + E_ * xi + H * xj)
        f = f + jax.ops.segment_sum(msg, edge_src, num_segments=n)
        return f

    def _L1_gnn_ref(embed, W1, root1, b1, W2, root2, b2, edge_index, edge_type):
        import jax, jax.numpy as jnp
        import numpy as np
        NUM_ENTITIES = 12500
        NUM_RELATIONS = 8
        NUM_CLASSES = 16
        HIDDEN = 16
        NUM_EDGES = 400000

        def rgcn_conv(x, src, dst, edge_type, W, root, bias):
            num_nodes = x.shape[0]
            x_src = x[src]
            msg = jnp.zeros((src.shape[0], W.shape[2]), x.dtype)
            for r in range(NUM_RELATIONS):
                msg = msg + jnp.where((edge_type == r)[:, None], x_src @ W[r], jnp.zeros((), x.dtype))
            cnt = jnp.zeros((num_nodes, NUM_RELATIONS), x.dtype).at[dst, edge_type].add(1.0)
            norm = 1.0 / jnp.maximum(cnt[dst, edge_type], 1.0)
            agg = jax.ops.segment_sum(msg * norm[:, None], dst, num_segments=num_nodes)
            return agg + x @ root + bias
        src, dst = (edge_index[0], edge_index[1])
        h = rgcn_conv(embed, src, dst, edge_type, W1, root1, b1)
        h = jax.nn.relu(h)
        h = rgcn_conv(h, src, dst, edge_type, W2, root2, b2)
        return jax.nn.log_softmax(h, axis=1)

    def _L2_gnn_ref(hx, edgefeats, edge_src, edge_dst, fnet_w1, fnet_b1, fnet_w2, fnet_b2, gru_w_ih, gru_w_hh, gru_b_ih, gru_b_hh):
        import jax, jax.numpy as jnp
        import numpy as np
        N = 6250
        E = 100000
        NC = 16
        FDIM = 13
        HID = 32
        NREPEATS = 2

        def _gru_cell(x, h, w_ih, w_hh, b_ih, b_hh):
            gi = x @ w_ih.T + b_ih
            gh = h @ w_hh.T + b_hh
            i_r, i_z, i_n = jnp.split(gi, 3, axis=1)
            h_r, h_z, h_n = jnp.split(gh, 3, axis=1)
            r = jax.nn.sigmoid(i_r + h_r)
            z = jax.nn.sigmoid(i_z + h_z)
            n = jnp.tanh(i_n + r * h_n)
            return (1.0 - z) * n + z * h
        n_nodes, nc = hx.shape
        w = jax.nn.relu(edgefeats @ fnet_w1 + fnet_b1) @ fnet_w2 + fnet_b2
        W = w.reshape(-1, nc, nc)
        deg = jax.ops.segment_sum(jnp.ones((edge_dst.shape[0],), hx.dtype), edge_dst, num_segments=n_nodes)
        inv_deg = 1.0 / jnp.maximum(deg, 1.0)
        for _ in range(NREPEATS):
            xj = hx[edge_src]
            m = jnp.einsum('ei,eio->eo', xj, W)
            agg = jax.ops.segment_sum(m, edge_dst, num_segments=n_nodes)
            agg = agg * inv_deg[:, None]
            hx = _gru_cell(agg, hx, gru_w_ih, gru_w_hh, gru_b_ih, gru_b_hh)
        return hx

    def _L3_gnn_ref(features, src, dst):
        import jax, jax.numpy as jnp
        import numpy as np
        N_NODES = 12500
        n = features.shape[0]
        ones = jnp.ones(src.shape[0], dtype=features.dtype)
        out_deg = jnp.zeros(n, dtype=features.dtype).at[src].add(ones)
        out_deg = jnp.clip(out_deg, 1.0, None)
        in_deg = jnp.zeros(n, dtype=features.dtype).at[dst].add(ones)
        in_deg = jnp.clip(in_deg, 1.0, None)
        x = features * (out_deg ** (-0.5))[:, None]
        agg = jnp.zeros_like(features).at[dst].add(x[src])
        return agg * (in_deg ** (-0.5))[:, None]
    edge_index = jnp.stack([src, dst])
    h = jnp.maximum(_layernorm(x, axis=-1), 0.0)
    x = x + _L0_gnn_ref(h, src, dst, edge_weight)
    h = jnp.maximum(_layernorm(x, axis=-1), 0.0)
    x = x + _L1_gnn_ref(h, L1_gnn_W1, L1_gnn_root1, L1_gnn_b1, L1_gnn_W2, L1_gnn_root2, L1_gnn_b2, edge_index, edge_type_8)
    h = jnp.maximum(_layernorm(x, axis=-1), 0.0)
    x = x + _L2_gnn_ref(h, edge_attr_13, src, dst, L2_gnn_fnet_w1, L2_gnn_fnet_b1, L2_gnn_fnet_w2, L2_gnn_fnet_b2, L2_gnn_gru_w_ih, L2_gnn_gru_w_hh, L2_gnn_gru_b_ih, L2_gnn_gru_b_hh)
    h = jnp.maximum(_layernorm(x, axis=-1), 0.0)
    x = x + _L3_gnn_ref(h, src, dst)
    return x

_drawn_inputs = setup_inputs


def setup_inputs(seed=0):
    import zlib

    import numpy as np

    out = dict(_drawn_inputs(seed))
    spreads = {'L1_gnn_b1': (0.0, 0.1),
     'L1_gnn_b2': (0.0, 0.479),
     'L2_gnn_fnet_b1': (0.0, 2.0),
     'L2_gnn_fnet_b2': (0.0, 0.341),
     'L2_gnn_gru_b_ih': (0.0, 2.0),
     'L2_gnn_gru_b_hh': (0.0, 2.0)}
    factors = {'edge_attr_13': 8.0,
     'L2_gnn_fnet_w1': 8.0,
     'L2_gnn_fnet_w2': 6.666,
     'L2_gnn_gru_w_ih': 3.541,
     'L2_gnn_gru_w_hh': 4.208}
    for name, (base, spread) in spreads.items():
        noise = np.random.default_rng([zlib.crc32(name.encode()), seed]).standard_normal(out[name].shape)
        drawn = base * np.exp(spread * noise) if base else spread * noise
        out[name] = jnp.asarray(drawn.astype(out[name].dtype))
    for name, factor in factors.items():
        out[name] = (out[name] * factor).astype(out[name].dtype)
    return out
```

```python
from contextlib import ExitStack

import concourse.bass as bass
from concourse import mybir

F32 = mybir.dt.float32
I32 = mybir.dt.int32
BF16 = mybir.dt.bfloat16
ALU = mybir.AluOpType
ACT = mybir.ActivationFunctionType
AX = mybir.AxisListType

P = 128
N, E = 12500, 412500
F = 16
R = 8
FD, HID = 13, 32
NJ = -(-N // P)
NPAD = NJ * P
C = 52
CHUNKS = 62
PAIRS = CHUNKS // 2
T = C * CHUNKS
EP = T * P
assert EP >= E and EP - E < 4 * P and NPAD > N
HALF = C // 2
G = 7
GROUPS = NJ // G
Q = 4
TILES = C // Q
NE = F + R
ACC = F + 1
SET = 13
SETS = C // SET
assert SETS % 2 == 0
BATCHES = [range(a, min(a + 4, TILES)) for a in range(0, TILES, 4)]
GATHERS = 16 * C
EPS = 1e-5
BIG = 9408


class Steps:

    def __init__(self, eng, sem):
        self.eng, self.sem, self.n, self.t, self.per = eng, sem, 0, None, 0

    def did(self, ins):
        ins.then_inc(self.sem, 1)
        self.n += 1

    def settle(self):
        at = self.n if self.t is None else self.t * self.per + (self.n - self.per)
        self.eng.wait_ge(self.sem, at)

    def do(self, ins):
        self.did(ins)
        self.settle()


def loop_pairs(eng, body, steps=None, end=PAIRS):
    n0 = steps.n if steps else 0
    body(0, True)
    if steps:
        steps.per = steps.n - n0
    with eng.Fori(1, end) as t:
        if steps:
            steps.t = t
            n1 = steps.n
        body(t, False)
        if steps:
            assert steps.n - n1 == steps.per
            steps.t = None
            steps.n += (end - 2) * steps.per


def gnn_kernel(nc, x, src, dst, edge_attr, edge_type, edge_weight, W1, root1, b1, W2, root2, b2,
               fw1, fb1, fw2, fb2, w_ih, w_hh, b_ih, b_hh, out):
    ctx = ExitStack()
    with ctx:
        ctx.enter_context(nc.allow_non_contiguous_dma(reason="small weights turned while they load"))

        def sb(name, shape, dt=F32):
            return ctx.enter_context(nc.sbuf_tensor(name, shape, dt))

        def ps(name, width):
            return ctx.enter_context(nc.psum_tensor(name, [P, width], F32))

        def sem(name):
            return ctx.enter_context(nc.semaphore(name))

        def dram(name, shape):
            return nc.dram_tensor(name, shape, F32).ap()

        h_rows = dram("h_rows", (NPAD, F))
        rel_rows = dram("rel_rows", (NPAD * R, F))
        pair_rows = dram("pair_rows", (NPAD, 2 * F))
        xi_rows = dram("xi_rows", (EP, F))
        seg_rows = dram("seg_rows", (EP, F))
        type_rows = dram("type_rows", (EP, R))
        spread_rows = dram("spread_rows", (EP + NPAD, NE))
        node_rows = dram("node_rows", (NPAD, NE))
        count_row = dram("count_row", (NJ, P))
        accs = [dram(f"acc{r}", (NPAD + P, ACC)) for r in range(2 * SET)]

        SRC, RIDX = sb("SRC", [P, T], I32), sb("RIDX", [P, T], I32)
        SAME, NORM = sb("SAME", [P, T]), sb("NORM", [P, T])
        X, H, TA, TB, AGG = (sb(n, [P, NJ * F]) for n in ("X", "H", "TA", "TB", "AGG"))
        ROOT = sb("ROOT", [P, NJ * F])
        CNT, END, START = sb("CNT", [P, NJ]), sb("END", [P, NJ], I32), sb("START", [P, NJ], I32)
        FULL, OUTDEG, NA, NB = (sb(n, [P, NJ]) for n in ("FULL", "OUTDEG", "NA", "NB"))
        big = sb("big", [P, BIG])
        GB = [sb(f"GB{h}", [P, C * 2 * F]) for h in range(2)]
        OS = [sb(f"OS{h}", [P, C * NE]) for h in range(2)]
        IN = [sb(f"IN{h}", [P, C * F]) for h in range(2)]
        ROWS = [sb(f"ROWS{h}", [P, C * ACC]) for h in range(2)]
        IDX = [sb(f"IDX{h}", [P, C], I32) for h in range(2)]
        EDST = [sb(f"EDST{h}", [P, C], I32) for h in range(2)]
        ETYP = [sb(f"ETYP{h}", [P, C], I32) for h in range(2)]
        EWT = [sb(f"EWT{h}", [P, C]) for h in range(2)]
        KEY, DUP, KT = (sb(n, [P, C]) for n in ("KEY", "DUP", "KT"))
        LOI, HII = sb("LOI", [P, C], I32), sb("HII", [P, C], I32)
        LOB, HIB = sb("LOB", [P, C], BF16), sb("HIB", [P, C], BF16)
        TH = sb("TH", [P, C * R])
        ROWI, COLI = sb("ROWI", [P, 1], I32), sb("COLI", [P, P], I32)
        ROWF, COLF = sb("ROWF", [P, 1]), sb("COLF", [P, P])
        COLB = sb("COLB", [P, P], BF16)
        NONE_HOT = sb("NONE_HOT", [P, P])
        IDENT, LOWER, UPPER = sb("IDENT", [P, P]), sb("LOWER", [P, P]), sb("UPPER", [P, P])
        EDGES = sb("EDGES", [P, 4], I32)
        SMALL = sb("SMALL", [P, 16])
        FIRSTROW, DST0 = sb("FIRSTROW", [P, 1], I32), sb("DST0", [P, 1], I32)
        FIRST = sb("FIRST", [P, NE])
        CO16, A16 = sb("CO16", [P, F]), sb("A16", [P, F])
        CONT_T, A_T, B_T, CARRY_T = (sb(n, [F, P]) for n in ("CONT_T", "A_T", "B_T", "CARRY_T"))
        LAST, CARRY = sb("LAST", [P, F]), sb("CARRY", [P, F])
        BD = {name: sb(f"BD_{name}", [G * F, G * w]) for name, w in
              (("rel", R * F), ("root", F), ("b2", F), ("ih", 3 * F), ("hh", 3 * F))}
        HT = sb("HT", [G * F, P])
        B1, B2 = sb("B1", [P, F]), sb("B2", [P, F])
        BIH, BHH = sb("BIH", [P, 3 * F]), sb("BHH", [P, 3 * F])
        FW1 = sb("FW1", [Q * FD, Q * HID])
        FB1 = sb("FB1", [P, 1])
        FW2IO, FW2 = sb("FW2IO", [P, F * F]), sb("FW2", [P, Q * F * F])
        AT, HIDT = sb("AT", [Q * FD, 4 * P]), sb("HIDT", [P, 4 * P])

        psW = [ps(f"psW{i}", 2 * 512) for i in range(2)]
        psM = ps("psM", 2 * 512)
        psT, psH = ps("psT", 512), ps("psH", 512)

        dst_all = big[:, 0:T].bitcast(I32)
        typ_all = big[:, T:2 * T].bitcast(I32)
        hot_w = HALF * P // 2
        hoth_w = HALF * NJ // 2
        hot_lo = [big[:, i * hot_w:(i + 1) * hot_w].bitcast(BF16).rearrange("p (c k) -> p c k", c=HALF) for i in range(2)]
        hot_hi = [big[:, 2 * hot_w + i * hoth_w:2 * hot_w + (i + 1) * hoth_w].bitcast(BF16)
                  .rearrange("p (c k) -> p c k", c=HALF) for i in range(2)]
        zeros = TB[:, 0:C * NE]
        meq = big[:, 0:C * P].rearrange("p (c k) -> p c k", c=C)
        meq_low = big[:, C * P:C * P + Q * P].rearrange("p (c k) -> p c k", c=Q)
        msg = big[:, C * P + Q * P:C * P + Q * P + C * ACC].rearrange("p (c k) -> p c k", c=C)
        den = GB[0]
        acc_in = [big[:, r * NJ * ACC:(r + 1) * NJ * ACC] for r in range(4)]
        acc_sum = big[:, 4 * NJ * ACC:5 * NJ * ACC]
        node_ext = big[:, 0:NJ * NE].rearrange("p (j k) -> p j k", j=NJ)
        type_cnt = big[:, NJ * NE:NJ * (NE + R)]
        stage = [big[:, i * G * R * F:(i + 1) * G * R * F] for i in range(2)]
        pair_tab = big[:, 0:NJ * 2 * F].rearrange("p (j k) -> p j k", j=NJ)
        prod = [big[:, i * Q * F * F:(i + 1) * Q * F * F] for i in range(3)]
        m_edge = big[:, 3 * Q * F * F:3 * Q * F * F + C * F].rearrange("p (c k) -> p c k", c=C)
        GI = big[:, 0:NJ * 3 * F].rearrange("p (j k) -> p j k", j=NJ)
        GH = big[:, NJ * 3 * F:2 * NJ * 3 * F].rearrange("p (j k) -> p j k", j=NJ)

        def node3(t, w=F):
            return t[:, 0:NJ * w].rearrange("p (j k) -> p j k", j=NJ)

        def cols(t, w):
            return t[:, 0:C * w].rearrange("p (c k) -> p c k", c=C)

        def spread(col, n, w):
            return col.unsqueeze(2).to_broadcast([P, n, w])

        def over(row, n, w):
            return row.unsqueeze(1).to_broadcast([P, n, w])

        PASSES = ["xi", "conv1", "conv2", "edge1", "edge2", "sum3"]
        idx_ready = {q: sem(f"{q}_idx_ready") for q in PASSES}
        gathered = {q: [sem(f"{q}_gathered{h}") for h in range(2)] for q in PASSES}
        scanned = {q: sem(f"{q}_scanned") for q in PASSES}
        stored = {q: [sem(f"{q}_stored{h}") for h in range(2)] for q in PASSES}
        held = {e: sem(f"held_{e}") for e in ("pool", "act", "pe", "dve", "sp")}
        edges_in, x_in, weights_in = sem("edges_in"), sem("x_in"), sem("weights_in")
        conv2_weights_in = sem("conv2_weights_in")
        iota_done, consts_ready, zero_ready = sem("iota_done"), sem("consts_ready"), sem("zero_ready")
        accs_cleared, spread_cleared = sem("accs_cleared"), [sem(f"spread_cleared{h}") for h in range(2)]
        prepared = sem("prepared")
        dve_step = sem("dve_step")
        to_act, from_act = sem("to_act"), sem("from_act")
        table_ready, table_stored = sem("table_ready"), sem("table_stored")
        hist_in = [sem(f"hist_in{h}") for h in range(2)]
        hist_read = sem("hist_read")
        hot_ready, hot_used = sem("hot_ready"), sem("hot_used")
        types_stored = [sem(f"types_stored{h}") for h in range(2)]
        hist_done, hist_copied, hist_stored, count_in = sem("hist_done"), sem("hist_copied"), sem("hist_stored"), sem("count_in")
        totals_ready, offsets_ready = sem("totals_ready"), sem("offsets_ready")
        cont_ready, cont_turned = sem("cont_ready"), sem("cont_turned")
        last_ready, last_turned, carry_ready, carry_turned, carry_out = (
            sem(n) for n in ("last_ready", "last_turned", "carry_ready", "carry_turned", "carry_out"))
        carry_added, ends_in = sem("carry_added"), sem("ends_in")
        starts_out, first_in = sem("starts_out"), sem("first_in")
        msg_in = [sem(f"msg_in{h}") for h in range(2)]
        msg_read, msg_scanned = sem("msg_read"), sem("msg_scanned")
        key_ready, key_spread, eq_done, msg_ready, key_used = (
            sem(n) for n in ("key_ready", "key_spread", "eq_done", "msg_ready", "key_used"))
        merged, rows_ready, scat_idx_ready = sem("merged"), sem("rows_ready"), sem("scat_idx_ready")
        scattered = [sem(f"scattered{i}") for i in range(2)]
        acc_loaded, acc_used = [sem(f"acc_loaded{i}") for i in range(4)], sem("acc_used")
        lin_in, lin_turned, lin_copied, lin_mult, lin_out = (
            sem(n) for n in ("lin_in", "lin_turned", "lin_copied", "lin_mult", "lin_out"))
        rel_stored = [sem(f"rel_stored{i}") for i in range(2)]
        attr_in = [sem(f"attr_in{h}") for h in range(2)]
        attr_turned, attr_copied, hid_done, hid_relu, w_ready, w_used, m_reduced = (
            sem(n) for n in ("attr_turned", "attr_copied", "hid_done", "hid_relu", "w_ready", "w_used", "m_reduced"))
        out_ready, out_stored = sem("out_ready"), sem("out_stored")

        LIN = ["rel", "root", "rel", "root", "b2", "ih", "hh", "b2", "ih", "hh"]
        LIN_OF = {"conv1": 0, "conv2": 2, "edge1": 4, "gru1": 5, "edge2": 7, "gru2": 8}

        N_WEIGHTS = 16 * (2 * G + 1 + 3 + 3 * G + 3 * Q)
        fw2_ready, first_placed = sem("fw2_ready"), sem("first_placed")

        def hold(eng, name, s, value):
            eng.wait_ge(s, value)
            eng.sem_inc(held[name], 1)

        block = ctx.enter_context(nc.Block())

        @block.sync
        def _(sp):
            def by_part(a):
                return a.rearrange("(p c) -> p c", p=P)

            sp.dma_start(SRC[:, :], by_part(src)).then_inc(edges_in, 16)
            sp.dma_start(dst_all, by_part(dst)).then_inc(edges_in, 16)
            sp.dma_start(typ_all, by_part(edge_type)).then_inc(edges_in, 16)
            sp.wait_ge(iota_done, 1)
            sp.dma_start(EDGES[1:P, 0:1], by_part(dst)[0:P - 1, 0:1]).then_inc(edges_in, 16)
            sp.dma_start(EDGES[1:P, 1:2], by_part(dst)[0:P - 1, T - 1:T]).then_inc(edges_in, 16)
            sp.dma_start(X[:, :], x.rearrange("(p j) f -> p (j f)", p=P)).then_inc(x_in, 16)
            sp.wait_ge(zero_ready, 1)
            n = 0

            def put(o, i, s=weights_in):
                sp.dma_start(o, i).then_inc(s, 16)

            def conv_weights(W, root, bias, B, s):
                for j in range(G):
                    rows = slice(j * F, (j + 1) * F)
                    put(BD["rel"][rows, j * R * F:(j + 1) * R * F].rearrange("i (r o) -> i r o", r=R),
                        W.rearrange("r i o -> i r o"), s)
                    put(BD["root"][rows, j * F:(j + 1) * F], root, s)
                if bias is not None:
                    put(B[:, :], bias.unsqueeze(0).to_broadcast([P, F]), s)

            conv_weights(W1, root1, b1, B1, weights_in)
            put(B2[:, :], b2.unsqueeze(0).to_broadcast([P, F]))
            put(BIH[:, :], b_ih.unsqueeze(0).to_broadcast([P, 3 * F]))
            put(BHH[:, :], b_hh.unsqueeze(0).to_broadcast([P, 3 * F]))
            for j in range(G):
                rows = slice(j * F, (j + 1) * F)
                put(BD["b2"][rows, j * F:(j + 1) * F], fb2.rearrange("(i o) -> i o", i=F))
                put(BD["ih"][rows, j * 3 * F:(j + 1) * 3 * F], w_ih.rearrange("o i -> i o"))
                put(BD["hh"][rows, j * 3 * F:(j + 1) * 3 * F], w_hh.rearrange("o i -> i o"))
            for q in range(Q):
                put(FW1[q * FD:(q + 1) * FD, q * HID:(q + 1) * HID], fw1)
                put(FB1[q * HID:(q + 1) * HID, :], fb1.unsqueeze(1))
                put(FW2IO[q * HID:(q + 1) * HID, :], fw2)

            def store_table(n, rows, tile):
                sp.wait_ge(table_ready, n)
                sp.dma_start(rows.rearrange("(p j) d -> p (j d)", p=P), tile).then_inc(table_stored, 16)

            def edge_cols(a, k, w):
                return a.rearrange("(p c) d -> p c d", p=P)[:, bass.ds(k * C, C), :].rearrange("p c d -> p (c d)") if w else \
                    a.rearrange("(p c) -> p c", p=P)[:, bass.ds(k * C, C)]

            def xi_pair(t, first):
                for h in range(2):
                    k = t * 2 + h
                    if not first:
                        hold(sp, "sp", hist_read, k - 1)
                    sp.dma_start(EDST[h][:, :], edge_cols(dst, k, 0)).then_inc(hist_in[h], 16)
                    sp.dma_start(ETYP[h][:, :], edge_cols(edge_type, k, 0)).then_inc(hist_in[h], 16)
                    sp.dma_start(edge_cols(spread_rows[0:EP, :], k, 1), zeros).then_inc(spread_cleared[h], 16)
                for h in range(2):
                    k = t * 2 + h
                    hold(sp, "sp", scanned["xi"], k + 1)
                    sp.dma_start(edge_cols(type_rows, k, 1), OS[h][:, 0:C * R]).then_inc(types_stored[h], 16)
                    hold(sp, "sp", gathered["xi"][h], (t + 1) * GATHERS)
                    sp.dma_start(edge_cols(xi_rows, k, 1), GB[h][:, 0:C * F]).then_inc(stored["xi"][h], 16)

            store_table(1, h_rows, H[:, :])
            sp.wait_ge(zero_ready, 2)
            loop_pairs(sp, xi_pair)
            for r in range(2 * SET):
                sp.dma_start(accs[r].rearrange("(p j) d -> p j d", p=P), over(zeros[:, 0:ACC], NJ + 1, ACC)).then_inc(accs_cleared, 16)
            for h in range(2):
                sp.wait_ge(stored["xi"][h], 16 * PAIRS)
                sp.wait_ge(types_stored[h], 16 * PAIRS)
            sp.wait_ge(hist_copied, 1)
            sp.dma_start(count_row, HIDT[0:NJ, 0:P]).then_inc(hist_stored, 16)
            sp.wait_ge(hist_stored, 16)
            sp.dma_start(CNT[:, :], count_row.rearrange("a b -> (a b)").rearrange("(p j) -> p j", p=P)).then_inc(count_in, 16)
            store_table(2, node_rows, big[:, 0:NJ * NE])

            def msg_pair(t, first):
                for h in range(2):
                    k = t * 2 + h
                    if not first:
                        hold(sp, "sp", msg_read, k - 1)
                    sp.dma_start(GB[h][:, 0:C * NE], edge_cols(spread_rows[0:EP, :], k, 1)).then_inc(msg_in[h], 16)
                    sp.dma_start(IN[h][:, :], edge_cols(xi_rows, k, 1)).then_inc(msg_in[h], 16)
                    sp.dma_start(EWT[h][:, :], edge_cols(edge_weight, k, 0)).then_inc(msg_in[h], 16)
                    sp.dma_start(ETYP[h][:, :], edge_cols(edge_type, k, 0)).then_inc(msg_in[h], 16)

            sp.wait_ge(starts_out, 16 * NJ)
            loop_pairs(sp, msg_pair)
            for i in range(2):
                sp.wait_ge(scattered[i], 8 * C * CHUNKS)
            for r in range(2 * SET):
                if r >= 4:
                    sp.wait_ge(acc_used, r - 3)
                sp.dma_start(acc_in[r % 4], accs[r][0:NPAD, :].rearrange("(p j) d -> p (j d)", p=P)).then_inc(acc_loaded[r % 4], 16)

            def store_rel(call):
                for g in range(GROUPS):
                    sp.wait_ge(lin_out, call * GROUPS + g + 1)
                    sp.dma_start(rel_rows.rearrange("(p j r) d -> p j (r d)", p=P, r=R)[:, g * G:(g + 1) * G, :],
                                 stage[g % 2].rearrange("p (j k) -> p j k", j=G)).then_inc(rel_stored[g % 2], 16)

            def store_pass(name):
                def pair(t, first):
                    for h in range(2):
                        hold(sp, "sp", scanned[name], t * 2 + h + 1)
                        sp.dma_start(edge_cols(seg_rows, t * 2 + h, 1), OS[h][:, 0:C * F]).then_inc(stored[name][h], 16)
                return pair

            store_rel(LIN_OF["conv1"])
            loop_pairs(sp, store_pass("conv1"))
            sp.wait_ge(lin_mult, 2 * GROUPS)
            conv_weights(W2, root2, None, None, conv2_weights_in)
            store_rel(LIN_OF["conv2"])
            loop_pairs(sp, store_pass("conv2"))

            def edge_pass(name, n):
                def load(k, h, t):
                    sp.dma_start(IN[h][:, 0:C * FD], edge_cols(edge_attr, k, 1)).then_inc(attr_in[h], 16)

                def pair(t, first):
                    for h in range(2):
                        hold(sp, "sp", attr_turned, (t * 2 + h + 1) * len(BATCHES) + n * CHUNKS * len(BATCHES))
                        load(t * 2 + h + 2, h, t)
                        hold(sp, "sp", scanned[name], t * 2 + h + 1)
                        sp.dma_start(edge_cols(seg_rows, t * 2 + h, 1), OS[h][:, 0:C * F]).then_inc(stored[name][h], 16)

                for h in range(2):
                    load(h, h, 0)
                loop_pairs(sp, pair, end=PAIRS - 1)
                for h in range(2):
                    sp.wait_ge(scanned[name], CHUNKS - 1 + h)
                    sp.dma_start(edge_cols(seg_rows, CHUNKS - 2 + h, 1), OS[h][:, 0:C * F]).then_inc(stored[name][h], 16)

            store_table(3, pair_rows, big[:, 0:NJ * 2 * F])
            edge_pass("edge1", 0)
            store_table(4, pair_rows, big[:, 0:NJ * 2 * F])
            edge_pass("edge2", 1)
            store_table(5, h_rows, H[:, :])
            loop_pairs(sp, store_pass("sum3"))
            sp.wait_ge(out_ready, 1)
            full = N // NJ
            sp.dma_start(out[0:full * NJ, :].rearrange("(p j) f -> p (j f)", p=full), X[0:full, :]).then_inc(out_stored, 16)
            sp.dma_start(out[full * NJ:N, :].rearrange("(a j) f -> a (j f)", a=1),
                         X[full:full + 1, 0:(N - full * NJ) * F]).then_inc(out_stored, 16)
            sp.wait_ge(out_stored, 32)

        @block.gpsimd
        def _(pool):
            nc.gpsimd.memset(EDGES[:, 0:1], -2).then_inc(held["pool"], 1)
            nc.gpsimd.memset(EDGES[:, 1:2], -1).then_inc(held["pool"], 1)
            nc.gpsimd.iota(ROWI[:, :], pattern=[[0, 1]], base=0, channel_multiplier=1).then_inc(held["pool"], 1)
            nc.gpsimd.iota(COLI[:, :], pattern=[[1, P]], base=0, channel_multiplier=0).then_inc(held["pool"], 1)
            pool.wait_ge(held["pool"], 4)
            pool.sem_inc(iota_done, 1)

            def gather(rows, w, slot, c, idx):
                return nc.gpsimd.indirect_dma_start(
                    out=slot[:, c * w:(c + 1) * w], out_offset=None, in_=rows[:, :],
                    in_offset=bass.IndirectOffsetOnAxis(ap=idx, axis=0))

            def scatter(rows, w, slot, c, idx, op=ALU.bypass):
                return nc.gpsimd.indirect_dma_start(
                    out=rows[:, :], out_offset=bass.IndirectOffsetOnAxis(ap=idx, axis=0),
                    in_=slot[:, c * w:(c + 1) * w], in_offset=None, compute_op=op)

            def gather_pass(name, rows, w, freed):
                def pair(t, first):
                    for h in range(2):
                        k = t * 2 + h
                        hold(pool, "pool", idx_ready[name], k + 1)
                        if not first:
                            if freed is None:
                                hold(pool, "pool", stored[name][h], t * 16)
                            else:
                                hold(pool, "pool", freed[0], k - 1)
                        for c in range(C):
                            gather(rows, w, GB[h], c, IDX[h][:, c:c + 1]).then_inc(gathered[name][h], 16)
                return pair

            carries = [0]

            def finish_segments(name, rows, w, dest):
                carries[0] += 1
                n = carries[0]
                pool.wait_ge(carry_out, n)
                for h in range(2):
                    pool.wait_ge(types_stored[h] if name == "types" else stored[name][h], 16 * PAIRS)
                scatter(rows, w, CARRY, 0, FIRSTROW[:, 0:1], ALU.add).then_inc(carry_added, 16)
                pool.wait_ge(carry_added, 16 * n)
                for j in range(NJ):
                    gather(rows, w, dest, j, END[:, j:j + 1]).then_inc(ends_in, 16)

            pool.wait_ge(table_stored, 16)
            loop_pairs(pool, gather_pass("xi", h_rows, F, None))
            finish_segments("types", type_rows, R, type_cnt)
            for h in range(2):
                pool.wait_ge(spread_cleared[h], 16 * PAIRS)
            pool.wait_ge(table_stored, 32)
            gather(node_rows, NE, FIRST, 0, DST0[:, 0:1]).then_inc(first_in, 16)
            for j in range(NJ):
                scatter(spread_rows, NE, big, j, START[:, j:j + 1]).then_inc(starts_out, 16)

            def scatter_pair(t, first):
                for h in range(2):
                    hold(pool, "pool", rows_ready, t * 2 + h + 1)
                    hold(pool, "pool", scat_idx_ready, t * 2 + h + 1)
                    for g in range(SETS):
                        before = (h * SETS + g) // 2
                        if not (first and before == 0):
                            hold(pool, "pool", scattered[g % 2], t * 16 * C + before * 16 * SET)
                        for q in range(SET):
                            c = g * SET + q
                            scatter(accs[(g % 2) * SET + q], ACC, ROWS[h], c, IDX[h][:, c:c + 1], ALU.add)\
                                .then_inc(scattered[g % 2], 16)

            pool.wait_ge(accs_cleared, 16 * 2 * SET)
            loop_pairs(pool, scatter_pair)

            for name in ("conv1", "conv2"):
                for i in range(2):
                    pool.wait_ge(rel_stored[i], 16 * GROUPS // 2 * (1 if name == "conv1" else 2))
                loop_pairs(pool, gather_pass(name, rel_rows, F, [scanned[name]]))
                finish_segments(name, seg_rows, F, AGG)
            for n, name in ((3, "edge1"), (4, "edge2")):
                pool.wait_ge(table_stored, 16 * n)
                loop_pairs(pool, gather_pass(name, pair_rows, 2 * F, [scanned[name]]))
                finish_segments(name, seg_rows, F, AGG)
            pool.wait_ge(table_stored, 16 * 5)
            loop_pairs(pool, gather_pass("sum3", h_rows, F, [scanned["sum3"]]))
            finish_segments("sum3", seg_rows, F, AGG)

        @block.scalar
        def _(act):
            asked = [0]
            lins = [0]

            def function(o, i, f, **kw):
                asked[0] += 1
                act.wait_ge(to_act, asked[0])
                nc.scalar.activation(o, i, f, **kw).then_inc(from_act, 1)

            def index_pass(name, table):
                def pair(t, first):
                    for h in range(2):
                        if not first:
                            hold(act, "act", gathered[name][h], t * GATHERS)
                        nc.scalar.copy(IDX[h][:, :], table[:, bass.ds((t * 2 + h) * C, C)]).then_inc(idx_ready[name], 1)
                return pair

            def linear(dest, staged=None):
                w = {"rel": R * F, "root": F, "b2": F, "ih": 3 * F, "hh": 3 * F}[LIN[lins[0]]]
                for g in range(GROUPS):
                    n = lins[0] * GROUPS + g + 1
                    act.wait_ge(lin_turned, n)
                    nc.scalar.copy(HT[:, :], psT[0:G * F, 0:P]).then_inc(lin_copied, 1)
                    act.wait_ge(lin_mult, n)
                    if staged is not None and staged * GROUPS // 2 + g // 2 > 0:
                        act.wait_ge(rel_stored[g % 2], 16 * (staged * GROUPS // 2 + g // 2))
                    parts = 2 if G * w > 512 else 1
                    for i in range(parts):
                        o, pw = dest(g), G * w // parts
                        s = psM[:, i * 512:i * 512 + pw]
                        if parts == 2:
                            o = o[:, i * pw:(i + 1) * pw]
                        elif len(o.shape) == 3:
                            s = s.rearrange("p (j k) -> p j k", j=G)
                        last = nc.scalar.copy(o, s)
                    last.then_inc(lin_out, 1)
                lins[0] += 1

            function(NB[:, :], NA[:, :], ACT.Sqrt)
            loop_pairs(act, index_pass("xi", SRC))

            def merge_pair(t, first):
                for h in range(2):
                    k = t * 2 + h
                    if not first:
                        for i in range(2):
                            hold(act, "act", scattered[i], t * 16 * C - (1 - h) * 8 * C)
                    for b in range(2):
                        hold(act, "act", merged, k * 2 + b + 1)
                        last = nc.scalar.copy(ROWS[h][:, b * HALF * ACC:(b + 1) * HALF * ACC],
                                              psM[:, b * 512:b * 512 + HALF * ACC])
                        if b == 0:
                            last.then_inc(held["act"], 1)
                    last.then_inc(rows_ready, 1)

            loop_pairs(act, merge_pair)
            function(NB[:, :], NA[:, :], ACT.Sqrt)
            for n, name in enumerate(("conv1", "conv2")):
                linear(lambda g: stage[g % 2], n)
                linear(lambda g: ROOT[:, g * G * F:(g + 1) * G * F])
                loop_pairs(act, index_pass(name, RIDX))
            function(TA[:, :], TB[:, :], ACT.Exp)
            function(NB[:, :], NA[:, :], ACT.Ln)
            function(NB[:, :], NA[:, :], ACT.Sqrt)

            def edge_pass(name, n):
                def index(k, h):
                    return nc.scalar.copy(IDX[h][:, :], SRC[:, bass.ds(k * C, C)]).then_inc(idx_ready[name], 1)

                def chunk(t, h):
                    for b, tiles in enumerate(BATCHES):
                        at = ((n * CHUNKS + h) * len(BATCHES) + b + 1) + t * 2 * len(BATCHES)
                        w = len(tiles) * P
                        hold(act, "act", attr_turned, at)
                        nc.scalar.copy(AT[:, 0:w], psT[0:Q * FD, 0:w]).then_inc(attr_copied, 1)
                        hold(act, "act", hid_done, at)
                        nc.scalar.activation(HIDT[:, 0:w], psH[:, 0:w], ACT.Relu, bias=FB1[:, 0:1]).then_inc(hid_relu, 1)

                def pair(t, first):
                    for h in range(2):
                        chunk(t, h)
                        hold(act, "act", gathered[name][h], (t + 1) * GATHERS)
                        index(t * 2 + h + 2, h)

                for h in range(2):
                    index(h, h)
                loop_pairs(act, pair, end=PAIRS - 1)
                for h in range(2):
                    chunk(PAIRS - 1, h)

            for n, name in enumerate(("edge1", "edge2")):
                linear(lambda g: pair_tab[:, g * G:(g + 1) * G, F:2 * F])
                edge_pass(name, n)
                linear(lambda g: GI[:, g * G:(g + 1) * G, :])
                linear(lambda g: GH[:, g * G:(g + 1) * G, :])
                function(GI[:, :, 0:2 * F], GI[:, :, 0:2 * F], ACT.Sigmoid)
                function(TA[:, :], TB[:, :], ACT.Tanh)
            function(NB[:, :], NA[:, :], ACT.Sqrt)
            function(NB[:, :], NA[:, :], ACT.Sqrt)
            loop_pairs(act, index_pass("sum3", SRC))
            function(NB[:, :], NA[:, :], ACT.Sqrt)

        @block.tensor
        def _(pe):
            lins = [0]
            ends = [0]
            lin_asked = [0]

            pe.wait_ge(consts_ready, 1)
            nc.tensor.matmul(psH[0:NJ, 0:P], LOWER[:, 0:NJ], NONE_HOT[:, :], start=True, stop=False)

            def hist_pair(t, first):
                for h in range(2):
                    for b in range(2):
                        n = t * 4 + (h * 2 + b + 1)
                        hold(pe, "pe", hot_ready, n)
                        for c in range(HALF):
                            mm = nc.tensor.matmul(psH[0:NJ, 0:P], hot_hi[b][:, c, :], hot_lo[b][:, c, :],
                                                  start=False, stop=False, skip_group_check=True)
                        mm.then_inc(hot_used, 1)

            pe.wait_ge(cont_ready, 1)
            nc.tensor.matmul(psT[0:F, 0:P], CO16[:, :], IDENT[:, :], start=True, stop=True)
            nc.tensor.matmul(psT[0:F, P:2 * P], A16[:, :], IDENT[:, :], start=True, stop=True).then_inc(cont_turned, 1)
            loop_pairs(pe, hist_pair)
            nc.tensor.matmul(psH[0:NJ, 0:P], LOWER[:, 0:NJ], NONE_HOT[:, :], start=False, stop=True)\
                .then_inc(hist_done, 1)
            pe.wait_ge(totals_ready, 1)
            nc.tensor.matmul(psH[:, 0:1], UPPER[:, :], SMALL[:, 0:1], start=True, stop=True).then_inc(offsets_ready, 1)

            def finish_segments(w):
                ends[0] += 1
                pe.wait_ge(last_ready, ends[0])
                nc.tensor.transpose(psT[0:w, 0:P], LAST[:, 0:w], IDENT[:, :]).then_inc(last_turned, 1)
                pe.wait_ge(carry_ready, ends[0])
                nc.tensor.transpose(psT[:, P:P + w], CARRY_T[0:w, :], IDENT[0:w, 0:w]).then_inc(carry_turned, 1)

            finish_segments(R)

            def merge_pair(t, first):
                for h in range(2):
                    k = t * 2 + h
                    hold(pe, "pe", key_ready, k + 1)
                    for g in range(TILES):
                        n = t * (2 * TILES) + h * TILES + g
                        if not (first and h == 0 and g < 2):
                            hold(pe, "pe", eq_done, n - 1)
                        for q in range(Q):
                            mm = nc.tensor.matmul(psW[g % 2][:, q * P:(q + 1) * P] if (h * TILES + g) % 2 == g % 2 else
                                                  psW[1 - g % 2][:, q * P:(q + 1) * P],
                                                  KEY[:, g * Q + q:g * Q + q + 1].to_broadcast([P, P]), IDENT[:, :],
                                                  start=True, stop=True)
                        mm.then_inc(key_spread, 1)
                    hold(pe, "pe", msg_ready, k + 1)
                    if not (first and h == 0):
                        hold(pe, "pe", rows_ready, k)
                    for b in range(2):
                        for c in range(HALF):
                            mm = nc.tensor.matmul(psM[:, b * 512 + c * ACC:b * 512 + (c + 1) * ACC],
                                                  meq[:, b * HALF + c, :], msg[:, b * HALF + c, :], start=True, stop=True)
                        mm.then_inc(merged, 1)

            loop_pairs(pe, merge_pair)

            def linear(source):
                name = LIN[lins[0]]
                w = G * {"rel": R * F, "root": F, "b2": F, "ih": 3 * F, "hh": 3 * F}[name]
                for g in range(GROUPS):
                    n = lins[0] * GROUPS + g
                    if n:
                        pe.wait_ge(lin_out, n)
                    nc.tensor.transpose(psT[0:G * F, 0:P], source[:, g * G * F:(g + 1) * G * F], IDENT[:, :]).then_inc(lin_turned, 1)
                    pe.wait_ge(lin_copied, n + 1)
                    parts = 2 if w > 512 else 1
                    pw = w // parts
                    for i in range(parts):
                        mm = nc.tensor.matmul(psM[:, i * 512:i * 512 + pw], HT[:, :], BD[name][:, i * pw:(i + 1) * pw],
                                              start=True, stop=True)
                    mm.then_inc(lin_mult, 1)
                lins[0] += 1

            def wait_nodes():
                lin_asked[0] += 1
                pe.wait_ge(lin_in, lin_asked[0])

            pe.wait_ge(weights_in, N_WEIGHTS)
            pe.wait_ge(fw2_ready, 1)
            for name in ("conv1", "conv2"):
                wait_nodes()
                if name == "conv2":
                    pe.wait_ge(conv2_weights_in, 16 * 2 * G)
                linear(H)
                linear(H)
                finish_segments(F)

            def edge_pass(n):
                def pair(t, first):
                    for h in range(2):
                        hold(pe, "pe", attr_in[h], t * 16 + (n * PAIRS + 1) * 16)
                        for b, tiles in enumerate(BATCHES):
                            at = ((n * CHUNKS + h) * len(BATCHES) + b) + t * 2 * len(BATCHES)
                            if not (first and n == 0 and h == 0 and b == 0):
                                hold(pe, "pe", attr_copied, at)
                            for i, g in enumerate(tiles):
                                mm = nc.tensor.transpose(psT[0:Q * FD, i * P:(i + 1) * P],
                                                         IN[h][:, g * Q * FD:(g + 1) * Q * FD], IDENT[:, :])
                            mm.then_inc(attr_turned, 1)
                            hold(pe, "pe", attr_copied, at + 1)
                            if not (first and n == 0 and h == 0 and b == 0):
                                hold(pe, "pe", hid_relu, at)
                            w = len(tiles) * P
                            nc.tensor.matmul(psH[:, 0:w], FW1[:, :], AT[:, 0:w], start=True, stop=True).then_inc(hid_done, 1)
                            hold(pe, "pe", hid_relu, at + 1)
                            for i, g in enumerate(tiles):
                                at_tile = (n * CHUNKS + h) * TILES + g + t * 2 * TILES
                                slot = (h * TILES + g) % 2
                                if not (first and n == 0 and h == 0 and g < 2):
                                    hold(pe, "pe", w_used, at_tile - 1)
                                for b2 in range(2):
                                    mm = nc.tensor.matmul(psW[slot][:, b2 * 512:(b2 + 1) * 512],
                                                          HIDT[:, i * P:(i + 1) * P], FW2[:, b2 * 512:(b2 + 1) * 512],
                                                          start=True, stop=True)
                                mm.then_inc(w_ready, 1)
                return pair

            for n in range(2):
                wait_nodes()
                linear(H)
                loop_pairs(pe, edge_pass(n))
                finish_segments(F)
                wait_nodes()
                linear(AGG)
                linear(H)
            finish_segments(F)

        @block.vector
        def _(dve):
            v = nc.vector
            st = Steps(dve, dve_step)
            asked, tables, ends, lin_asked, lin_done = [0], [0], [0], [0], [0]

            def ask():
                dve.wait_ge(dve_step, st.n)
                dve.sem_inc(to_act, 1)
                asked[0] += 1
                dve.wait_ge(from_act, asked[0])

            def signal(s):
                dve.wait_ge(dve_step, st.n)
                dve.sem_inc(s, 1)

            def linear_done(calls):
                lin_done[0] += calls
                dve.wait_ge(lin_out, lin_done[0] * GROUPS)

            X3, H3, TA3, TB3, AGG3 = (node3(t) for t in (X, H, TA, TB, AGG))

            def layer_norm():
                st.do(v.tensor_reduce(NA[:, :], X3, AX.X, ALU.add))
                st.do(v.tensor_scalar(NA[:, :], NA[:, :], 1.0 / F, None, ALU.mult))
                st.do(v.tensor_tensor(TA3, X3, spread(NA[:, :], NJ, F), ALU.subtract))
                st.do(v.tensor_tensor(TB[:, :], TA[:, :], TA[:, :], ALU.mult))
                st.do(v.tensor_reduce(NA[:, :], TB3, AX.X, ALU.add))
                st.do(v.tensor_scalar(NA[:, :], NA[:, :], 1.0 / F, EPS, ALU.mult, ALU.add))
                ask()
                st.do(v.reciprocal(NA[:, :], NB[:, :]))
                st.do(v.tensor_tensor(TA3, TA3, spread(NA[:, :], NJ, F), ALU.mult))
                st.do(v.tensor_scalar(H[:, :], TA[:, :], 0.0, None, ALU.max))

            dve.wait_ge(iota_done, 1)
            for w in BD.values():
                st.did(v.memset(w[:, :], 0.0))
            st.did(v.memset(FW1[:, :], 0.0))
            st.did(v.memset(FW2[:, :], 0.0))
            st.did(v.memset(NONE_HOT[:, :], 0.0))
            st.did(v.tensor_copy(ROWF[:, :], ROWI[:, :]))
            st.did(v.tensor_copy(COLF[:, :], COLI[:, :]))
            st.settle()
            signal(zero_ready)
            st.did(v.tensor_copy(COLB[:, :], COLF[:, :]))
            st.did(v.tensor_scalar(IDENT[:, :], COLF[:, :], ROWF[:, 0:1], None, ALU.is_equal))
            st.did(v.tensor_scalar(LOWER[:, :], COLF[:, :], ROWF[:, 0:1], None, ALU.is_lt))
            st.did(v.tensor_scalar(UPPER[:, :], COLF[:, :], ROWF[:, 0:1], None, ALU.is_gt))
            st.settle()
            signal(consts_ready)
            dve.wait_ge(x_in, 16)
            layer_norm()
            signal(table_ready)
            st.do(v.tensor_scalar(TA[:, :], H[:, :], -1.0 / 5.0, 1.0, ALU.mult, ALU.add))
            st.do(v.tensor_tensor(TA[:, :], TA[:, :], H[:, :], ALU.mult))
            st.do(v.scalar_tensor_tensor(out=TA[:, :], in0=H[:, :], scalar=1.0, in1=TA[:, :], op0=ALU.subtract, op1=ALU.mult))
            st.do(v.scalar_tensor_tensor(out=X[:, :], in0=TA[:, :], scalar=0.1, in1=X[:, :], op0=ALU.add, op1=ALU.add))
            st.do(v.memset(TB[:, :], 0.0))
            signal(zero_ready)

            dve.wait_ge(edges_in, 16 * 5)
            st.did(v.memset(SAME[:, 0:1], 0.0))
            st.did(v.tensor_tensor(SAME[:, 1:T], dst_all[:, 1:T], dst_all[:, 0:T - 1], ALU.is_equal))
            st.did(v.tensor_scalar(RIDX[:, :], SRC[:, :], float(R), None, ALU.mult))
            st.did(v.tensor_tensor(NORM[:, :], dst_all, dst_all[:, 0:1].to_broadcast([P, T]), ALU.is_equal))
            st.did(v.tensor_copy(DST0[:, :], dst_all[:, 0:1]))
            st.settle()
            st.did(v.tensor_tensor(RIDX[:, :], RIDX[:, :], typ_all, ALU.add))
            st.did(v.tensor_tensor(SMALL[:, 1:2], dst_all[:, 0:1], EDGES[:, 1:2], ALU.is_equal))
            st.did(v.tensor_tensor(SMALL[:, 2:3], EDGES[:, 0:1], EDGES[:, 1:2], ALU.is_equal))
            st.did(v.tensor_reduce(SMALL[:, 3:4], NORM[:, :], AX.X, ALU.add))
            st.settle()
            st.did(v.tensor_scalar(SMALL[:, 4:5], ROWF[:, :], float(T), -1.0, ALU.mult, ALU.add))
            st.did(v.tensor_tensor(SMALL[:, 2:3], SMALL[:, 1:2], SMALL[:, 2:3], ALU.mult))
            st.settle()
            st.did(v.tensor_tensor(FIRSTROW[:, :], SMALL[:, 3:4], SMALL[:, 4:5], ALU.add))
            st.did(v.tensor_copy(CO16[:, :], SMALL[:, 1:2].to_broadcast([P, F])))
            st.did(v.tensor_copy(A16[:, :], SMALL[:, 2:3].to_broadcast([P, F])))
            st.settle()
            signal(cont_ready)
            dve.wait_ge(cont_turned, 1)
            st.did(v.tensor_copy(CONT_T[:, :], psT[0:F, 0:P]))
            st.did(v.tensor_copy(A_T[:, :], psT[0:F, P:2 * P]))
            st.settle()

            dve.wait_ge(weights_in, N_WEIGHTS)
            for q in range(Q):
                rows = slice(q * HID, (q + 1) * HID)
                st.did(v.tensor_copy(FW2[rows, q * F * F:(q + 1) * F * F].rearrange("k (o i) -> k o i", o=F),
                                     FW2IO[rows, :].rearrange("k (i o) -> k o i", i=F)))
            st.settle()
            signal(fw2_ready)

            def scans(h, src3, w, k, start, s):
                o = cols(OS[h], w)
                prev = cols(OS[1 - h], w)
                for f in range(w):
                    last = v.tensor_tensor_scan(o[:, :, f], SAME[:, bass.ds(k * C, C)], src3[:, :, f],
                                                0.0 if start else prev[:, C - 1, f:f + 1], ALU.mult, ALU.add)
                last.then_inc(s, 1)

            def hist_pair(t, first):
                for h in range(2):
                    k = t * 2 + h
                    hold(dve, "dve", hist_in[h], (t + 1) * 32)
                    st.did(v.tensor_scalar(LOI[:, :], EDST[h][:, :], P - 1, None, ALU.bitwise_and))
                    st.did(v.tensor_scalar(HII[:, :], EDST[h][:, :], 7, None, ALU.logical_shift_right))
                    st.settle()
                    st.did(v.tensor_copy(LOB[:, :], LOI[:, :]))
                    st.did(v.tensor_copy(HIB[:, :], HII[:, :]))
                    st.did(v.tensor_tensor(cols(TH, R), over(COLF[:, 0:R], C, R), spread(ETYP[h][:, :], C, R), ALU.is_equal))
                    st.settle()
                    dve.sem_inc(hist_read, 1)
                    for b in range(2):
                        if not (first and h == 0):
                            hold(dve, "dve", hot_used, k * 2 + b - 1)
                        sl = slice(b * HALF, (b + 1) * HALF)
                        st.did(v.tensor_tensor(hot_lo[b], over(COLB[:, :], HALF, P), spread(LOB[:, sl], HALF, P), ALU.is_equal))
                        v.tensor_tensor(hot_hi[b], over(COLB[:, 0:NJ], HALF, NJ), spread(HIB[:, sl], HALF, NJ),
                                        ALU.is_equal).then_inc(hot_ready, 1)
                    if not first:
                        hold(dve, "dve", types_stored[h], t * 16)
                    if not (first and h == 0):
                        hold(dve, "dve", scanned["xi"], k)
                    scans(h, cols(TH, R), R, k, first and h == 0, scanned["xi"])

            loop_pairs(dve, hist_pair, st)
            dve.wait_ge(hist_done, 1)
            st.do(v.tensor_copy(HIDT[0:NJ, 0:P], psH[0:NJ, 0:P]))
            signal(hist_copied)

            def finish_segments(name, w, dest):
                ends[0] += 1
                n = ends[0]
                dve.wait_ge(scanned["xi" if name == "types" else name], CHUNKS)
                st.do(v.tensor_copy(LAST[:, 0:w], cols(OS[1], w)[:, C - 1, :]))
                signal(last_ready)
                dve.wait_ge(last_turned, n)
                st.did(v.memset(B_T[:, 0:1], 0.0))
                st.did(v.tensor_tensor(B_T[0:w, 1:P], psT[0:w, 0:P - 1], CONT_T[0:w, 1:P], ALU.mult))
                st.settle()
                st.do(v.tensor_tensor_scan(CARRY_T[0:w, :], A_T[0:w, :], B_T[0:w, :], 0.0, ALU.mult, ALU.add))
                signal(carry_ready)
                dve.wait_ge(carry_turned, n)
                st.do(v.tensor_copy(CARRY[:, 0:w], psT[:, P:P + w]))
                signal(carry_out)
                dve.wait_ge(ends_in, 16 * NJ * n)
                st.do(v.tensor_tensor(node3(dest, w), node3(dest, w), spread(FULL[:, :], NJ, w), ALU.mult))

            dve.wait_ge(count_in, 16)
            st.do(v.memset(FULL[:, :], 1.0))
            st.do(v.tensor_tensor_scan(NA[:, :], FULL[:, :], CNT[:, :], 0.0, ALU.mult, ALU.add))
            st.do(v.tensor_copy(SMALL[:, 0:1], NA[:, NJ - 1:NJ]))
            signal(totals_ready)
            dve.wait_ge(offsets_ready, 1)
            st.do(v.tensor_copy(SMALL[:, 5:6], psH[:, 0:1]))
            st.do(v.tensor_scalar(NA[:, :], NA[:, :], SMALL[:, 5:6], None, ALU.add))
            st.did(v.tensor_scalar(END[:, :], NA[:, :], -1.0, 0.0, ALU.add, ALU.max))
            st.did(v.tensor_tensor(NA[:, :], NA[:, :], CNT[:, :], ALU.subtract))
            st.did(v.tensor_scalar(FULL[:, :], CNT[:, :], 1.0, None, ALU.min))
            st.did(v.tensor_scalar(NB[:, :], ROWF[:, 0:1].to_broadcast([P, NJ]), float(NJ), float(EP), ALU.mult, ALU.add))
            st.settle()
            st.do(v.tensor_tensor(NB[:, :], NB[:, :], COLF[:, 0:NJ], ALU.add))
            st.do(v.tensor_tensor(NA[:, :], NA[:, :], NB[:, :], ALU.subtract))
            st.do(v.tensor_tensor(NA[:, :], NA[:, :], FULL[:, :], ALU.mult))
            st.do(v.tensor_tensor(START[:, :], NA[:, :], NB[:, :], ALU.add))
            finish_segments("types", R, type_cnt)
            st.do(v.tensor_scalar(type_cnt, type_cnt, 1.0, None, ALU.max))
            st.did(v.reciprocal(node_ext[:, :, F:NE], node3(type_cnt, R)))
            st.did(v.tensor_copy(node_ext[:, :, 0:F], H3))
            st.settle()
            signal(table_ready)
            dve.wait_ge(starts_out, 16 * NJ)
            dve.wait_ge(first_in, 16)
            st.did(v.tensor_copy(KT[:, :], ROWF[:, 0:1].to_broadcast([P, C])))
            st.did(v.memset(msg[:, :, F:ACC], 1.0))
            st.settle()

            def msg_pair(t, first):
                for h in range(2):
                    k = t * 2 + h
                    st.settle()
                    hold(dve, "dve", msg_in[h], (t + 1) * 64)
                    if first and h == 0:
                        v.tensor_copy(GB[h][:, 0:NE], FIRST[:, :]).then_inc(first_placed, 1)
                        dve.wait_ge(first_placed, 1)
                    if not (first and h == 0):
                        hold(dve, "dve", msg_scanned, k)
                        hold(dve, "dve", key_spread, t * 2 * TILES + h * TILES)
                    st.did(v.tensor_copy(KEY[:, :], SRC[:, bass.ds(k * C, C)]))
                    st.settle()
                    dve.sem_inc(key_ready, 1)
                    scans(h, cols(GB[h], NE), NE, k, first and h == 0, msg_scanned)
                    st.did(v.tensor_tensor(cols(TH, R), over(COLF[:, 0:R], C, R), spread(ETYP[h][:, :], C, R), ALU.is_equal))
                    hold(dve, "dve", msg_scanned, k + 1)
                    st.settle()
                    xj, xi = cols(OS[h], NE)[:, :, 0:F], cols(IN[h], F)
                    dn, mm = cols(GB[h], F), msg[:, :, 0:F]
                    st.did(v.tensor_tensor(cols(TH, R), cols(TH, R), cols(OS[h], NE)[:, :, F:NE], ALU.mult))
                    st.did(v.tensor_scalar(dn, xj, 0.1, 5.0, ALU.mult, ALU.add))
                    if not (first and h == 0):
                        hold(dve, "dve", merged, k * 2)
                    st.did(v.tensor_tensor(mm, xi, xj, ALU.mult))
                    st.settle()
                    st.did(v.tensor_reduce(DUP[:, :], cols(TH, R), AX.X, ALU.add))
                    st.did(v.scalar_tensor_tensor(out=dn, in0=xi, scalar=0.9, in1=dn, op0=ALU.mult, op1=ALU.add))
                    st.did(v.tensor_tensor(mm, mm, spread(EWT[h][:, :], C, F), ALU.mult))
                    st.settle()
                    st.did(v.tensor_copy(NORM[:, bass.ds(k * C, C)], DUP[:, :]))
                    st.do(v.reciprocal(dn, dn))
                    st.do(v.tensor_tensor(mm, mm, dn, ALU.mult))
                    dve.sem_inc(msg_read, 1)
                    for g in range(TILES):
                        bank = psW[(h * TILES + g) % 2][:, 0:Q * P].rearrange("p (c k) -> p c k", c=Q)
                        gs = slice(g * Q, (g + 1) * Q)
                        hold(dve, "dve", key_spread, t * 2 * TILES + h * TILES + g + 1)
                        v.tensor_tensor(meq[:, gs, :], bank, spread(KEY[:, gs], Q, P), ALU.is_equal).then_inc(eq_done, 1)
                        hold(dve, "dve", eq_done, t * 2 * TILES + h * TILES + g + 1)
                        st.do(v.tensor_tensor(meq_low, meq[:, gs, :], over(LOWER[:, :], Q, P), ALU.mult))
                        st.did(v.tensor_reduce(DUP[:, gs], meq_low, AX.X, ALU.add))
                    st.settle()
                    dve.sem_inc(msg_ready, 1)
                    st.do(v.tensor_scalar(DUP[:, :], DUP[:, :], 1.0, None, ALU.min))
                    st.do(v.scalar_tensor_tensor(out=TH[:, 0:C], in0=KT[:, :], scalar=float(NPAD), in1=KEY[:, :],
                                                 op0=ALU.add, op1=ALU.subtract))
                    st.do(v.tensor_tensor(DUP[:, :], DUP[:, :], TH[:, 0:C], ALU.mult))
                    if not first:
                        for i in range(2):
                            hold(dve, "dve", scattered[i], t * 16 * C - (1 - h) * 8 * C)
                    v.tensor_tensor(IDX[h][:, :], DUP[:, :], KEY[:, :], ALU.add).then_inc(scat_idx_ready, 1)
                    hold(dve, "dve", scat_idx_ready, k + 1)

            loop_pairs(dve, msg_pair, st)
            dve.wait_ge(merged, 2 * CHUNKS)
            st.do(v.memset(acc_sum, 0.0))
            for r in range(2 * SET):
                dve.wait_ge(acc_loaded[r % 4], 16 * (r // 4 + 1))
                st.do(v.tensor_tensor(acc_sum, acc_sum, acc_in[r % 4], ALU.add))
                signal(acc_used)
            sum3 = acc_sum.rearrange("p (j k) -> p j k", j=NJ)
            st.did(v.tensor_tensor(X3, X3, sum3[:, :, 0:F], ALU.add))
            st.did(v.tensor_copy(OUTDEG[:, :], sum3[:, :, F]))
            st.settle()
            layer_norm()
            signal(lin_in)

            def scan_pass(name, normed):
                def pair(t, first):
                    for h in range(2):
                        k = t * 2 + h
                        hold(dve, "dve", gathered[name][h], (t + 1) * GATHERS)
                        if not first:
                            hold(dve, "dve", stored[name][h], t * 16)
                        if not (first and h == 0):
                            hold(dve, "dve", scanned[name], k)
                        if normed:
                            st.did(v.tensor_tensor(cols(GB[h], F), cols(GB[h], F), spread(NORM[:, bass.ds(k * C, C)], C, F), ALU.mult))
                            st.settle()
                        scans(h, cols(GB[h], F), F, k, first and h == 0, scanned[name])
                return pair

            for n, name in enumerate(("conv1", "conv2")):
                linear_done(2)
                loop_pairs(dve, scan_pass(name, True), st)
                finish_segments(name, F, AGG)
                st.do(v.tensor_tensor(AGG[:, :], AGG[:, :], ROOT[:, :], ALU.add))
                st.do(v.tensor_tensor(AGG3, AGG3, over((B1, B2)[n][:, :], NJ, F), ALU.add))
                if n == 0:
                    st.do(v.tensor_scalar(H[:, :], AGG[:, :], 0.0, None, ALU.max))
                    signal(lin_in)
            st.do(v.tensor_reduce(NA[:, :], AGG3, AX.X, ALU.max))
            st.do(v.tensor_tensor(TB3, AGG3, spread(NA[:, :], NJ, F), ALU.subtract))
            ask()
            st.do(v.tensor_reduce(NA[:, :], TA3, AX.X, ALU.add))
            ask()
            st.do(v.tensor_tensor(TB3, TB3, spread(NB[:, :], NJ, F), ALU.subtract))
            st.do(v.tensor_tensor(X[:, :], X[:, :], TB[:, :], ALU.add))
            layer_norm()

            def edge_pass(name, n):
                def mult(t, h, g):
                    at = t * 2 * TILES + (n * CHUNKS + h) * TILES + g
                    hold(dve, "dve", w_ready, at + 1)
                    if g >= 3:
                        hold(dve, "dve", m_reduced, at - 2)
                    bank = psW[(h * TILES + g) % 2][:, :].rearrange("p (c o i) -> p c o i", c=Q, o=F)
                    xs = cols(GB[h], 2 * F)[:, g * Q:(g + 1) * Q, 0:F].unsqueeze(2).to_broadcast([P, Q, F, F])
                    v.tensor_tensor(prod[g % 3].rearrange("p (c o i) -> p c o i", c=Q, o=F), bank, xs, ALU.mult).then_inc(w_used, 1)

                def reduce(t, h, g):
                    hold(dve, "dve", w_used, t * 2 * TILES + (n * CHUNKS + h) * TILES + g + 1)
                    v.tensor_reduce(m_edge[:, g * Q:(g + 1) * Q, :], prod[g % 3].rearrange("p (c o i) -> p c o i", c=Q, o=F),
                                    AX.X, ALU.add).then_inc(m_reduced, 1)

                def pair(t, first):
                    for h in range(2):
                        k = t * 2 + h
                        hold(dve, "dve", gathered[name][h], (t + 1) * GATHERS)
                        if not (first and h == 0):
                            hold(dve, "dve", scanned[name], k)
                        mult(t, h, 0)
                        for g in range(1, TILES):
                            mult(t, h, g)
                            reduce(t, h, g - 1)
                        reduce(t, h, TILES - 1)
                        hold(dve, "dve", m_reduced, t * 2 * TILES + (n * CHUNKS + h + 1) * TILES)
                        st.did(v.tensor_tensor(m_edge, m_edge, cols(GB[h], 2 * F)[:, :, F:2 * F], ALU.add))
                        st.settle()
                        if not first:
                            hold(dve, "dve", stored[name][h], t * 16)
                        scans(h, m_edge, F, k, first and h == 0, scanned[name])
                return pair

            for n, name in enumerate(("edge1", "edge2")):
                signal(lin_in)
                st.did(v.tensor_copy(pair_tab[:, :, 0:F], H3))
                st.settle()
                linear_done(1)
                signal(table_ready)
                dve.wait_ge(table_stored, 16 * (3 + n))
                loop_pairs(dve, edge_pass(name, n), st)
                finish_segments(name, F, AGG)
                st.do(v.tensor_scalar(NA[:, :], CNT[:, :], 1.0, None, ALU.max))
                st.do(v.reciprocal(NA[:, :], NA[:, :]))
                st.do(v.tensor_tensor(AGG3, AGG3, spread(NA[:, :], NJ, F), ALU.mult))
                signal(lin_in)
                linear_done(2)
                st.did(v.tensor_tensor(GI, GI, over(BIH[:, :], NJ, 3 * F), ALU.add))
                st.did(v.tensor_tensor(GH, GH, over(BHH[:, :], NJ, 3 * F), ALU.add))
                st.settle()
                st.do(v.tensor_tensor(GI[:, :, 0:2 * F], GI[:, :, 0:2 * F], GH[:, :, 0:2 * F], ALU.add))
                ask()
                st.do(v.tensor_tensor(TB3, GI[:, :, 0:F], GH[:, :, 2 * F:3 * F], ALU.mult))
                st.do(v.tensor_tensor(TB3, TB3, GI[:, :, 2 * F:3 * F], ALU.add))
                ask()
                st.do(v.tensor_tensor(TB[:, :], H[:, :], TA[:, :], ALU.subtract))
                st.do(v.tensor_tensor(TB3, TB3, GI[:, :, F:2 * F], ALU.mult))
                st.do(v.tensor_tensor(H[:, :], TA[:, :], TB[:, :], ALU.add))
            st.do(v.tensor_tensor(X[:, :], X[:, :], H[:, :], ALU.add))
            layer_norm()
            st.do(v.tensor_scalar(NA[:, :], OUTDEG[:, :], 1.0, None, ALU.max))
            ask()
            st.do(v.reciprocal(NA[:, :], NB[:, :]))
            st.do(v.tensor_tensor(H3, H3, spread(NA[:, :], NJ, F), ALU.mult))
            signal(table_ready)
            loop_pairs(dve, scan_pass("sum3", False), st)
            finish_segments("sum3", F, AGG)
            st.do(v.tensor_scalar(NA[:, :], CNT[:, :], 1.0, None, ALU.max))
            ask()
            st.do(v.reciprocal(NA[:, :], NB[:, :]))
            st.do(v.tensor_tensor(AGG3, AGG3, spread(NA[:, :], NJ, F), ALU.mult))
            st.do(v.tensor_tensor(X[:, :], X[:, :], AGG[:, :], ALU.add))
            signal(out_ready)


_INS = ['x', 'src', 'dst', 'edge_attr_13', 'edge_type_8', 'edge_weight', 'L1_gnn_W1', 'L1_gnn_root1', 'L1_gnn_b1',
        'L1_gnn_W2', 'L1_gnn_root2', 'L1_gnn_b2', 'L2_gnn_fnet_w1', 'L2_gnn_fnet_b1', 'L2_gnn_fnet_w2',
        'L2_gnn_fnet_b2', 'L2_gnn_gru_w_ih', 'L2_gnn_gru_w_hh', 'L2_gnn_gru_b_ih', 'L2_gnn_gru_b_hh']


def kernel(**inputs):
    import numpy as _np
    import concourse.bacc as _bacc
    from concourse import mybir as _mybir
    from concourse.bass_utils import run_bass_kernel_spmd as _run

    nc = _bacc.Bacc("TRN2", target_bir_lowering=False, num_devices=1)
    rows = {'x': (NPAD, 0), 'src': (EP, N), 'dst': (EP, N), 'edge_attr_13': (EP, 0), 'edge_type_8': (EP, 0),
            'edge_weight': (EP, 0)}
    arrays, args = {}, []
    for name in _INS:
        a = _np.ascontiguousarray(inputs[name])
        if name in rows:
            n, fill = rows[name]
            a = _np.concatenate([a, _np.full((n - a.shape[0],) + a.shape[1:], fill, a.dtype)])
        arrays[f"in_{name}_dram"] = a
        args.append(nc.dram_tensor(f"in_{name}_dram", a.shape, _mybir.dt.from_np(a.dtype), kind="ExternalInput").ap())
    out = nc.dram_tensor("out_0_dram", (N, F), F32, kind="ExternalOutput").ap()
    gnn_kernel(nc, *args, out)
    r = _run(nc, [arrays], core_ids=[0])
    return r.results[0]["out_0_dram"]
```

```python
from contextlib import ExitStack

import concourse.bass as bass
from concourse import mybir

F32 = mybir.dt.float32
I32 = mybir.dt.int32
BF16 = mybir.dt.bfloat16
ALU = mybir.AluOpType
ACT = mybir.ActivationFunctionType
AX = mybir.AxisListType

P = 128
N, E = 12500, 412500
F = 16
R = 8
FD, HID = 13, 32
NJ = -(-N // P)
NPAD = NJ * P
C = 52
CHUNKS = 62
PAIRS = CHUNKS // 2
T = C * CHUNKS
EP = T * P
assert EP >= E and EP - E < 4 * P and NPAD > N
HALF = C // 2
G = 7
GROUPS = NJ // G
Q = 4
TILES = C // Q
NE = F + R
ACC = F + 1
SET = 13
SETS = C // SET
assert SETS % 2 == 0
BY_PRODUCT = {"xi": 10, "sum3": 14}
HUGE = 2.0 ** 100
QB = 25
BLOCKS = 4 * QB
HIST_PAIRS = (2, 4)
HIST_PARTS = 4
SCAN_AT = (3, 5, 7, 9)
BATCHES = [range(a, min(a + 4, TILES)) for a in range(0, TILES, 4)]
EPS = 1e-5
BIG = 9408


def gathers(name):
    return 16 * (C - BY_PRODUCT.get(name, 0))


class Steps:

    def __init__(self, eng, sem):
        self.eng, self.sem, self.n, self.t, self.per, self.peeled = eng, sem, 0, None, 0, True

    def did(self, ins):
        ins.then_inc(self.sem, 1)
        self.n += 1

    def settle(self):
        at = self.n if self.t is None else self.t * self.per + (self.n - self.per * self.peeled)
        self.eng.wait_ge(self.sem, at)

    def do(self, ins):
        self.did(ins)
        self.settle()


def loop_pairs(eng, body, steps=None, end=PAIRS):
    n0 = steps.n if steps else 0
    body(0, True)
    if steps:
        steps.per = steps.n - n0
    with eng.Fori(1, end) as t:
        if steps:
            steps.t = t
            n1 = steps.n
        body(t, False)
        if steps:
            assert steps.n - n1 == steps.per
            steps.t = None
            steps.n += (end - 2) * steps.per


def gnn_kernel(nc, x, src, dst, edge_attr, edge_type, edge_weight, W1, root1, b1, W2, root2, b2,
               fw1, fb1, fw2, fb2, w_ih, w_hh, b_ih, b_hh, out):
    ctx = ExitStack()
    with ctx:
        ctx.enter_context(nc.allow_non_contiguous_dma(reason="small weights turned while they load"))

        def sb(name, shape, dt=F32):
            return ctx.enter_context(nc.sbuf_tensor(name, shape, dt))

        def ps(name, width):
            return ctx.enter_context(nc.psum_tensor(name, [P, width], F32))

        def sem(name):
            return ctx.enter_context(nc.semaphore(name))

        def dram(name, shape, dt=F32):
            return nc.dram_tensor(name, shape, dt).ap()

        h_rows = dram("h_rows", (NPAD, F))
        rel_rows = dram("rel_rows", (NPAD * R, F))
        pair_rows = dram("pair_rows", (NPAD, 2 * F))
        xi_rows = dram("xi_rows", (EP, F))
        seg_rows = dram("seg_rows", (EP, F))
        type_rows = dram("type_rows", (EP, R))
        spread_rows = dram("spread_rows", (EP + NPAD, NE))
        node_rows = dram("node_rows", (NPAD, NE))
        count_row = dram("count_row", (NJ, P))
        accs = [dram(f"acc{r}", (NPAD + P, ACC)) for r in range(2 * SET)]

        given = {"src": src, "dst": dst, "type": edge_type, "weight": edge_weight, "attr": edge_attr}
        ordered = {"src": dram("ordered_src", (EP, 1), I32), "dst": dram("ordered_dst", (EP, 1), I32),
                   "type": dram("ordered_type", (EP, 1), I32), "weight": dram("ordered_weight", (EP, 1)),
                   "attr": dram("ordered_attr", (EP, FD))}
        next_rows = dram("next_rows", (NPAD + P, 1))

        SRC, RIDX = sb("SRC", [P, T], I32), sb("RIDX", [P, T], I32)
        SAME, NORM = sb("SAME", [P, T]), sb("NORM", [P, T])
        X, H, TA, TB, AGG = (sb(n, [P, NJ * F]) for n in ("X", "H", "TA", "TB", "AGG"))
        ROOT = sb("ROOT", [P, NJ * F])
        CNT, END, START = sb("CNT", [P, NJ]), sb("END", [P, NJ], I32), sb("START", [P, NJ], I32)
        FULL, OUTDEG, NA, NB = (sb(n, [P, NJ]) for n in ("FULL", "OUTDEG", "NA", "NB"))
        big = sb("big", [P, BIG])
        GB = [sb(f"GB{h}", [P, C * 2 * F]) for h in range(2)]
        OS = [sb(f"OS{h}", [P, C * NE]) for h in range(2)]
        IN = [sb(f"IN{h}", [P, C * F]) for h in range(2)]
        ROWS = [sb(f"ROWS{h}", [P, C * ACC]) for h in range(2)]
        IDX = [sb(f"IDX{h}", [P, C], I32) for h in range(2)]
        EDST = [sb(f"EDST{h}", [P, C], I32) for h in range(2)]
        ETYP = [sb(f"ETYP{h}", [P, C], I32) for h in range(2)]
        EWT = [sb(f"EWT{h}", [P, C]) for h in range(2)]
        KEY, DUP, KT = (sb(n, [P, C]) for n in ("KEY", "DUP", "KT"))
        LOI, HII = sb("LOI", [P, C], I32), sb("HII", [P, C], I32)
        LOB, HIB = sb("LOB", [P, C], BF16), sb("HIB", [P, C], BF16)
        TH = sb("TH", [P, C * R])
        ROWI, COLI = sb("ROWI", [P, 1], I32), sb("COLI", [P, P], I32)
        ROWF, COLF = sb("ROWF", [P, 1]), sb("COLF", [P, P])
        COLB = sb("COLB", [P, P], BF16)
        NONE_HOT, ONE = sb("NONE_HOT", [P, P]), sb("ONE", [P, 1])
        IDENT, LOWER, UPPER = sb("IDENT", [P, P]), sb("LOWER", [P, P]), sb("UPPER", [P, P])
        EDGES = sb("EDGES", [P, 4], I32)
        SMALL = sb("SMALL", [P, 16])
        UNSORTED = sb("UNSORTED", [1, 1], I32)
        COLUMN = {n: sb(f"COLUMN_{n}", [P, FD if n == "attr" else 1], F32 if n in ("weight", "attr") else I32) for n in given}
        COLKEY, NEXT, NEWNEXT = sb("COLKEY", [P, 1]), sb("NEXT", [P, 1]), sb("NEWNEXT", [P, 1])
        PLACE, NEXTROW = sb("PLACE", [P, 1], I32), sb("NEXTROW", [P, 1], I32)
        FIRSTROW, DST0 = sb("FIRSTROW", [P, 1], I32), sb("DST0", [P, 1], I32)
        FIRST = sb("FIRST", [P, NE])
        CO16, A16 = sb("CO16", [P, F]), sb("A16", [P, F])
        CONT_T, A_T, B_T, CARRY_T = (sb(n, [F, P]) for n in ("CONT_T", "A_T", "B_T", "CARRY_T"))
        LAST, CARRY = sb("LAST", [P, F]), sb("CARRY", [P, F])
        BD = {name: sb(f"BD_{name}", [G * F, G * w]) for name, w in
              (("rel", R * F), ("root", F), ("b2", F), ("ih", 3 * F), ("hh", 3 * F))}
        HT = sb("HT", [G * F, P])
        B1, B2 = sb("B1", [P, F]), sb("B2", [P, F])
        BIH, BHH = sb("BIH", [P, 3 * F]), sb("BHH", [P, 3 * F])
        FW1 = sb("FW1", [Q * FD, Q * HID])
        FB1 = sb("FB1", [P, 1])
        FW2IO, FW2 = sb("FW2IO", [P, F * F]), sb("FW2", [P, Q * F * F])
        PART = [sb(f"PART{i}", [P, BLOCKS * F], BF16) for i in range(3)]
        PUSH = sb("PUSH", [P, BLOCKS * F], BF16)
        IDENTB = sb("IDENTB", [P, P], BF16)
        DI = [sb(f"DI{i}", [P, 16], I32) for i in range(2)]
        DK = [sb(f"DK{i}", [P, 2 * 16], BF16) for i in range(2)]
        HOTLO = [sb(f"HOTLO{i}", [P, 2 * P], BF16) for i in range(2)]
        OFFHI = [sb(f"OFFHI{i}", [P, 2 * P], BF16) for i in range(2)]
        OTHER = sb("OTHER", [P, 16 * F])
        AT, HIDT = sb("AT", [Q * FD, 4 * P]), sb("HIDT", [P, 4 * P])

        psW = [ps(f"psW{i}", 2 * 512) for i in range(2)]
        psM = ps("psM", 2 * 512)
        psT, psH = ps("psT", 512), ps("psH", 512)

        dst_all = big[:, 0:T].bitcast(I32)
        typ_all = big[:, T:2 * T].bitcast(I32)
        hot_w = HALF * P // 2
        hoth_w = HALF * NJ // 2
        hot_lo = [big[:, i * hot_w:(i + 1) * hot_w].bitcast(BF16).rearrange("p (c k) -> p c k", c=HALF) for i in range(2)]
        hot_hi = [big[:, 2 * hot_w + i * hoth_w:2 * hot_w + (i + 1) * hoth_w].bitcast(BF16)
                  .rearrange("p (c k) -> p c k", c=HALF) for i in range(2)]
        zeros = TB[:, 0:C * NE]
        col_eq, col_low = big[:, 2 * T:2 * T + P], big[:, 2 * T + P:2 * T + 2 * P]
        meq = big[:, 0:C * P].rearrange("p (c k) -> p c k", c=C)
        meq_low = big[:, C * P:C * P + Q * P].rearrange("p (c k) -> p c k", c=Q)
        msg = big[:, C * P + Q * P:C * P + Q * P + C * ACC].rearrange("p (c k) -> p c k", c=C)
        den = GB[0]
        acc_in = [big[:, r * NJ * ACC:(r + 1) * NJ * ACC] for r in range(4)]
        acc_sum = big[:, 4 * NJ * ACC:5 * NJ * ACC]
        node_ext = big[:, 0:NJ * NE].rearrange("p (j k) -> p j k", j=NJ)
        type_cnt = big[:, NJ * NE:NJ * (NE + R)]
        stage = [big[:, i * G * R * F:(i + 1) * G * R * F] for i in range(2)]
        pair_tab = big[:, 0:NJ * 2 * F].rearrange("p (j k) -> p j k", j=NJ)
        prod = [big[:, i * Q * F * F:(i + 1) * Q * F * F] for i in range(3)]
        m_edge = big[:, 3 * Q * F * F:3 * Q * F * F + C * F].rearrange("p (c k) -> p c k", c=C)
        GI = big[:, 0:NJ * 3 * F].rearrange("p (j k) -> p j k", j=NJ)
        GH = big[:, NJ * 3 * F:2 * NJ * 3 * F].rearrange("p (j k) -> p j k", j=NJ)

        def node3(t, w=F):
            return t[:, 0:NJ * w].rearrange("p (j k) -> p j k", j=NJ)

        def cols(t, w):
            return t[:, 0:C * w].rearrange("p (c k) -> p c k", c=C)

        def spread(col, n, w):
            return col.unsqueeze(2).to_broadcast([P, n, w])

        def over(row, n, w):
            return row.unsqueeze(1).to_broadcast([P, n, w])

        PASSES = ["xi", "conv1", "conv2", "edge1", "edge2", "sum3"]
        idx_ready = {q: sem(f"{q}_idx_ready") for q in PASSES}
        gathered = {q: [sem(f"{q}_gathered{h}") for h in range(2)] for q in PASSES}
        scanned = {q: sem(f"{q}_scanned") for q in PASSES}
        stored = {q: [sem(f"{q}_stored{h}") for h in range(2)] for q in PASSES}
        held = {e: sem(f"held_{e}") for e in ("pool", "act", "pe", "dve", "sp")}
        dst_in, spoiled, unsorted_sum, unsorted_known = (
            sem(n) for n in ("dst_in", "spoiled", "unsorted_sum", "unsorted_known"))
        order_next, order_turn, order_in, order_key, order_keys, order_spread, order_placed, \
            order_step, order_totals, order_offsets, order_starts = (
                sem(f"order_{n}") for n in ("next", "turn", "in", "key", "keys", "spread", "placed",
                                            "step", "totals", "offsets", "starts"))
        order_got, order_put = ([sem(f"order_{n}{run}") for run in range(2)] for n in ("got", "put"))
        order_moved = {name: sem(f"order_moved_{name}") for name in ordered}
        edges_in, x_in, weights_in = sem("edges_in"), sem("x_in"), sem("weights_in")
        conv2_weights_in = sem("conv2_weights_in")
        iota_done, consts_ready, zero_ready = sem("iota_done"), sem("consts_ready"), sem("zero_ready")
        accs_cleared, spread_cleared = sem("accs_cleared"), [sem(f"spread_cleared{h}") for h in range(2)]
        prepared = sem("prepared")
        dve_step = sem("dve_step")
        to_act, from_act = sem("to_act"), sem("from_act")
        table_ready, table_stored = sem("table_ready"), sem("table_stored")
        hist_in = [sem(f"hist_in{h}") for h in range(2)]
        hist_read = sem("hist_read")
        hot_ready, hot_used = sem("hot_ready"), sem("hot_used")
        types_stored = [sem(f"types_stored{h}") for h in range(2)]
        hist_done, hist_copied, hist_stored, count_in = sem("hist_done"), sem("hist_copied"), sem("hist_stored"), sem("count_in")
        totals_ready, offsets_ready = sem("totals_ready"), sem("offsets_ready")
        cont_ready, cont_turned = sem("cont_ready"), sem("cont_turned")
        last_ready, last_turned, carry_ready, carry_turned, carry_out = (
            sem(n) for n in ("last_ready", "last_turned", "carry_ready", "carry_turned", "carry_out"))
        carry_added, ends_in = sem("carry_added"), sem("ends_in")
        starts_out, first_in = sem("starts_out"), sem("first_in")
        msg_in = [sem(f"msg_in{h}") for h in range(2)]
        msg_read, msg_scanned = sem("msg_read"), sem("msg_scanned")
        key_ready, key_spread, eq_done, msg_ready, key_used = (
            sem(n) for n in ("key_ready", "key_spread", "eq_done", "msg_ready", "key_used"))
        merged, rows_ready, scat_idx_ready = sem("merged"), sem("rows_ready"), sem("scat_idx_ready")
        scattered = [sem(f"scattered{i}") for i in range(2)]
        acc_loaded, acc_used = [sem(f"acc_loaded{i}") for i in range(4)], sem("acc_used")
        lin_in, lin_turned, lin_copied, lin_mult, lin_out = (
            sem(n) for n in ("lin_in", "lin_turned", "lin_copied", "lin_mult", "lin_out"))
        rel_stored = [sem(f"rel_stored{i}") for i in range(2)]
        attr_in = [sem(f"attr_in{h}") for h in range(2)]
        attr_turned, attr_copied, hid_done, hid_relu, w_ready, w_used, m_reduced = (
            sem(n) for n in ("attr_turned", "attr_copied", "hid_done", "hid_relu", "w_ready", "w_used", "m_reduced"))
        table_in = sem("table_in")
        dense_cols, dense_keys, dense_hot, dense_sum, dense_read, dense_done = (
            sem(f"dense_{n}") for n in ("cols", "keys", "hot", "sum", "read", "done"))
        out_ready, out_stored = sem("out_ready"), sem("out_stored")

        LIN = ["rel", "root", "rel", "root", "b2", "ih", "hh", "b2", "ih", "hh"]
        LIN_OF = {"conv1": 0, "conv2": 2, "edge1": 4, "gru1": 5, "edge2": 7, "gru2": 8}

        N_WEIGHTS = 16 * (2 * G + 1 + 3 + 3 * G + 3 * Q)
        fw2_ready, first_placed = sem("fw2_ready"), sem("first_placed")

        DENSE, at_chunk, at_pair = {}, 0, 0
        for name, n in BY_PRODUCT.items():
            DENSE[name] = (at_chunk, at_pair, 4 * at_pair)
            at_chunk += CHUNKS
            at_pair += CHUNKS * n // 2

        def hold(eng, name, s, value):
            eng.wait_ge(s, value)
            eng.sem_inc(held[name], 1)

        block = ctx.enter_context(nc.Block())

        @block.sync
        def _(sp):
            def by_part(a):
                return a.rearrange("(p c) -> p c", p=P)

            def load_dst(a, s):
                sp.dma_start(dst_all, by_part(a)).then_inc(s, 16)
                sp.dma_start(EDGES[1:P, 0:1], by_part(a)[0:P - 1, 0:1]).then_inc(s, 16)
                sp.dma_start(EDGES[1:P, 1:2], by_part(a)[0:P - 1, T - 1:T]).then_inc(s, 16)

            sp.wait_ge(iota_done, 1)
            load_dst(dst, dst_in)
            sp.dma_start(X[:, :], x.rearrange("(p j) f -> p (j f)", p=P)).then_inc(x_in, 16)
            sp.wait_ge(zero_ready, 1)
            n = 0

            def put(o, i, s=weights_in):
                sp.dma_start(o, i).then_inc(s, 16)

            def conv_weights(W, root, bias, B, s):
                for j in range(G):
                    rows = slice(j * F, (j + 1) * F)
                    put(BD["rel"][rows, j * R * F:(j + 1) * R * F].rearrange("i (r o) -> i r o", r=R),
                        W.rearrange("r i o -> i r o"), s)
                    put(BD["root"][rows, j * F:(j + 1) * F], root, s)
                if bias is not None:
                    put(B[:, :], bias.unsqueeze(0).to_broadcast([P, F]), s)

            conv_weights(W1, root1, b1, B1, weights_in)
            put(B2[:, :], b2.unsqueeze(0).to_broadcast([P, F]))
            put(BIH[:, :], b_ih.unsqueeze(0).to_broadcast([P, 3 * F]))
            put(BHH[:, :], b_hh.unsqueeze(0).to_broadcast([P, 3 * F]))
            for j in range(G):
                rows = slice(j * F, (j + 1) * F)
                put(BD["b2"][rows, j * F:(j + 1) * F], fb2.rearrange("(i o) -> i o", i=F))
                put(BD["ih"][rows, j * 3 * F:(j + 1) * 3 * F], w_ih.rearrange("o i -> i o"))
                put(BD["hh"][rows, j * 3 * F:(j + 1) * 3 * F], w_hh.rearrange("o i -> i o"))
            for q in range(Q):
                put(FW1[q * FD:(q + 1) * FD, q * HID:(q + 1) * HID], fw1)
                put(FB1[q * HID:(q + 1) * HID, :], fb1.unsqueeze(1))
                put(FW2IO[q * HID:(q + 1) * HID, :], fw2)

            def store_table(n, rows, tile):
                sp.wait_ge(table_ready, n)
                sp.dma_start(rows.rearrange("(p j) d -> p (j d)", p=P), tile).then_inc(table_stored, 16)

            def edge_cols(a, k, w=1):
                if len(a.shape) == 1:
                    return by_part(a)[:, bass.ds(k * C, C)]
                return a.rearrange("(p c) d -> p c d", p=P)[:, bass.ds(k * C, C), :].rearrange("p c d -> p (c d)")

            def load_edges(loads, k=None):
                def put_all(arrays):
                    for tile, name, s in loads:
                        a = arrays[name]
                        if k is None:
                            a = by_part(a) if len(a.shape) == 1 else by_part(a.rearrange("e d -> (e d)"))
                        else:
                            a = edge_cols(a, k)
                        sp.dma_start(tile, a).then_inc(s, 16)

                with sp.If(unsorted > 0):
                    put_all(ordered)
                with sp.Else():
                    put_all(given)

            def xi_pair(t, first):
                for h in range(2):
                    k = t * 2 + h
                    if not first:
                        hold(sp, "sp", hist_read, k - 1)
                    load_edges([(EDST[h][:, :], "dst", hist_in[h]), (ETYP[h][:, :], "type", hist_in[h])], k)
                    sp.dma_start(edge_cols(spread_rows[0:EP, :], k, 1), zeros).then_inc(spread_cleared[h], 16)
                for h in range(2):
                    k = t * 2 + h
                    hold(sp, "sp", scanned["xi"], k + 1)
                    sp.dma_start(edge_cols(type_rows, k, 1), OS[h][:, 0:C * R]).then_inc(types_stored[h], 16)
                    hold(sp, "sp", gathered["xi"][h], (t + 1) * gathers("xi"))
                    hold(sp, "sp", dense_done, k + 1)
                    sp.dma_start(edge_cols(xi_rows, k, 1), GB[h][:, 0:C * F]).then_inc(stored["xi"][h], 16)

            sp.wait_ge(unsorted_known, 1)
            unsorted = nc.sync.value_load(UNSORTED[0:1, 0:1], min_val=0, max_val=1)
            sp.wait_ge(zero_ready, 2)
            with sp.If(unsorted > 0):
                sp.dma_start(next_rows.rearrange("(p j) d -> p (j d)", p=P), zeros[:, 0:NJ + 1]).then_inc(order_next, 16)
                sp.wait_ge(order_next, 16)
                sp.sem_inc(order_turn, 1)
                for run in range(2):
                    names = list(given) if run else ["dst"]
                    with sp.Fori(0, T) as t:
                        hold(sp, "sp", order_turn, t + 1 + run * (T + 1))
                        for name in names:
                            a = given[name]
                            a = a.rearrange("(p c) d -> p c d", p=P) if len(a.shape) == 2 else a.rearrange("(p c d) -> p c d", p=P, d=1)
                            sp.dma_start(COLUMN[name][:, :], a[:, bass.ds(t, 1), :].rearrange("p c d -> p (c d)")).then_inc(order_in, 16)
                    if run == 0:
                        sp.wait_ge(order_turn, T + 1)
                        sp.dma_start(CNT[:, :], next_rows[0:NPAD, :].rearrange("(p j) d -> p (j d)", p=P)).then_inc(order_next, 16)
                        sp.wait_ge(order_starts, 1)
                        sp.dma_start(next_rows[0:NPAD, :].rearrange("(p j) d -> p (j d)", p=P), NA[:, :]).then_inc(order_next, 16)
                        sp.wait_ge(order_next, 48)
                        sp.sem_inc(order_turn, 1)
                sp.wait_ge(order_turn, 2 * T + 2)
                load_dst(ordered["dst"].rearrange("e d -> (e d)"), spoiled)
                sp.wait_ge(spoiled, 48)
            load_edges([(SRC[:, :], "src", edges_in), (typ_all, "type", edges_in)])
            store_table(1, h_rows, H[:, :])
            def load_blocks(n):
                sp.wait_ge(table_stored, 16 * n)
                sp.dma_start(AGG[:, :].rearrange("p (b f) -> p b f", f=F), h_rows.rearrange("(b p) f -> p b f", p=P)).then_inc(table_in, 16)

            load_blocks(1)
            loop_pairs(sp, xi_pair)
            for r in range(2 * SET):
                sp.dma_start(accs[r].rearrange("(p j) d -> p j d", p=P), over(zeros[:, 0:ACC], NJ + 1, ACC)).then_inc(accs_cleared, 16)
            for h in range(2):
                sp.wait_ge(stored["xi"][h], 16 * PAIRS)
                sp.wait_ge(types_stored[h], 16 * PAIRS)
            sp.wait_ge(hist_copied, 1)
            sp.dma_start(count_row, HIDT[0:NJ, 0:P]).then_inc(hist_stored, 16)
            sp.wait_ge(hist_stored, 16)
            sp.dma_start(CNT[:, :], count_row.rearrange("a b -> (a b)").rearrange("(p j) -> p j", p=P)).then_inc(count_in, 16)
            store_table(2, node_rows, big[:, 0:NJ * NE])

            def msg_pair(t, first):
                for h in range(2):
                    k = t * 2 + h
                    if not first:
                        hold(sp, "sp", msg_read, k - 1)
                    sp.dma_start(GB[h][:, 0:C * NE], edge_cols(spread_rows[0:EP, :], k, 1)).then_inc(msg_in[h], 16)
                    sp.dma_start(IN[h][:, :], edge_cols(xi_rows, k, 1)).then_inc(msg_in[h], 16)
                    load_edges([(EWT[h][:, :], "weight", msg_in[h]), (ETYP[h][:, :], "type", msg_in[h])], k)

            sp.wait_ge(starts_out, 16 * NJ)
            loop_pairs(sp, msg_pair)
            for i in range(2):
                sp.wait_ge(scattered[i], 8 * C * CHUNKS)
            for r in range(2 * SET):
                if r >= 4:
                    sp.wait_ge(acc_used, r - 3)
                sp.dma_start(acc_in[r % 4], accs[r][0:NPAD, :].rearrange("(p j) d -> p (j d)", p=P)).then_inc(acc_loaded[r % 4], 16)

            def store_rel(call):
                for g in range(GROUPS):
                    sp.wait_ge(lin_out, call * GROUPS + g + 1)
                    sp.dma_start(rel_rows.rearrange("(p j r) d -> p j (r d)", p=P, r=R)[:, g * G:(g + 1) * G, :],
                                 stage[g % 2].rearrange("p (j k) -> p j k", j=G)).then_inc(rel_stored[g % 2], 16)

            def store_pass(name):
                def pair(t, first):
                    for h in range(2):
                        hold(sp, "sp", scanned[name], t * 2 + h + 1)
                        sp.dma_start(edge_cols(seg_rows, t * 2 + h, 1), OS[h][:, 0:C * F]).then_inc(stored[name][h], 16)
                return pair

            store_rel(LIN_OF["conv1"])
            loop_pairs(sp, store_pass("conv1"))
            sp.wait_ge(lin_mult, 2 * GROUPS)
            conv_weights(W2, root2, None, None, conv2_weights_in)
            store_rel(LIN_OF["conv2"])
            loop_pairs(sp, store_pass("conv2"))

            def edge_pass(name, n):
                def load(k, h, t):
                    load_edges([(IN[h][:, 0:C * FD], "attr", attr_in[h])], k)

                def pair(t, first):
                    for h in range(2):
                        hold(sp, "sp", attr_turned, (t * 2 + h + 1) * len(BATCHES) + n * CHUNKS * len(BATCHES))
                        load(t * 2 + h + 2, h, t)
                        hold(sp, "sp", scanned[name], t * 2 + h + 1)
                        sp.dma_start(edge_cols(seg_rows, t * 2 + h, 1), OS[h][:, 0:C * F]).then_inc(stored[name][h], 16)

                for h in range(2):
                    load(h, h, 0)
                loop_pairs(sp, pair, end=PAIRS - 1)
                for h in range(2):
                    sp.wait_ge(scanned[name], CHUNKS - 1 + h)
                    sp.dma_start(edge_cols(seg_rows, CHUNKS - 2 + h, 1), OS[h][:, 0:C * F]).then_inc(stored[name][h], 16)

            store_table(3, pair_rows, big[:, 0:NJ * 2 * F])
            edge_pass("edge1", 0)
            store_table(4, pair_rows, big[:, 0:NJ * 2 * F])
            edge_pass("edge2", 1)
            store_table(5, h_rows, H[:, :])
            load_blocks(5)
            loop_pairs(sp, store_pass("sum3"))
            sp.wait_ge(out_ready, 1)
            full = N // NJ
            sp.dma_start(out[0:full * NJ, :].rearrange("(p j) f -> p (j f)", p=full), X[0:full, :]).then_inc(out_stored, 16)
            sp.dma_start(out[full * NJ:N, :].rearrange("(a j) f -> a (j f)", a=1),
                         X[full:full + 1, 0:(N - full * NJ) * F]).then_inc(out_stored, 16)
            sp.wait_ge(out_stored, 32)

        @block.gpsimd
        def _(pool):
            nc.gpsimd.memset(EDGES[:, 0:1], -2).then_inc(held["pool"], 1)
            nc.gpsimd.memset(EDGES[:, 1:2], -1).then_inc(held["pool"], 1)
            nc.gpsimd.iota(ROWI[:, :], pattern=[[0, 1]], base=0, channel_multiplier=1).then_inc(held["pool"], 1)
            nc.gpsimd.iota(COLI[:, :], pattern=[[1, P]], base=0, channel_multiplier=0).then_inc(held["pool"], 1)
            pool.wait_ge(held["pool"], 4)
            pool.sem_inc(iota_done, 1)

            def gather(rows, w, slot, c, idx):
                return nc.gpsimd.indirect_dma_start(
                    out=slot[:, c * w:(c + 1) * w], out_offset=None, in_=rows[:, :],
                    in_offset=bass.IndirectOffsetOnAxis(ap=idx, axis=0))

            def scatter(rows, w, slot, c, idx, op=ALU.bypass):
                return nc.gpsimd.indirect_dma_start(
                    out=rows[:, :], out_offset=bass.IndirectOffsetOnAxis(ap=idx, axis=0),
                    in_=slot[:, c * w:(c + 1) * w], in_offset=None, compute_op=op)

            def gather_pass(name, rows, w, freed):
                def pair(t, first):
                    for h in range(2):
                        k = t * 2 + h
                        hold(pool, "pool", idx_ready[name], k + 1)
                        if not first:
                            if freed is None:
                                hold(pool, "pool", stored[name][h], t * 16)
                            else:
                                hold(pool, "pool", freed[0], k - 1)
                        for c in range(gathers(name) // 16):
                            gather(rows, w, GB[h], c, IDX[h][:, c:c + 1]).then_inc(gathered[name][h], 16)
                return pair

            carries = [0]

            def finish_segments(name, rows, w, dest):
                carries[0] += 1
                n = carries[0]
                pool.wait_ge(carry_out, n)
                for h in range(2):
                    pool.wait_ge(types_stored[h] if name == "types" else stored[name][h], 16 * PAIRS)
                scatter(rows, w, CARRY, 0, FIRSTROW[:, 0:1], ALU.add).then_inc(carry_added, 16)
                pool.wait_ge(carry_added, 16 * n)
                for j in range(NJ):
                    gather(rows, w, dest, j, END[:, j:j + 1]).then_inc(ends_in, 16)

            pool.wait_ge(unsorted_known, 1)
            unsorted = nc.gpsimd.value_load(UNSORTED[0:1, 0:1], min_val=0, max_val=1)
            with pool.If(unsorted > 0):
                for run in range(2):
                    with pool.Fori(0, T) as t:
                        hold(pool, "pool", order_keys, t + 1 + run * T)
                        gather(next_rows, 1, NEXT, 0, COLUMN["dst"][:, 0:1]).then_inc(order_got[run], 16)
                        hold(pool, "pool", order_placed, t + 1 + run * T)
                        scatter(next_rows, 1, NEWNEXT, 0, NEXTROW[:, 0:1]).then_inc(order_put[run], 16)
                        if run:
                            for name, a in ordered.items():
                                scatter(a, a.shape[1], COLUMN[name], 0, PLACE[:, 0:1]).then_inc(order_moved[name], 16)
                            for name in ordered:
                                hold(pool, "pool", order_moved[name], t * 16 + 16)
                        hold(pool, "pool", order_put[run], t * 16 + 16)
                        pool.sem_inc(order_turn, 1)

            pool.wait_ge(table_stored, 16)
            loop_pairs(pool, gather_pass("xi", h_rows, F, None))
            finish_segments("types", type_rows, R, type_cnt)
            for h in range(2):
                pool.wait_ge(spread_cleared[h], 16 * PAIRS)
            pool.wait_ge(table_stored, 32)
            gather(node_rows, NE, FIRST, 0, DST0[:, 0:1]).then_inc(first_in, 16)
            for j in range(NJ):
                scatter(spread_rows, NE, big, j, START[:, j:j + 1]).then_inc(starts_out, 16)

            def scatter_pair(t, first):
                for h in range(2):
                    hold(pool, "pool", rows_ready, t * 2 + h + 1)
                    hold(pool, "pool", scat_idx_ready, t * 2 + h + 1)
                    for g in range(SETS):
                        before = (h * SETS + g) // 2
                        if not (first and before == 0):
                            hold(pool, "pool", scattered[g % 2], t * 16 * C + before * 16 * SET)
                        for q in range(SET):
                            c = g * SET + q
                            scatter(accs[(g % 2) * SET + q], ACC, ROWS[h], c, IDX[h][:, c:c + 1], ALU.add)\
                                .then_inc(scattered[g % 2], 16)

            pool.wait_ge(accs_cleared, 16 * 2 * SET)
            loop_pairs(pool, scatter_pair)

            for name in ("conv1", "conv2"):
                for i in range(2):
                    pool.wait_ge(rel_stored[i], 16 * GROUPS // 2 * (1 if name == "conv1" else 2))
                loop_pairs(pool, gather_pass(name, rel_rows, F, [scanned[name]]))
                finish_segments(name, seg_rows, F, AGG)
            for n, name in ((3, "edge1"), (4, "edge2")):
                pool.wait_ge(table_stored, 16 * n)
                loop_pairs(pool, gather_pass(name, pair_rows, 2 * F, [scanned[name]]))
                finish_segments(name, seg_rows, F, AGG)
            pool.wait_ge(table_stored, 16 * 5)
            loop_pairs(pool, gather_pass("sum3", h_rows, F, [scanned["sum3"]]))
            finish_segments("sum3", seg_rows, F, AGG)

        @block.scalar
        def _(act):
            asked = [0]
            lins = [0]

            def function(o, i, f, **kw):
                asked[0] += 1
                act.wait_ge(to_act, asked[0])
                nc.scalar.activation(o, i, f, **kw).then_inc(from_act, 1)

            def index_pass(name, table):
                def pair(t, first):
                    for h in range(2):
                        if not first:
                            hold(act, "act", gathered[name][h], t * gathers(name))
                        nc.scalar.copy(IDX[h][:, :], table[:, bass.ds((t * 2 + h) * C, C)]).then_inc(idx_ready[name], 1)
                return pair

            def linear(dest, staged=None):
                w = {"rel": R * F, "root": F, "b2": F, "ih": 3 * F, "hh": 3 * F}[LIN[lins[0]]]
                for g in range(GROUPS):
                    n = lins[0] * GROUPS + g + 1
                    act.wait_ge(lin_turned, n)
                    nc.scalar.copy(HT[:, :], psT[0:G * F, 0:P]).then_inc(lin_copied, 1)
                    act.wait_ge(lin_mult, n)
                    if staged is not None and staged * GROUPS // 2 + g // 2 > 0:
                        act.wait_ge(rel_stored[g % 2], 16 * (staged * GROUPS // 2 + g // 2))
                    parts = 2 if G * w > 512 else 1
                    for i in range(parts):
                        o, pw = dest(g), G * w // parts
                        s = psM[:, i * 512:i * 512 + pw]
                        if parts == 2:
                            o = o[:, i * pw:(i + 1) * pw]
                        elif len(o.shape) == 3:
                            s = s.rearrange("p (j k) -> p j k", j=G)
                        last = nc.scalar.copy(o, s)
                    last.then_inc(lin_out, 1)
                lins[0] += 1

            function(NB[:, :], NA[:, :], ACT.Sqrt)
            act.wait_ge(edges_in, 32)
            loop_pairs(act, index_pass("xi", SRC))

            def merge_pair(t, first):
                for h in range(2):
                    k = t * 2 + h
                    if not first:
                        for i in range(2):
                            hold(act, "act", scattered[i], t * 16 * C - (1 - h) * 8 * C)
                    for b in range(2):
                        hold(act, "act", merged, k * 2 + b + 1)
                        last = nc.scalar.copy(ROWS[h][:, b * HALF * ACC:(b + 1) * HALF * ACC],
                                              psM[:, b * 512:b * 512 + HALF * ACC])
                        if b == 0:
                            last.then_inc(held["act"], 1)
                    last.then_inc(rows_ready, 1)

            loop_pairs(act, merge_pair)
            function(NB[:, :], NA[:, :], ACT.Sqrt)
            for n, name in enumerate(("conv1", "conv2")):
                linear(lambda g: stage[g % 2], n)
                linear(lambda g: ROOT[:, g * G * F:(g + 1) * G * F])
                loop_pairs(act, index_pass(name, RIDX))
            function(TA[:, :], TB[:, :], ACT.Exp)
            function(NB[:, :], NA[:, :], ACT.Ln)
            function(NB[:, :], NA[:, :], ACT.Sqrt)

            def edge_pass(name, n):
                def index(k, h):
                    return nc.scalar.copy(IDX[h][:, :], SRC[:, bass.ds(k * C, C)]).then_inc(idx_ready[name], 1)

                def chunk(t, h):
                    for b, tiles in enumerate(BATCHES):
                        at = ((n * CHUNKS + h) * len(BATCHES) + b + 1) + t * 2 * len(BATCHES)
                        w = len(tiles) * P
                        hold(act, "act", attr_turned, at)
                        nc.scalar.copy(AT[:, 0:w], psT[0:Q * FD, 0:w]).then_inc(attr_copied, 1)
                        hold(act, "act", hid_done, at)
                        nc.scalar.activation(HIDT[:, 0:w], psH[:, 0:w], ACT.Relu, bias=FB1[:, 0:1]).then_inc(hid_relu, 1)

                def pair(t, first):
                    for h in range(2):
                        chunk(t, h)
                        hold(act, "act", gathered[name][h], (t + 1) * gathers(name))
                        index(t * 2 + h + 2, h)

                for h in range(2):
                    index(h, h)
                loop_pairs(act, pair, end=PAIRS - 1)
                for h in range(2):
                    chunk(PAIRS - 1, h)

            for n, name in enumerate(("edge1", "edge2")):
                linear(lambda g: pair_tab[:, g * G:(g + 1) * G, F:2 * F])
                edge_pass(name, n)
                linear(lambda g: GI[:, g * G:(g + 1) * G, :])
                linear(lambda g: GH[:, g * G:(g + 1) * G, :])
                function(GI[:, :, 0:2 * F], GI[:, :, 0:2 * F], ACT.Sigmoid)
                function(TA[:, :], TB[:, :], ACT.Tanh)
            function(NB[:, :], NA[:, :], ACT.Sqrt)
            function(NB[:, :], NA[:, :], ACT.Sqrt)
            loop_pairs(act, index_pass("sum3", SRC))
            function(NB[:, :], NA[:, :], ACT.Sqrt)

        @block.tensor
        def _(pe):
            lins = [0]
            ends = [0]
            lin_asked = [0]

            pe.wait_ge(consts_ready, 1)
            nc.tensor.matmul(psH[0:NJ, 0:P], LOWER[:, 0:NJ], NONE_HOT[:, :], start=True, stop=False)

            def dense(name, t, h, start, last, between=None):
                chunk0, pair0, half0 = DENSE[name]
                pairs = BY_PRODUCT[name] // 2
                done = t * 2 * pairs + h * pairs

                def keys(j):
                    slot, c0 = (h + j // pairs) % 2, 2 * (j % pairs)
                    if j % pairs == 0:
                        hold(pe, "pe", dense_cols, t * 2 + h + j // pairs + 1 + chunk0)
                    if not (start and chunk0 == 0 and j == 0):
                        hold(pe, "pe", dense_hot, done + pair0 + j)
                    for i in range(2):
                        c = c0 + i
                        for part in range(2):
                            mm = nc.tensor.matmul(psT[:, (part * 2 + i) * P:(part * 2 + i + 1) * P],
                                                  DK[part][:, slot * 16 + c:slot * 16 + c + 1].to_broadcast([P, P]),
                                                  IDENTB[:, :], start=True, stop=True)
                    mm.then_inc(dense_keys, 1)

                def products(j):
                    slot = (h * pairs + j) % 2
                    hold(pe, "pe", dense_hot, done + pair0 + j + 1)
                    for i in range(2):
                        for half in range(2):
                            n = 4 * j + 2 * i + half
                            if not (start and chunk0 == 0 and n < 2):
                                hold(pe, "pe", dense_read, done * 4 + half0 + n - 1)
                            for b in range(2):
                                o = psW[half][:, b * 512:b * 512 + QB * F]
                                at = slice((2 * half + b) * QB * F, (2 * half + b + 1) * QB * F)
                                for part in range(3):
                                    nc.tensor.matmul(o, HOTLO[slot][:, i * P:(i + 1) * P], PART[part][:, at],
                                                     start=(part == 0), stop=False)
                                mm = nc.tensor.matmul(o, OFFHI[slot][0:NJ, i * P:(i + 1) * P], PUSH[0:NJ, at],
                                                      start=False, stop=True)
                            mm.then_inc(dense_sum, 1)

                if start:
                    keys(0)
                for j in range(pairs):
                    if j + 1 < pairs or not last:
                        keys(j + 1)
                    products(j)
                    if between:
                        between(j)

            def hist_pair(t, first, last=False):
                for h in range(2):
                    def between(j):
                        if j not in HIST_PAIRS:
                            return
                        b = HIST_PAIRS.index(j)
                        hold(pe, "pe", hot_ready, t * 4 + (h * 2 + b + 1))
                        for c in range(HALF):
                            mm = nc.tensor.matmul(psH[0:NJ, 0:P], hot_hi[b][:, c, :], hot_lo[b][:, c, :],
                                                  start=False, stop=False, skip_group_check=True)
                        mm.then_inc(hot_used, 1)

                    dense("xi", t, h, first and h == 0, last and h == 1, between)

            def sum3_products(t, first, last=False):
                for h in range(2):
                    dense("sum3", t, h, first and h == 0, last and h == 1)

            pe.wait_ge(unsorted_sum, 1)
            nc.tensor.matmul(psT[0:1, 0:1], SMALL[:, 6:7], ONE[:, :], start=True, stop=True).then_inc(unsorted_sum, 1)
            pe.wait_ge(unsorted_known, 1)
            unsorted = nc.tensor.value_load(UNSORTED[0:1, 0:1], min_val=0, max_val=1)
            with pe.If(unsorted > 0):
                for run in range(2):
                    with pe.Fori(0, T) as t:
                        hold(pe, "pe", order_keys, t + 1 + run * T)
                        nc.tensor.matmul(psT[:, 0:P], COLKEY[:, 0:1].to_broadcast([P, P]), IDENT[:, :],
                                         start=True, stop=True).then_inc(order_spread, 1)
                    if run == 0:
                        pe.wait_ge(order_totals, 1)
                        nc.tensor.matmul(psT[:, 0:1], UPPER[:, :], SMALL[:, 0:1], start=True, stop=True).then_inc(order_offsets, 1)

            pe.wait_ge(cont_ready, 1)
            nc.tensor.matmul(psT[0:F, 0:P], CO16[:, :], IDENT[:, :], start=True, stop=True)
            nc.tensor.matmul(psT[0:F, P:2 * P], A16[:, :], IDENT[:, :], start=True, stop=True).then_inc(cont_turned, 1)
            loop_pairs(pe, hist_pair, end=PAIRS - 1)
            hist_pair(PAIRS - 1, False, last=True)
            nc.tensor.matmul(psH[0:NJ, 0:P], LOWER[:, 0:NJ], NONE_HOT[:, :], start=False, stop=True)\
                .then_inc(hist_done, 1)
            pe.wait_ge(totals_ready, 1)
            nc.tensor.matmul(psH[:, 0:1], UPPER[:, :], SMALL[:, 0:1], start=True, stop=True).then_inc(offsets_ready, 1)

            def finish_segments(w):
                ends[0] += 1
                pe.wait_ge(last_ready, ends[0])
                nc.tensor.transpose(psT[0:w, 0:P], LAST[:, 0:w], IDENT[:, :]).then_inc(last_turned, 1)
                pe.wait_ge(carry_ready, ends[0])
                nc.tensor.transpose(psT[:, P:P + w], CARRY_T[0:w, :], IDENT[0:w, 0:w]).then_inc(carry_turned, 1)

            finish_segments(R)

            def merge_pair(t, first):
                for h in range(2):
                    k = t * 2 + h
                    hold(pe, "pe", key_ready, k + 1)
                    for g in range(TILES):
                        n = t * (2 * TILES) + h * TILES + g
                        if not (first and h == 0 and g < 2):
                            hold(pe, "pe", eq_done, n - 1)
                        for q in range(Q):
                            mm = nc.tensor.matmul(psW[g % 2][:, q * P:(q + 1) * P] if (h * TILES + g) % 2 == g % 2 else
                                                  psW[1 - g % 2][:, q * P:(q + 1) * P],
                                                  KEY[:, g * Q + q:g * Q + q + 1].to_broadcast([P, P]), IDENT[:, :],
                                                  start=True, stop=True)
                        mm.then_inc(key_spread, 1)
                    hold(pe, "pe", msg_ready, k + 1)
                    if not (first and h == 0):
                        hold(pe, "pe", rows_ready, k)
                    for b in range(2):
                        for c in range(HALF):
                            mm = nc.tensor.matmul(psM[:, b * 512 + c * ACC:b * 512 + (c + 1) * ACC],
                                                  meq[:, b * HALF + c, :], msg[:, b * HALF + c, :], start=True, stop=True)
                        mm.then_inc(merged, 1)

            loop_pairs(pe, merge_pair)

            def linear(source):
                name = LIN[lins[0]]
                w = G * {"rel": R * F, "root": F, "b2": F, "ih": 3 * F, "hh": 3 * F}[name]
                for g in range(GROUPS):
                    n = lins[0] * GROUPS + g
                    if n:
                        pe.wait_ge(lin_out, n)
                    nc.tensor.transpose(psT[0:G * F, 0:P], source[:, g * G * F:(g + 1) * G * F], IDENT[:, :]).then_inc(lin_turned, 1)
                    pe.wait_ge(lin_copied, n + 1)
                    parts = 2 if w > 512 else 1
                    pw = w // parts
                    for i in range(parts):
                        mm = nc.tensor.matmul(psM[:, i * 512:i * 512 + pw], HT[:, :], BD[name][:, i * pw:(i + 1) * pw],
                                              start=True, stop=True)
                    mm.then_inc(lin_mult, 1)
                lins[0] += 1

            def wait_nodes():
                lin_asked[0] += 1
                pe.wait_ge(lin_in, lin_asked[0])

            pe.wait_ge(weights_in, N_WEIGHTS)
            pe.wait_ge(fw2_ready, 1)
            for name in ("conv1", "conv2"):
                wait_nodes()
                if name == "conv2":
                    pe.wait_ge(conv2_weights_in, 16 * 2 * G)
                linear(H)
                linear(H)
                finish_segments(F)

            def edge_pass(n):
                def pair(t, first):
                    for h in range(2):
                        hold(pe, "pe", attr_in[h], t * 16 + (n * PAIRS + 1) * 16)
                        for b, tiles in enumerate(BATCHES):
                            at = ((n * CHUNKS + h) * len(BATCHES) + b) + t * 2 * len(BATCHES)
                            if not (first and n == 0 and h == 0 and b == 0):
                                hold(pe, "pe", attr_copied, at)
                            for i, g in enumerate(tiles):
                                mm = nc.tensor.transpose(psT[0:Q * FD, i * P:(i + 1) * P],
                                                         IN[h][:, g * Q * FD:(g + 1) * Q * FD], IDENT[:, :])
                            mm.then_inc(attr_turned, 1)
                            hold(pe, "pe", attr_copied, at + 1)
                            if not (first and n == 0 and h == 0 and b == 0):
                                hold(pe, "pe", hid_relu, at)
                            w = len(tiles) * P
                            nc.tensor.matmul(psH[:, 0:w], FW1[:, :], AT[:, 0:w], start=True, stop=True).then_inc(hid_done, 1)
                            hold(pe, "pe", hid_relu, at + 1)
                            for i, g in enumerate(tiles):
                                at_tile = (n * CHUNKS + h) * TILES + g + t * 2 * TILES
                                slot = (h * TILES + g) % 2
                                if not (first and n == 0 and h == 0 and g < 2):
                                    hold(pe, "pe", w_used, at_tile - 1)
                                for b2 in range(2):
                                    mm = nc.tensor.matmul(psW[slot][:, b2 * 512:(b2 + 1) * 512],
                                                          HIDT[:, i * P:(i + 1) * P], FW2[:, b2 * 512:(b2 + 1) * 512],
                                                          start=True, stop=True)
                                mm.then_inc(w_ready, 1)
                return pair

            for n in range(2):
                wait_nodes()
                linear(H)
                loop_pairs(pe, edge_pass(n))
                finish_segments(F)
                wait_nodes()
                linear(AGG)
                linear(H)
            loop_pairs(pe, sum3_products, end=PAIRS - 1)
            sum3_products(PAIRS - 1, False, last=True)
            finish_segments(F)

        @block.vector
        def _(dve):
            v = nc.vector
            st = Steps(dve, dve_step)
            asked, tables, ends, lin_asked, lin_done = [0], [0], [0], [0], [0]

            def ask():
                dve.wait_ge(dve_step, st.n)
                dve.sem_inc(to_act, 1)
                asked[0] += 1
                dve.wait_ge(from_act, asked[0])

            def signal(s):
                dve.wait_ge(dve_step, st.n)
                dve.sem_inc(s, 1)

            def linear_done(calls):
                lin_done[0] += calls
                dve.wait_ge(lin_out, lin_done[0] * GROUPS)

            X3, H3, TA3, TB3, AGG3 = (node3(t) for t in (X, H, TA, TB, AGG))

            def layer_norm():
                st.do(v.tensor_reduce(NA[:, :], X3, AX.X, ALU.add))
                st.do(v.tensor_scalar(NA[:, :], NA[:, :], 1.0 / F, None, ALU.mult))
                st.do(v.tensor_tensor(TA3, X3, spread(NA[:, :], NJ, F), ALU.subtract))
                st.do(v.tensor_tensor(TB[:, :], TA[:, :], TA[:, :], ALU.mult))
                st.do(v.tensor_reduce(NA[:, :], TB3, AX.X, ALU.add))
                st.do(v.tensor_scalar(NA[:, :], NA[:, :], 1.0 / F, EPS, ALU.mult, ALU.add))
                ask()
                st.do(v.reciprocal(NA[:, :], NB[:, :]))
                st.do(v.tensor_tensor(TA3, TA3, spread(NA[:, :], NJ, F), ALU.mult))
                st.do(v.tensor_scalar(H[:, :], TA[:, :], 0.0, None, ALU.max))

            dve.wait_ge(iota_done, 1)
            for w in BD.values():
                st.did(v.memset(w[:, :], 0.0))
            st.did(v.memset(FW1[:, :], 0.0))
            st.did(v.memset(FW2[:, :], 0.0))
            st.did(v.memset(NONE_HOT[:, :], 0.0))
            st.did(v.memset(ONE[:, :], 1.0))
            st.did(v.tensor_copy(ROWF[:, :], ROWI[:, :]))
            st.did(v.tensor_copy(COLF[:, :], COLI[:, :]))
            st.settle()
            signal(zero_ready)
            st.did(v.tensor_copy(COLB[:, :], COLF[:, :]))
            st.did(v.tensor_scalar(IDENT[:, :], COLF[:, :], ROWF[:, 0:1], None, ALU.is_equal))
            st.did(v.tensor_scalar(LOWER[:, :], COLF[:, :], ROWF[:, 0:1], None, ALU.is_lt))
            st.did(v.tensor_scalar(UPPER[:, :], COLF[:, :], ROWF[:, 0:1], None, ALU.is_gt))
            st.settle()
            signal(consts_ready)
            dve.wait_ge(dst_in, 16 * 3)
            st.did(v.tensor_tensor(NORM[:, 1:T], dst_all[:, 0:T - 1], dst_all[:, 1:T], ALU.is_gt))
            st.did(v.tensor_tensor(NORM[:, 0:1], EDGES[:, 1:2], dst_all[:, 0:1], ALU.is_gt))
            st.settle()
            st.do(v.tensor_reduce(SMALL[:, 6:7], NORM[:, :], AX.X, ALU.max))
            signal(unsorted_sum)
            dve.wait_ge(unsorted_sum, 2)
            st.do(v.tensor_scalar(UNSORTED[:, :], psT[0:1, 0:1], 1.0, None, ALU.min))
            signal(unsorted_known)
            dve.wait_ge(x_in, 16)
            layer_norm()
            signal(table_ready)
            st.do(v.tensor_scalar(TA[:, :], H[:, :], -1.0 / 5.0, 1.0, ALU.mult, ALU.add))
            st.do(v.tensor_tensor(TA[:, :], TA[:, :], H[:, :], ALU.mult))
            st.do(v.scalar_tensor_tensor(out=TA[:, :], in0=H[:, :], scalar=1.0, in1=TA[:, :], op0=ALU.subtract, op1=ALU.mult))
            st.do(v.scalar_tensor_tensor(out=X[:, :], in0=TA[:, :], scalar=0.1, in1=X[:, :], op0=ALU.add, op1=ALU.add))
            st.do(v.memset(TB[:, :], 0.0))
            signal(zero_ready)

            def starts(step, where, asked, answered):
                step.do(v.memset(FULL[:, :], 1.0))
                step.do(v.tensor_tensor_scan(NA[:, :], FULL[:, :], CNT[:, :], 0.0, ALU.mult, ALU.add))
                step.do(v.tensor_copy(SMALL[:, 0:1], NA[:, NJ - 1:NJ]))
                dve.sem_inc(asked, 1)
                dve.wait_ge(answered, 1)
                step.do(v.tensor_copy(SMALL[:, 5:6], where))
                step.do(v.tensor_scalar(NA[:, :], NA[:, :], SMALL[:, 5:6], None, ALU.add))

            dve.wait_ge(unsorted_known, 1)
            unsorted = nc.vector.value_load(UNSORTED[0:1, 0:1], min_val=0, max_val=1)
            with dve.If(unsorted > 0):
                od = Steps(dve, order_step)
                od.peeled = False
                for run in range(2):
                    n0 = od.n
                    od.per = 9
                    with dve.Fori(0, T) as t:
                        od.t = t
                        hold(dve, "dve", order_in, (t * 80 + 80 + 16 * T) if run else (t * 16 + 16))
                        v.tensor_copy(COLKEY[:, :], COLUMN["dst"][:, :]).then_inc(order_key, 1)
                        hold(dve, "dve", order_key, t + 1 + run * T)
                        dve.sem_inc(order_keys, 1)
                        hold(dve, "dve", order_spread, t + 1 + run * T)
                        od.do(v.tensor_scalar(col_eq, psT[:, 0:P], COLKEY[:, 0:1], None, ALU.is_equal))
                        od.did(v.tensor_tensor(col_low, col_eq, LOWER[:, :], ALU.mult))
                        od.did(v.tensor_reduce(SMALL[:, 9:10], col_eq, AX.X, ALU.add))
                        od.settle()
                        od.do(v.tensor_reduce(SMALL[:, 10:11], col_low, AX.X, ALU.add))
                        hold(dve, "dve", order_got[run], t * 16 + 16)
                        od.did(v.tensor_tensor(PLACE[:, :], NEXT[:, :], SMALL[:, 10:11], ALU.add))
                        od.did(v.tensor_tensor(NEWNEXT[:, :], NEXT[:, :], SMALL[:, 9:10], ALU.add))
                        od.did(v.tensor_scalar(SMALL[:, 11:12], SMALL[:, 10:11], 1.0, None, ALU.min))
                        od.did(v.scalar_tensor_tensor(out=SMALL[:, 12:13], in0=ROWF[:, :], scalar=float(NPAD), in1=COLKEY[:, :],
                                                      op0=ALU.add, op1=ALU.subtract))
                        od.settle()
                        od.do(v.tensor_tensor(SMALL[:, 12:13], SMALL[:, 12:13], SMALL[:, 11:12], ALU.mult))
                        v.tensor_tensor(NEXTROW[:, :], SMALL[:, 12:13], COLKEY[:, :], ALU.add).then_inc(order_placed, 1)
                    assert od.n - n0 == od.per
                    od.t = None
                    od.n += (T - 1) * od.per
                    if run == 0:
                        dve.wait_ge(order_next, 32)
                        starts(od, psT[:, 0:1], order_totals, order_offsets)
                        od.do(v.tensor_tensor(NA[:, :], NA[:, :], CNT[:, :], ALU.subtract))
                        dve.sem_inc(order_starts, 1)
                dve.wait_ge(spoiled, 48)

            dve.wait_ge(edges_in, 16 * 2)
            st.did(v.memset(SAME[:, 0:1], 0.0))
            st.did(v.tensor_tensor(SAME[:, 1:T], dst_all[:, 1:T], dst_all[:, 0:T - 1], ALU.is_equal))
            st.did(v.tensor_scalar(RIDX[:, :], SRC[:, :], float(R), None, ALU.mult))
            st.did(v.tensor_tensor(NORM[:, :], dst_all, dst_all[:, 0:1].to_broadcast([P, T]), ALU.is_equal))
            st.did(v.tensor_copy(DST0[:, :], dst_all[:, 0:1]))
            st.settle()
            st.did(v.tensor_tensor(RIDX[:, :], RIDX[:, :], typ_all, ALU.add))
            st.did(v.tensor_tensor(SMALL[:, 1:2], dst_all[:, 0:1], EDGES[:, 1:2], ALU.is_equal))
            st.did(v.tensor_tensor(SMALL[:, 2:3], EDGES[:, 0:1], EDGES[:, 1:2], ALU.is_equal))
            st.did(v.tensor_reduce(SMALL[:, 3:4], NORM[:, :], AX.X, ALU.add))
            st.settle()
            st.did(v.tensor_scalar(SMALL[:, 4:5], ROWF[:, :], float(T), -1.0, ALU.mult, ALU.add))
            st.did(v.tensor_tensor(SMALL[:, 2:3], SMALL[:, 1:2], SMALL[:, 2:3], ALU.mult))
            st.settle()
            st.did(v.tensor_tensor(FIRSTROW[:, :], SMALL[:, 3:4], SMALL[:, 4:5], ALU.add))
            st.did(v.tensor_copy(CO16[:, :], SMALL[:, 1:2].to_broadcast([P, F])))
            st.did(v.tensor_copy(A16[:, :], SMALL[:, 2:3].to_broadcast([P, F])))
            st.settle()
            signal(cont_ready)
            dve.wait_ge(cont_turned, 1)
            st.did(v.tensor_copy(CONT_T[:, :], psT[0:F, 0:P]))
            st.did(v.tensor_copy(A_T[:, :], psT[0:F, P:2 * P]))
            st.settle()

            dve.wait_ge(weights_in, N_WEIGHTS)
            for q in range(Q):
                rows = slice(q * HID, (q + 1) * HID)
                st.did(v.tensor_copy(FW2[rows, q * F * F:(q + 1) * F * F].rearrange("k (o i) -> k o i", o=F),
                                     FW2IO[rows, :].rearrange("k (i o) -> k o i", i=F)))
            st.settle()
            signal(fw2_ready)

            def scans(h, src3, w, k, start, s, features=None):
                o = cols(OS[h], w)
                prev = cols(OS[1 - h], w)
                features = features or range(w)
                for f in features:
                    last = v.tensor_tensor_scan(o[:, :, f], SAME[:, bass.ds(k * C, C)], src3[:, :, f],
                                                0.0 if start else prev[:, C - 1, f:f + 1], ALU.mult, ALU.add)
                if w - 1 in features:
                    last.then_inc(s, 1)

            tables_in = [0]

            def split_table():
                tables_in[0] += 1
                dve.wait_ge(table_in, 16 * tables_in[0])
                w = NJ * F
                for part in range(3):
                    st.do(v.tensor_copy(PART[part][:, 0:w], AGG[:, :]))
                    if part < 2:
                        st.do(v.tensor_tensor(AGG[:, :], AGG[:, :], PART[part][:, 0:w], ALU.subtract))

            def dense_columns(name, t, h):
                n2 = BY_PRODUCT[name]
                src_cols = SRC[:, bass.ds(t * 2 * C + (h * C + C - n2), n2)]
                st.did(v.tensor_scalar(DI[0][:, 0:n2], src_cols, P - 1, None, ALU.bitwise_and))
                st.did(v.tensor_scalar(DI[1][:, 0:n2], src_cols, 7, None, ALU.logical_shift_right))
                st.settle()
                slot = h % 2 * 16
                st.did(v.tensor_copy(DK[0][:, slot:slot + n2], DI[0][:, 0:n2]))
                st.did(v.tensor_copy(DK[1][:, slot:slot + n2], DI[1][:, 0:n2]))
                st.settle()
                dve.sem_inc(dense_cols, 1)

            def hot(slot, keys):
                hold(dve, "dve", dense_keys, keys)
                v.tensor_scalar(HOTLO[slot][:, :], psT[:, 0:2 * P], ROWF[:, 0:1], None, ALU.is_equal)
                v.tensor_scalar(OFFHI[slot][:, :], psT[:, 2 * P:4 * P], ROWF[:, 0:1], None, ALU.not_equal)\
                    .then_inc(dense_hot, 1)

            def dense_start(name):
                dense_columns(name, 0, 0)
                hot(0, DENSE[name][1] + 1)

            def dense(name, t, h, start, last, between):
                chunk0, pair0, half0 = DENSE[name]
                n2 = BY_PRODUCT[name]
                pairs = n2 // 2
                done = t * 2 * pairs + h * pairs
                found = GB[h][:, (C - n2) * F:C * F]

                def read(j):
                    for i in range(2):
                        for half in range(2):
                            hold(dve, "dve", dense_sum, done * 4 + half0 + 4 * j + 2 * i + half + 1)
                            o = (found, OTHER)[half][:, (2 * j + i) * F:(2 * j + i + 1) * F]
                            v.tensor_reduce(o, psW[half][:, :].rearrange("p (b x) -> p b x", b=2)[:, :, 0:QB * F]
                                            .rearrange("p b (q f) -> p f b q", f=F), AX.XY, ALU.max).then_inc(dense_read, 1)
                            between(4 * j + 2 * i + half)

                if not start:
                    hold(dve, "dve", dense_done, t * 2 + h + chunk0)
                for j in range(pairs):
                    if j == pairs - 2 and not last:
                        dense_columns(name, t, h + 1)
                    if j + 1 < pairs or not last:
                        hot((h * pairs + j + 1) % 2, done + pair0 + j + 2)
                    read(j)
                hold(dve, "dve", dense_read, done * 4 + half0 + 4 * pairs)
                v.tensor_tensor(found, found, OTHER[:, 0:n2 * F], ALU.max).then_inc(dense_done, 1)

            st.did(v.tensor_copy(IDENTB[:, :], IDENT[:, :]))
            st.did(v.memset(PUSH[:, NJ * F:BLOCKS * F], -HUGE))
            st.did(v.tensor_scalar(PUSH[:, 0:NJ * F].rearrange("p (b f) -> p b f", f=F), spread(IDENT[:, 0:NJ], NJ, F), -HUGE, None, ALU.mult))
            for part in range(3):
                st.did(v.memset(PART[part][:, NJ * F:BLOCKS * F], 0.0))
            st.settle()
            split_table()

            def hist_pair(t, first, last=False):
                for h in range(2):
                    k = t * 2 + h

                    def hist_columns():
                        hold(dve, "dve", hist_in[h], (t + 1) * 32)
                        st.did(v.tensor_scalar(LOI[:, :], EDST[h][:, :], P - 1, None, ALU.bitwise_and))
                        st.did(v.tensor_scalar(HII[:, :], EDST[h][:, :], 7, None, ALU.logical_shift_right))
                        st.settle()
                        st.did(v.tensor_copy(LOB[:, :], LOI[:, :]))
                        st.did(v.tensor_copy(HIB[:, :], HII[:, :]))
                        st.did(v.tensor_tensor(cols(TH, R), over(COLF[:, 0:R], C, R), spread(ETYP[h][:, :], C, R), ALU.is_equal))
                        st.settle()
                        dve.sem_inc(hist_read, 1)

                    def hist_hot(b, part):
                        if part == 0 and not (first and h == 0):
                            hold(dve, "dve", hot_used, k * 2 + b - 1)
                        a, z = part * HALF // HIST_PARTS, (part + 1) * HALF // HIST_PARTS
                        sl = slice(b * HALF + a, b * HALF + z)
                        st.did(v.tensor_tensor(hot_lo[b][:, a:z, :], over(COLB[:, :], z - a, P), spread(LOB[:, sl], z - a, P), ALU.is_equal))
                        hi = v.tensor_tensor(hot_hi[b][:, a:z, :], over(COLB[:, 0:NJ], z - a, NJ),
                                             spread(HIB[:, sl], z - a, NJ), ALU.is_equal)
                        if part == HIST_PARTS - 1:
                            hi.then_inc(hot_ready, 1)

                    def type_scans(half):
                        if half == 0:
                            if not first:
                                hold(dve, "dve", types_stored[h], t * 16)
                            if not (first and h == 0):
                                hold(dve, "dve", scanned["xi"], k)
                        scans(h, cols(TH, R), R, k, first and h == 0, scanned["xi"],
                              range(half * R // 2, (half + 1) * R // 2))

                    steps = {0: hist_columns, 17: lambda: type_scans(0), 18: lambda: type_scans(1)}
                    for b in range(2):
                        for part in range(HIST_PARTS):
                            steps[2 + (b * HIST_PARTS + part) * 2] = lambda b=b, part=part: hist_hot(b, part)

                    def between(n):
                        if n in steps:
                            steps[n]()

                    if not first:
                        hold(dve, "dve", stored["xi"][h], t * 16)
                    dense("xi", t, h, first and h == 0, last and h == 1, between)

            dense_start("xi")
            loop_pairs(dve, hist_pair, st, end=PAIRS - 1)
            hist_pair(PAIRS - 1, False, last=True)
            dve.wait_ge(hist_done, 1)
            st.do(v.tensor_copy(HIDT[0:NJ, 0:P], psH[0:NJ, 0:P]))
            signal(hist_copied)

            def finish_segments(name, w, dest):
                ends[0] += 1
                n = ends[0]
                dve.wait_ge(scanned["xi" if name == "types" else name], CHUNKS)
                st.do(v.tensor_copy(LAST[:, 0:w], cols(OS[1], w)[:, C - 1, :]))
                signal(last_ready)
                dve.wait_ge(last_turned, n)
                st.did(v.memset(B_T[:, 0:1], 0.0))
                st.did(v.tensor_tensor(B_T[0:w, 1:P], psT[0:w, 0:P - 1], CONT_T[0:w, 1:P], ALU.mult))
                st.settle()
                st.do(v.tensor_tensor_scan(CARRY_T[0:w, :], A_T[0:w, :], B_T[0:w, :], 0.0, ALU.mult, ALU.add))
                signal(carry_ready)
                dve.wait_ge(carry_turned, n)
                st.do(v.tensor_copy(CARRY[:, 0:w], psT[:, P:P + w]))
                signal(carry_out)
                dve.wait_ge(ends_in, 16 * NJ * n)
                st.do(v.tensor_tensor(node3(dest, w), node3(dest, w), spread(FULL[:, :], NJ, w), ALU.mult))

            dve.wait_ge(count_in, 16)
            starts(st, psH[:, 0:1], totals_ready, offsets_ready)
            st.did(v.tensor_scalar(END[:, :], NA[:, :], -1.0, 0.0, ALU.add, ALU.max))
            st.did(v.tensor_tensor(NA[:, :], NA[:, :], CNT[:, :], ALU.subtract))
            st.did(v.tensor_scalar(FULL[:, :], CNT[:, :], 1.0, None, ALU.min))
            st.did(v.tensor_scalar(NB[:, :], ROWF[:, 0:1].to_broadcast([P, NJ]), float(NJ), float(EP), ALU.mult, ALU.add))
            st.settle()
            st.do(v.tensor_tensor(NB[:, :], NB[:, :], COLF[:, 0:NJ], ALU.add))
            st.do(v.tensor_tensor(NA[:, :], NA[:, :], NB[:, :], ALU.subtract))
            st.do(v.tensor_tensor(NA[:, :], NA[:, :], FULL[:, :], ALU.mult))
            st.do(v.tensor_tensor(START[:, :], NA[:, :], NB[:, :], ALU.add))
            finish_segments("types", R, type_cnt)
            st.do(v.tensor_scalar(type_cnt, type_cnt, 1.0, None, ALU.max))
            st.did(v.reciprocal(node_ext[:, :, F:NE], node3(type_cnt, R)))
            st.did(v.tensor_copy(node_ext[:, :, 0:F], H3))
            st.settle()
            signal(table_ready)
            dve.wait_ge(starts_out, 16 * NJ)
            dve.wait_ge(first_in, 16)
            st.did(v.tensor_copy(KT[:, :], ROWF[:, 0:1].to_broadcast([P, C])))
            st.did(v.memset(msg[:, :, F:ACC], 1.0))
            st.settle()

            def msg_pair(t, first):
                for h in range(2):
                    k = t * 2 + h
                    st.settle()
                    hold(dve, "dve", msg_in[h], (t + 1) * 64)
                    if first and h == 0:
                        v.tensor_copy(GB[h][:, 0:NE], FIRST[:, :]).then_inc(first_placed, 1)
                        dve.wait_ge(first_placed, 1)
                    if not (first and h == 0):
                        hold(dve, "dve", msg_scanned, k)
                        hold(dve, "dve", key_spread, t * 2 * TILES + h * TILES)
                    st.did(v.tensor_copy(KEY[:, :], SRC[:, bass.ds(k * C, C)]))
                    st.settle()
                    dve.sem_inc(key_ready, 1)
                    scans(h, cols(GB[h], NE), NE, k, first and h == 0, msg_scanned)
                    st.did(v.tensor_tensor(cols(TH, R), over(COLF[:, 0:R], C, R), spread(ETYP[h][:, :], C, R), ALU.is_equal))
                    hold(dve, "dve", msg_scanned, k + 1)
                    st.settle()
                    xj, xi = cols(OS[h], NE)[:, :, 0:F], cols(IN[h], F)
                    dn, mm = cols(GB[h], F), msg[:, :, 0:F]
                    st.did(v.tensor_tensor(cols(TH, R), cols(TH, R), cols(OS[h], NE)[:, :, F:NE], ALU.mult))
                    st.did(v.tensor_scalar(dn, xj, 0.1, 5.0, ALU.mult, ALU.add))
                    if not (first and h == 0):
                        hold(dve, "dve", merged, k * 2)
                    st.did(v.tensor_tensor(mm, xi, xj, ALU.mult))
                    st.settle()
                    st.did(v.tensor_reduce(DUP[:, :], cols(TH, R), AX.X, ALU.add))
                    st.did(v.scalar_tensor_tensor(out=dn, in0=xi, scalar=0.9, in1=dn, op0=ALU.mult, op1=ALU.add))
                    st.did(v.tensor_tensor(mm, mm, spread(EWT[h][:, :], C, F), ALU.mult))
                    st.settle()
                    st.did(v.tensor_copy(NORM[:, bass.ds(k * C, C)], DUP[:, :]))
                    st.do(v.reciprocal(dn, dn))
                    st.do(v.tensor_tensor(mm, mm, dn, ALU.mult))
                    dve.sem_inc(msg_read, 1)
                    for g in range(TILES):
                        bank = psW[(h * TILES + g) % 2][:, 0:Q * P].rearrange("p (c k) -> p c k", c=Q)
                        gs = slice(g * Q, (g + 1) * Q)
                        hold(dve, "dve", key_spread, t * 2 * TILES + h * TILES + g + 1)
                        v.tensor_tensor(meq[:, gs, :], bank, spread(KEY[:, gs], Q, P), ALU.is_equal).then_inc(eq_done, 1)
                        hold(dve, "dve", eq_done, t * 2 * TILES + h * TILES + g + 1)
                        st.do(v.tensor_tensor(meq_low, meq[:, gs, :], over(LOWER[:, :], Q, P), ALU.mult))
                        st.did(v.tensor_reduce(DUP[:, gs], meq_low, AX.X, ALU.add))
                    st.settle()
                    dve.sem_inc(msg_ready, 1)
                    st.do(v.tensor_scalar(DUP[:, :], DUP[:, :], 1.0, None, ALU.min))
                    st.do(v.scalar_tensor_tensor(out=TH[:, 0:C], in0=KT[:, :], scalar=float(NPAD), in1=KEY[:, :],
                                                 op0=ALU.add, op1=ALU.subtract))
                    st.do(v.tensor_tensor(DUP[:, :], DUP[:, :], TH[:, 0:C], ALU.mult))
                    if not first:
                        for i in range(2):
                            hold(dve, "dve", scattered[i], t * 16 * C - (1 - h) * 8 * C)
                    v.tensor_tensor(IDX[h][:, :], DUP[:, :], KEY[:, :], ALU.add).then_inc(scat_idx_ready, 1)
                    hold(dve, "dve", scat_idx_ready, k + 1)

            loop_pairs(dve, msg_pair, st)
            dve.wait_ge(merged, 2 * CHUNKS)
            st.do(v.memset(acc_sum, 0.0))
            for r in range(2 * SET):
                dve.wait_ge(acc_loaded[r % 4], 16 * (r // 4 + 1))
                st.do(v.tensor_tensor(acc_sum, acc_sum, acc_in[r % 4], ALU.add))
                signal(acc_used)
            sum3 = acc_sum.rearrange("p (j k) -> p j k", j=NJ)
            st.did(v.tensor_tensor(X3, X3, sum3[:, :, 0:F], ALU.add))
            st.did(v.tensor_copy(OUTDEG[:, :], sum3[:, :, F]))
            st.settle()
            layer_norm()
            signal(lin_in)

            def scan_pass(name, normed):
                def pair(t, first):
                    for h in range(2):
                        k = t * 2 + h
                        hold(dve, "dve", gathered[name][h], (t + 1) * gathers(name))
                        if not first:
                            hold(dve, "dve", stored[name][h], t * 16)
                        if not (first and h == 0):
                            hold(dve, "dve", scanned[name], k)
                        if normed:
                            st.did(v.tensor_tensor(cols(GB[h], F), cols(GB[h], F), spread(NORM[:, bass.ds(k * C, C)], C, F), ALU.mult))
                            st.settle()
                        scans(h, cols(GB[h], F), F, k, first and h == 0, scanned[name])
                return pair

            for n, name in enumerate(("conv1", "conv2")):
                linear_done(2)
                loop_pairs(dve, scan_pass(name, True), st)
                finish_segments(name, F, AGG)
                st.do(v.tensor_tensor(AGG[:, :], AGG[:, :], ROOT[:, :], ALU.add))
                st.do(v.tensor_tensor(AGG3, AGG3, over((B1, B2)[n][:, :], NJ, F), ALU.add))
                if n == 0:
                    st.do(v.tensor_scalar(H[:, :], AGG[:, :], 0.0, None, ALU.max))
                    signal(lin_in)
            st.do(v.tensor_reduce(NA[:, :], AGG3, AX.X, ALU.max))
            st.do(v.tensor_tensor(TB3, AGG3, spread(NA[:, :], NJ, F), ALU.subtract))
            ask()
            st.do(v.tensor_reduce(NA[:, :], TA3, AX.X, ALU.add))
            ask()
            st.do(v.tensor_tensor(TB3, TB3, spread(NB[:, :], NJ, F), ALU.subtract))
            st.do(v.tensor_tensor(X[:, :], X[:, :], TB[:, :], ALU.add))
            layer_norm()

            def edge_pass(name, n):
                def mult(t, h, g):
                    at = t * 2 * TILES + (n * CHUNKS + h) * TILES + g
                    hold(dve, "dve", w_ready, at + 1)
                    if g >= 3:
                        hold(dve, "dve", m_reduced, at - 2)
                    bank = psW[(h * TILES + g) % 2][:, :].rearrange("p (c o i) -> p c o i", c=Q, o=F)
                    xs = cols(GB[h], 2 * F)[:, g * Q:(g + 1) * Q, 0:F].unsqueeze(2).to_broadcast([P, Q, F, F])
                    v.tensor_tensor(prod[g % 3].rearrange("p (c o i) -> p c o i", c=Q, o=F), bank, xs, ALU.mult).then_inc(w_used, 1)

                def reduce(t, h, g):
                    hold(dve, "dve", w_used, t * 2 * TILES + (n * CHUNKS + h) * TILES + g + 1)
                    v.tensor_reduce(m_edge[:, g * Q:(g + 1) * Q, :], prod[g % 3].rearrange("p (c o i) -> p c o i", c=Q, o=F),
                                    AX.X, ALU.add).then_inc(m_reduced, 1)

                def pair(t, first):
                    for h in range(2):
                        k = t * 2 + h
                        hold(dve, "dve", gathered[name][h], (t + 1) * gathers(name))
                        if not (first and h == 0):
                            hold(dve, "dve", scanned[name], k)
                        mult(t, h, 0)
                        for g in range(1, TILES):
                            mult(t, h, g)
                            reduce(t, h, g - 1)
                        reduce(t, h, TILES - 1)
                        hold(dve, "dve", m_reduced, t * 2 * TILES + (n * CHUNKS + h + 1) * TILES)
                        st.did(v.tensor_tensor(m_edge, m_edge, cols(GB[h], 2 * F)[:, :, F:2 * F], ALU.add))
                        st.settle()
                        if not first:
                            hold(dve, "dve", stored[name][h], t * 16)
                        scans(h, m_edge, F, k, first and h == 0, scanned[name])
                return pair

            for n, name in enumerate(("edge1", "edge2")):
                signal(lin_in)
                st.did(v.tensor_copy(pair_tab[:, :, 0:F], H3))
                st.settle()
                linear_done(1)
                signal(table_ready)
                dve.wait_ge(table_stored, 16 * (3 + n))
                loop_pairs(dve, edge_pass(name, n), st)
                finish_segments(name, F, AGG)
                st.do(v.tensor_scalar(NA[:, :], CNT[:, :], 1.0, None, ALU.max))
                st.do(v.reciprocal(NA[:, :], NA[:, :]))
                st.do(v.tensor_tensor(AGG3, AGG3, spread(NA[:, :], NJ, F), ALU.mult))
                signal(lin_in)
                linear_done(2)
                st.did(v.tensor_tensor(GI, GI, over(BIH[:, :], NJ, 3 * F), ALU.add))
                st.did(v.tensor_tensor(GH, GH, over(BHH[:, :], NJ, 3 * F), ALU.add))
                st.settle()
                st.do(v.tensor_tensor(GI[:, :, 0:2 * F], GI[:, :, 0:2 * F], GH[:, :, 0:2 * F], ALU.add))
                ask()
                st.do(v.tensor_tensor(TB3, GI[:, :, 0:F], GH[:, :, 2 * F:3 * F], ALU.mult))
                st.do(v.tensor_tensor(TB3, TB3, GI[:, :, 2 * F:3 * F], ALU.add))
                ask()
                st.do(v.tensor_tensor(TB[:, :], H[:, :], TA[:, :], ALU.subtract))
                st.do(v.tensor_tensor(TB3, TB3, GI[:, :, F:2 * F], ALU.mult))
                st.do(v.tensor_tensor(H[:, :], TA[:, :], TB[:, :], ALU.add))
            st.do(v.tensor_tensor(X[:, :], X[:, :], H[:, :], ALU.add))
            layer_norm()
            st.do(v.tensor_scalar(NA[:, :], OUTDEG[:, :], 1.0, None, ALU.max))
            ask()
            st.do(v.reciprocal(NA[:, :], NB[:, :]))
            st.do(v.tensor_tensor(H3, H3, spread(NA[:, :], NJ, F), ALU.mult))
            signal(table_ready)
            split_table()

            def sum3_scan(t, h, first, quarter):
                k = t * 2 + h
                features = range(quarter * F // 4, (quarter + 1) * F // 4)
                if quarter > 0:
                    scans(h, cols(GB[h], F), F, k, first and h == 0, scanned["sum3"], features)
                    return
                hold(dve, "dve", gathered["sum3"][h], (t + 1) * gathers("sum3"))
                hold(dve, "dve", dense_done, DENSE["sum3"][0] + k + 1)
                if not first:
                    hold(dve, "dve", stored["sum3"][h], t * 16)
                if not (first and h == 0):
                    hold(dve, "dve", scanned["sum3"], k)
                scans(h, cols(GB[h], F), F, k, first and h == 0, scanned["sum3"], features)

            def sum3_dense(t, h, first, last=False, scan=None):
                if not first:
                    hold(dve, "dve", scanned["sum3"], t * 2 + h - 1)
                dense("sum3", t, h, scan is None, last, lambda n: scan(SCAN_AT.index(n)) if scan and n in SCAN_AT else None)

            def sum3_pair(t, first, last=False):
                sum3_dense(t, 1, first, last, lambda quarter: sum3_scan(t, 0, first, quarter))
                if last:
                    for quarter in range(4):
                        sum3_scan(t, 1, first, quarter)
                else:
                    sum3_dense(t + 1, 0, False, False, lambda quarter: sum3_scan(t, 1, first, quarter))

            dense_start("sum3")
            sum3_dense(0, 0, True)
            loop_pairs(dve, sum3_pair, st, end=PAIRS - 1)
            sum3_pair(PAIRS - 1, False, last=True)
            finish_segments("sum3", F, AGG)
            st.do(v.tensor_scalar(NA[:, :], CNT[:, :], 1.0, None, ALU.max))
            ask()
            st.do(v.reciprocal(NA[:, :], NB[:, :]))
            st.do(v.tensor_tensor(AGG3, AGG3, spread(NA[:, :], NJ, F), ALU.mult))
            st.do(v.tensor_tensor(X[:, :], X[:, :], AGG[:, :], ALU.add))
            signal(out_ready)


_INS = ['x', 'src', 'dst', 'edge_attr_13', 'edge_type_8', 'edge_weight', 'L1_gnn_W1', 'L1_gnn_root1', 'L1_gnn_b1',
        'L1_gnn_W2', 'L1_gnn_root2', 'L1_gnn_b2', 'L2_gnn_fnet_w1', 'L2_gnn_fnet_b1', 'L2_gnn_fnet_w2',
        'L2_gnn_fnet_b2', 'L2_gnn_gru_w_ih', 'L2_gnn_gru_w_hh', 'L2_gnn_gru_b_ih', 'L2_gnn_gru_b_hh']


def kernel(**inputs):
    import numpy as _np
    import concourse.bacc as _bacc
    from concourse import mybir as _mybir
    from concourse.bass_utils import run_bass_kernel_spmd as _run

    nc = _bacc.Bacc("TRN2", target_bir_lowering=False, num_devices=1)
    rows = {'x': (NPAD, 0), 'src': (EP, N), 'dst': (EP, N), 'edge_attr_13': (EP, 0), 'edge_type_8': (EP, 0),
            'edge_weight': (EP, 0)}
    arrays, args = {}, []
    for name in _INS:
        a = _np.ascontiguousarray(inputs[name])
        if name in rows:
            n, fill = rows[name]
            a = _np.concatenate([a, _np.full((n - a.shape[0],) + a.shape[1:], fill, a.dtype)])
        arrays[f"in_{name}_dram"] = a
        args.append(nc.dram_tensor(f"in_{name}_dram", a.shape, _mybir.dt.from_np(a.dtype), kind="ExternalInput").ap())
    out = nc.dram_tensor("out_0_dram", (N, F), F32, kind="ExternalOutput").ap()
    gnn_kernel(nc, *args, out)
    r = _run(nc, [arrays], core_ids=[0])
    return r.results[0]["out_0_dram"]
```

```python
from contextlib import ExitStack

import concourse.bass as bass
from concourse import mybir

F32 = mybir.dt.float32
I32 = mybir.dt.int32
BF16 = mybir.dt.bfloat16
ALU = mybir.AluOpType
ACT = mybir.ActivationFunctionType
AX = mybir.AxisListType

P = 128
N, E = 12500, 412500
F = 16
R = 8
FD, HID = 13, 32
NJ = -(-N // P)
NPAD = NJ * P
C = 52
CHUNKS = 62
PAIRS = CHUNKS // 2
T = C * CHUNKS
EP = T * P
assert EP >= E and EP - E < 4 * P and NPAD > N
HALF = C // 2
G = 7
GROUPS = NJ // G
Q = 4
TILES = C // Q
NE = F + R
ACC = F + 1
SET = 13
SETS = C // SET
assert SETS % 2 == 0
BY_PRODUCT = {"xi": 10, "conv1": 12, "conv2": 12, "edge1": Q, "edge2": Q, "sum3": 12}
HUGE = 2.0 ** 100
QB = 25
BLOCKS = 4 * QB
HIST_PAIRS = (2, 4)
HIST_PARTS = 4
TURNS = BY_PRODUCT["conv1"] // Q
assert BY_PRODUCT["conv1"] == BY_PRODUCT["conv2"] == TURNS * Q
BATCHES = [range(a, min(a + 4, TILES)) for a in range(0, TILES, 4)]
EPS = 1e-5
BIG = 9408


def gathers(name):
    return 16 * (C - BY_PRODUCT.get(name, 0))


class Steps:

    def __init__(self, eng, sem):
        self.eng, self.sem, self.n, self.t, self.per, self.peeled = eng, sem, 0, None, 0, True

    def did(self, ins):
        ins.then_inc(self.sem, 1)
        self.n += 1

    def settle(self):
        at = self.n if self.t is None else self.t * self.per + (self.n - self.per * self.peeled)
        self.eng.wait_ge(self.sem, at)

    def do(self, ins):
        self.did(ins)
        self.settle()


def loop_pairs(eng, body, steps=None, end=PAIRS):
    n0 = steps.n if steps else 0
    body(0, True)
    if steps:
        steps.per = steps.n - n0
    with eng.Fori(1, end) as t:
        if steps:
            steps.t = t
            n1 = steps.n
        body(t, False)
        if steps:
            assert steps.n - n1 == steps.per
            steps.t = None
            steps.n += (end - 2) * steps.per


def gnn_kernel(nc, x, src, dst, edge_attr, edge_type, edge_weight, W1, root1, b1, W2, root2, b2,
               fw1, fb1, fw2, fb2, w_ih, w_hh, b_ih, b_hh, out):
    ctx = ExitStack()
    with ctx:
        ctx.enter_context(nc.allow_non_contiguous_dma(reason="small weights turned while they load"))

        def sb(name, shape, dt=F32):
            return ctx.enter_context(nc.sbuf_tensor(name, shape, dt))

        def ps(name, width):
            return ctx.enter_context(nc.psum_tensor(name, [P, width], F32))

        def sem(name):
            return ctx.enter_context(nc.semaphore(name))

        def dram(name, shape, dt=F32):
            return nc.dram_tensor(name, shape, dt).ap()

        h_rows = dram("h_rows", (NPAD, F))
        rel_rows = dram("rel_rows", (NPAD * R, F))
        pair_rows = dram("pair_rows", (NPAD, 2 * F))
        xi_rows = dram("xi_rows", (EP, F))
        seg_rows = dram("seg_rows", (EP, F))
        type_rows = dram("type_rows", (EP, R))
        spread_rows = dram("spread_rows", (EP + NPAD, NE))
        node_rows = dram("node_rows", (NPAD, NE))
        count_row = dram("count_row", (NJ, P))
        accs = [dram(f"acc{r}", (NPAD + P, ACC)) for r in range(2 * SET)]

        given = {"src": src, "dst": dst, "type": edge_type, "weight": edge_weight, "attr": edge_attr}
        ordered = {"src": dram("ordered_src", (EP, 1), I32), "dst": dram("ordered_dst", (EP, 1), I32),
                   "type": dram("ordered_type", (EP, 1), I32), "weight": dram("ordered_weight", (EP, 1)),
                   "attr": dram("ordered_attr", (EP, FD))}
        next_rows = dram("next_rows", (NPAD + P, 1))

        SRC, RIDX = sb("SRC", [P, T], I32), sb("RIDX", [P, T], I32)
        SAME, NORM = sb("SAME", [P, T]), sb("NORM", [P, T])
        X, H, TA, TB, AGG = (sb(n, [P, NJ * F]) for n in ("X", "H", "TA", "TB", "AGG"))
        ROOT = sb("ROOT", [P, NJ * F])
        CNT, END, START = sb("CNT", [P, NJ]), sb("END", [P, NJ], I32), sb("START", [P, NJ], I32)
        FULL, OUTDEG, NA, NB = (sb(n, [P, NJ]) for n in ("FULL", "OUTDEG", "NA", "NB"))
        big = sb("big", [P, BIG])
        GB = [sb(f"GB{h}", [P, C * 2 * F]) for h in range(2)]
        OS = [sb(f"OS{h}", [P, C * NE]) for h in range(2)]
        IN = [sb(f"IN{h}", [P, C * F]) for h in range(2)]
        ROWS = [sb(f"ROWS{h}", [P, C * ACC]) for h in range(2)]
        IDX = [sb(f"IDX{h}", [P, C], I32) for h in range(2)]
        EDST = [sb(f"EDST{h}", [P, C], I32) for h in range(2)]
        ETYP = [sb(f"ETYP{h}", [P, C], I32) for h in range(2)]
        EWT = [sb(f"EWT{h}", [P, C]) for h in range(2)]
        KEY, DUP, KT = (sb(n, [P, C]) for n in ("KEY", "DUP", "KT"))
        LOI, HII = sb("LOI", [P, C], I32), sb("HII", [P, C], I32)
        LOB, HIB = sb("LOB", [P, C], BF16), sb("HIB", [P, C], BF16)
        TH = sb("TH", [P, C * R])
        ROWI, COLI = sb("ROWI", [P, 1], I32), sb("COLI", [P, P], I32)
        ROWF, COLF = sb("ROWF", [P, 1]), sb("COLF", [P, P])
        COLB = sb("COLB", [P, P], BF16)
        NONE_HOT, ONE = sb("NONE_HOT", [P, P]), sb("ONE", [P, 1])
        IDENT, LOWER, UPPER = sb("IDENT", [P, P]), sb("LOWER", [P, P]), sb("UPPER", [P, P])
        EDGES = sb("EDGES", [P, 4], I32)
        SMALL = sb("SMALL", [P, 16])
        UNSORTED = sb("UNSORTED", [1, 1], I32)
        COLUMN = {n: sb(f"COLUMN_{n}", [P, FD if n == "attr" else 1], F32 if n in ("weight", "attr") else I32) for n in given}
        COLKEY, NEXT, NEWNEXT = sb("COLKEY", [P, 1]), sb("NEXT", [P, 1]), sb("NEWNEXT", [P, 1])
        PLACE, NEXTROW = sb("PLACE", [P, 1], I32), sb("NEXTROW", [P, 1], I32)
        FIRSTROW, DST0 = sb("FIRSTROW", [P, 1], I32), sb("DST0", [P, 1], I32)
        FIRST = sb("FIRST", [P, NE])
        CO16, A16 = sb("CO16", [P, F]), sb("A16", [P, F])
        CONT_T, A_T, B_T, CARRY_T = (sb(n, [F, P]) for n in ("CONT_T", "A_T", "B_T", "CARRY_T"))
        LAST, CARRY = sb("LAST", [P, F]), sb("CARRY", [P, F])
        BD = {name: sb(f"BD_{name}", [G * F, G * w]) for name, w in
              (("rel", R * F), ("root", F), ("b2", F), ("ih", 3 * F), ("hh", 3 * F))}
        HT = [sb(f"HT{i}", [G * F, P]) for i in range(2)]
        B1, B2 = sb("B1", [P, F]), sb("B2", [P, F])
        BIH, BHH = sb("BIH", [P, 3 * F]), sb("BHH", [P, 3 * F])
        FW1 = sb("FW1", [Q * FD, Q * HID])
        FB1 = sb("FB1", [P, 1])
        FB2, ONES = sb("FB2", [1, F * F]), sb("ONES", [1, P])
        FW2IO, FW2 = sb("FW2IO", [P, F * F]), sb("FW2", [P, Q * F * F])
        PART = [sb(f"PART{i}", [P, BLOCKS * F], BF16) for i in range(3)]
        PUSH = sb("PUSH", [P, BLOCKS * F], BF16)
        IDENTB = sb("IDENTB", [P, P], BF16)
        TI = sb("TI", [P, 16], I32)
        DI = [sb(f"DI{i}", [P, 16], I32) for i in range(2)]
        DK = [sb(f"DK{i}", [P, 2 * 16], BF16) for i in range(2)]
        HOTLO = [sb(f"HOTLO{i}", [P, 2 * P], BF16) for i in range(2)]
        OFFHI = [sb(f"OFFHI{i}", [P, 2 * P], BF16) for i in range(2)]
        WREL = [sb(f"WREL{i}", [R * F, F]) for i in range(2)]
        OTHER = sb("OTHER", [P, 16 * F])
        HIDT = sb("HIDT", [P, 4 * P])

        psW = [ps(f"psW{i}", 2 * 512) for i in range(2)]
        psM = ps("psM", 2 * 512)
        psT, psH = ps("psT", 512), ps("psH", 512)
        turn_banks, lin_banks = [psT, psH], [psM, psW[0]]

        dst_all = big[:, 0:T].bitcast(I32)
        typ_all = big[:, T:2 * T].bitcast(I32)
        hot_w = HALF * P // 2
        hoth_w = HALF * NJ // 2
        hot_lo = [big[:, i * hot_w:(i + 1) * hot_w].bitcast(BF16).rearrange("p (c k) -> p c k", c=HALF) for i in range(2)]
        hot_hi = [big[:, 2 * hot_w + i * hoth_w:2 * hot_w + (i + 1) * hoth_w].bitcast(BF16)
                  .rearrange("p (c k) -> p c k", c=HALF) for i in range(2)]
        zeros = TB[:, 0:C * NE]
        col_eq, col_low = big[:, 2 * T:2 * T + P], big[:, 2 * T + P:2 * T + 2 * P]
        meq = big[:, 0:C * P].rearrange("p (c k) -> p c k", c=C)
        meq_low = big[:, C * P:C * P + Q * P].rearrange("p (c k) -> p c k", c=Q)
        msg_at = [C * P + Q * P + h * C * ACC for h in range(2)]
        msg = [big[:, at:at + C * ACC].rearrange("p (c k) -> p c k", c=C) for at in msg_at]
        acc_in = [big[:, r * NJ * ACC:(r + 1) * NJ * ACC] for r in range(4)]
        acc_sum = big[:, 4 * NJ * ACC:5 * NJ * ACC]
        node_ext = big[:, 0:NJ * NE].rearrange("p (j k) -> p j k", j=NJ)
        type_cnt = big[:, NJ * NE:NJ * (NE + R)]
        by_type = [big[:, 2 * G * R * F + i * Q * P:2 * G * R * F + (i + 1) * Q * P] for i in range(2)]
        by_type_t = [big[:, 2 * G * R * F + (2 + i) * Q * P:2 * G * R * F + (3 + i) * Q * P] for i in range(2)]
        stage = [big[:, i * G * R * F:(i + 1) * G * R * F] for i in range(2)]
        pair_tab = big[:, 0:NJ * 2 * F].rearrange("p (j k) -> p j k", j=NJ)
        prod = [big[:, i * Q * F * F:(i + 1) * Q * F * F] for i in range(3)]
        m_edge = big[:, 3 * Q * F * F:3 * Q * F * F + C * F].rearrange("p (c k) -> p c k", c=C)
        AT = big[0:Q * FD, 4 * Q * F * F:4 * Q * F * F + 4 * P]
        HIDT_OF = [HIDT, big[:, 5 * Q * F * F:5 * Q * F * F + 4 * P]]
        GI = big[:, 0:NJ * 3 * F].rearrange("p (j k) -> p j k", j=NJ)
        GH = big[:, NJ * 3 * F:2 * NJ * 3 * F].rearrange("p (j k) -> p j k", j=NJ)

        def node3(t, w=F):
            return t[:, 0:NJ * w].rearrange("p (j k) -> p j k", j=NJ)

        def cols(t, w):
            return t[:, 0:C * w].rearrange("p (c k) -> p c k", c=C)

        def spread(col, n, w):
            return col.unsqueeze(2).to_broadcast([P, n, w])

        def over(row, n, w):
            return row.unsqueeze(1).to_broadcast([P, n, w])

        PASSES = ["xi", "conv1", "conv2", "edge1", "edge2", "sum3"]
        idx_ready = {q: sem(f"{q}_idx_ready") for q in PASSES}
        gathered = {q: [sem(f"{q}_gathered{h}") for h in range(2)] for q in PASSES}
        scanned = {q: sem(f"{q}_scanned") for q in PASSES}
        stored = {q: [sem(f"{q}_stored{h}") for h in range(2)] for q in PASSES}
        held = {e: sem(f"held_{e}") for e in ("pool", "act", "pe", "dve", "sp")}
        dst_in, spoiled, unsorted_sum, unsorted_known = (
            sem(n) for n in ("dst_in", "spoiled", "unsorted_sum", "unsorted_known"))
        order_next, order_turn, order_in, order_key, order_keys, order_spread, order_placed, \
            order_step, order_totals, order_offsets, order_starts = (
                sem(f"order_{n}") for n in ("next", "turn", "in", "key", "keys", "spread", "placed",
                                            "step", "totals", "offsets", "starts"))
        order_got, order_put = ([sem(f"order_{n}{run}") for run in range(2)] for n in ("got", "put"))
        order_moved = {name: sem(f"order_moved_{name}") for name in ordered}
        edges_in, x_in, weights_in = sem("edges_in"), sem("x_in"), sem("weights_in")
        conv2_weights_in = sem("conv2_weights_in")
        iota_done, consts_ready, zero_ready = sem("iota_done"), sem("consts_ready"), sem("zero_ready")
        accs_cleared, spread_cleared = sem("accs_cleared"), [sem(f"spread_cleared{h}") for h in range(2)]
        prepared = sem("prepared")
        dve_step = sem("dve_step")
        to_act, from_act = sem("to_act"), sem("from_act")
        table_ready, table_stored = sem("table_ready"), sem("table_stored")
        hist_in = [sem(f"hist_in{h}") for h in range(2)]
        hist_read = sem("hist_read")
        hot_ready, hot_used = sem("hot_ready"), sem("hot_used")
        types_stored = [sem(f"types_stored{h}") for h in range(2)]
        hist_done, hist_copied, hist_stored, count_in = sem("hist_done"), sem("hist_copied"), sem("hist_stored"), sem("count_in")
        totals_ready, offsets_ready = sem("totals_ready"), sem("offsets_ready")
        cont_ready, cont_turned = sem("cont_ready"), sem("cont_turned")
        last_ready, last_turned, carry_ready, carry_turned, carry_out = (
            sem(n) for n in ("last_ready", "last_turned", "carry_ready", "carry_turned", "carry_out"))
        carry_added, ends_in = sem("carry_added"), sem("ends_in")
        starts_out, first_in = sem("starts_out"), sem("first_in")
        msg_in = [sem(f"msg_in{h}") for h in range(2)]
        msg_read, msg_scanned = sem("msg_read"), sem("msg_scanned")
        key_ready, key_spread, eq_done, msg_ready, key_used = (
            sem(n) for n in ("key_ready", "key_spread", "eq_done", "msg_ready", "key_used"))
        merged, rows_ready, scat_idx_ready = sem("merged"), sem("rows_ready"), sem("scat_idx_ready")
        scattered = [sem(f"scattered{i}") for i in range(2)]
        acc_loaded, acc_used = [sem(f"acc_loaded{i}") for i in range(4)], sem("acc_used")
        lin_in, lin_turned, lin_copied, lin_mult, lin_out = (
            sem(n) for n in ("lin_in", "lin_turned", "lin_copied", "lin_mult", "lin_out"))
        rel_stored = [sem(f"rel_stored{i}") for i in range(2)]
        attr_in = [sem(f"attr_in{h}") for h in range(2)]
        attr_turned, attr_copied, hid_done, hid_relu, w_ready, w_used, m_reduced = (
            sem(n) for n in ("attr_turned", "attr_copied", "hid_done", "hid_relu", "w_ready", "w_used", "m_reduced"))
        table_in = sem("table_in")
        typed_ready, typed_turned, typed_copied, typed_used, typed_out = (
            sem(f"typed_{n}") for n in ("ready", "turned", "copied", "used", "out"))
        dense_cols, dense_keys, dense_hot, dense_sum, dense_read, dense_done = (
            sem(f"dense_{n}") for n in ("cols", "keys", "hot", "sum", "read", "done"))
        out_ready, out_stored = sem("out_ready"), sem("out_stored")

        LIN = ["rel", "root", "rel", "root", "b2", "ih", "hh", "b2", "ih", "hh"]
        LIN_OF = {"conv1": 0, "conv2": 2, "edge1": 4, "gru1": 5, "edge2": 7, "gru2": 8}

        N_WEIGHTS = 16 * (2 * G + 1 + 3 + 3 * G + 3 * Q + 3)
        fw2_ready, first_placed = sem("fw2_ready"), sem("first_placed")

        DENSE, at_chunk, at_pair = {}, 0, 0
        for name, n in BY_PRODUCT.items():
            DENSE[name] = (at_chunk, at_pair, 4 * at_pair)
            at_chunk += CHUNKS
            at_pair += CHUNKS * n // 2

        def hold(eng, name, s, value):
            eng.wait_ge(s, value)
            eng.sem_inc(held[name], 1)

        block = ctx.enter_context(nc.Block())

        @block.sync
        def _(sp):
            def by_part(a):
                return a.rearrange("(p c) -> p c", p=P)

            def load_dst(a, s):
                sp.dma_start(dst_all, by_part(a)).then_inc(s, 16)
                sp.dma_start(EDGES[1:P, 0:1], by_part(a)[0:P - 1, 0:1]).then_inc(s, 16)
                sp.dma_start(EDGES[1:P, 1:2], by_part(a)[0:P - 1, T - 1:T]).then_inc(s, 16)

            sp.wait_ge(iota_done, 1)
            load_dst(dst, dst_in)
            sp.dma_start(X[:, :], x.rearrange("(p j) f -> p (j f)", p=P)).then_inc(x_in, 16)
            sp.wait_ge(zero_ready, 1)

            def put(o, i, s=weights_in):
                sp.dma_start(o, i).then_inc(s, 16)

            def conv_weights(W, root, bias, B, s):
                for j in range(G):
                    rows = slice(j * F, (j + 1) * F)
                    put(BD["rel"][rows, j * R * F:(j + 1) * R * F].rearrange("i (r o) -> i r o", r=R),
                        W.rearrange("r i o -> i r o"), s)
                    put(BD["root"][rows, j * F:(j + 1) * F], root, s)
                if bias is not None:
                    put(B[:, :], bias.unsqueeze(0).to_broadcast([P, F]), s)

            conv_weights(W1, root1, b1, B1, weights_in)
            put(B2[:, :], b2.unsqueeze(0).to_broadcast([P, F]))
            put(BIH[:, :], b_ih.unsqueeze(0).to_broadcast([P, 3 * F]))
            put(BHH[:, :], b_hh.unsqueeze(0).to_broadcast([P, 3 * F]))
            for j in range(G):
                rows = slice(j * F, (j + 1) * F)
                put(BD["b2"][rows, j * F:(j + 1) * F], fb2.rearrange("(i o) -> i o", i=F))
                put(BD["ih"][rows, j * 3 * F:(j + 1) * 3 * F], w_ih.rearrange("o i -> i o"))
                put(BD["hh"][rows, j * 3 * F:(j + 1) * 3 * F], w_hh.rearrange("o i -> i o"))
            for q in range(Q):
                put(FW1[q * FD:(q + 1) * FD, q * HID:(q + 1) * HID], fw1)
                put(FB1[q * HID:(q + 1) * HID, :], fb1.unsqueeze(1))
                put(FW2IO[q * HID:(q + 1) * HID, :], fw2)

            put(OTHER[0:1, :], fb2.unsqueeze(0))
            for i, W in enumerate((W1, W2)):
                put(WREL[i][:, :], W.rearrange("r i o -> (r i) o"))

            def store_table(n, rows, tile):
                sp.wait_ge(table_ready, n)
                sp.dma_start(rows.rearrange("(p j) d -> p (j d)", p=P), tile).then_inc(table_stored, 16)

            def edge_cols(a, k, w=1):
                if len(a.shape) == 1:
                    return by_part(a)[:, bass.ds(k * C, C)]
                return a.rearrange("(p c) d -> p c d", p=P)[:, bass.ds(k * C, C), :].rearrange("p c d -> p (c d)")

            def load_edges(loads, k=None):
                def put_all(arrays):
                    for tile, name, s in loads:
                        a = arrays[name]
                        if k is None:
                            a = by_part(a) if len(a.shape) == 1 else by_part(a.rearrange("e d -> (e d)"))
                        else:
                            a = edge_cols(a, k)
                        sp.dma_start(tile, a).then_inc(s, 16)

                with sp.If(unsorted > 0):
                    put_all(ordered)
                with sp.Else():
                    put_all(given)

            def xi_pair(t, first):
                for h in range(2):
                    k = t * 2 + h
                    if not first:
                        hold(sp, "sp", hist_read, k - 1)
                    load_edges([(EDST[h][:, :], "dst", hist_in[h]), (ETYP[h][:, :], "type", hist_in[h])], k)
                    sp.dma_start(edge_cols(spread_rows[0:EP, :], k, 1), zeros).then_inc(spread_cleared[h], 16)
                for h in range(2):
                    k = t * 2 + h
                    hold(sp, "sp", scanned["xi"], k + 1)
                    sp.dma_start(edge_cols(type_rows, k, 1), OS[h][:, 0:C * R]).then_inc(types_stored[h], 16)
                    hold(sp, "sp", gathered["xi"][h], (t + 1) * gathers("xi"))
                    hold(sp, "sp", dense_done, k + 1)
                    sp.dma_start(edge_cols(xi_rows, k, 1), GB[h][:, 0:C * F]).then_inc(stored["xi"][h], 16)

            sp.wait_ge(unsorted_known, 1)
            unsorted = nc.sync.value_load(UNSORTED[0:1, 0:1], min_val=0, max_val=1)
            sp.wait_ge(zero_ready, 2)
            with sp.If(unsorted > 0):
                sp.dma_start(next_rows.rearrange("(p j) d -> p (j d)", p=P), zeros[:, 0:NJ + 1]).then_inc(order_next, 16)
                sp.wait_ge(order_next, 16)
                sp.sem_inc(order_turn, 1)
                for run in range(2):
                    names = list(given) if run else ["dst"]
                    with sp.Fori(0, T) as t:
                        hold(sp, "sp", order_turn, t + 1 + run * (T + 1))
                        for name in names:
                            a = given[name]
                            a = a.rearrange("(p c) d -> p c d", p=P) if len(a.shape) == 2 else a.rearrange("(p c d) -> p c d", p=P, d=1)
                            sp.dma_start(COLUMN[name][:, :], a[:, bass.ds(t, 1), :].rearrange("p c d -> p (c d)")).then_inc(order_in, 16)
                    if run == 0:
                        sp.wait_ge(order_turn, T + 1)
                        sp.dma_start(CNT[:, :], next_rows[0:NPAD, :].rearrange("(p j) d -> p (j d)", p=P)).then_inc(order_next, 16)
                        sp.wait_ge(order_starts, 1)
                        sp.dma_start(next_rows[0:NPAD, :].rearrange("(p j) d -> p (j d)", p=P), NA[:, :]).then_inc(order_next, 16)
                        sp.wait_ge(order_next, 48)
                        sp.sem_inc(order_turn, 1)
                sp.wait_ge(order_turn, 2 * T + 2)
                load_dst(ordered["dst"].rearrange("e d -> (e d)"), spoiled)
                sp.wait_ge(spoiled, 48)
            load_edges([(SRC[:, :], "src", edges_in), (typ_all, "type", edges_in)])
            store_table(1, h_rows, H[:, :])

            def load_blocks(n, rows=h_rows):
                sp.wait_ge(table_stored, 16 * n)
                sp.dma_start(AGG[:, :].rearrange("p (b f) -> p b f", f=F),
                             rows.rearrange("(b p) f -> p b f", p=P)[:, :, 0:F]).then_inc(table_in, 16)

            load_blocks(1)
            loop_pairs(sp, xi_pair)
            for h in range(2):
                sp.wait_ge(stored["xi"][h], 16 * PAIRS)
                sp.wait_ge(types_stored[h], 16 * PAIRS)
            sp.wait_ge(hist_copied, 1)
            sp.dma_start(count_row, HIDT[0:NJ, 0:P]).then_inc(hist_stored, 16)
            sp.wait_ge(hist_stored, 16)
            sp.dma_start(CNT[:, :], count_row.rearrange("a b -> (a b)").rearrange("(p j) -> p j", p=P)).then_inc(count_in, 16)
            for r in range(2 * SET):
                sp.dma_start(accs[r].rearrange("(p j) d -> p j d", p=P), over(zeros[:, 0:ACC], NJ + 1, ACC)).then_inc(accs_cleared, 16)
            store_table(2, node_rows, big[:, 0:NJ * NE])

            def msg_pair(t, first):
                for h in range(2):
                    k = t * 2 + h
                    if not first:
                        hold(sp, "sp", msg_read, k - 1)
                    sp.dma_start(GB[h][:, 0:C * NE], edge_cols(spread_rows[0:EP, :], k, 1)).then_inc(msg_in[h], 16)
                    sp.dma_start(IN[h][:, :], edge_cols(xi_rows, k, 1)).then_inc(msg_in[h], 16)
                    load_edges([(EWT[h][:, :], "weight", msg_in[h]), (ETYP[h][:, :], "type", msg_in[h])], k)

            sp.wait_ge(starts_out, 16 * NJ)
            loop_pairs(sp, msg_pair)
            for i in range(2):
                sp.wait_ge(scattered[i], 8 * C * CHUNKS)
            for r in range(2 * SET):
                if r >= 4:
                    sp.wait_ge(acc_used, r - 3)
                sp.dma_start(acc_in[r % 4], accs[r][0:NPAD, :].rearrange("(p j) d -> p (j d)", p=P)).then_inc(acc_loaded[r % 4], 16)

            def store_rel(call):
                for g in range(GROUPS):
                    sp.wait_ge(lin_out, call * GROUPS + g + 1)
                    sp.dma_start(rel_rows.rearrange("(p j r) d -> p j (r d)", p=P, r=R)[:, g * G:(g + 1) * G, :],
                                 stage[g % 2].rearrange("p (j k) -> p j k", j=G)).then_inc(rel_stored[g % 2], 16)

            def store_pass(name):
                def pair(t, first):
                    for h in range(2):
                        hold(sp, "sp", scanned[name], t * 2 + h + 1)
                        sp.dma_start(edge_cols(seg_rows, t * 2 + h, 1), OS[h][:, 0:C * F]).then_inc(stored[name][h], 16)
                return pair

            store_table(3, h_rows, H[:, :])
            load_blocks(3)
            store_rel(LIN_OF["conv1"])
            loop_pairs(sp, store_pass("conv1"))
            sp.wait_ge(lin_mult, 2 * GROUPS)
            conv_weights(W2, root2, None, None, conv2_weights_in)
            store_table(4, h_rows, H[:, :])
            load_blocks(4)
            store_rel(LIN_OF["conv2"])
            loop_pairs(sp, store_pass("conv2"))

            def edge_pass(name, n):
                def load(k, h, t):
                    load_edges([(IN[h][:, 0:C * FD], "attr", attr_in[h])], k)

                def pair(t, first):
                    for h in range(2):
                        hold(sp, "sp", attr_turned, (t * 2 + h + 1) * len(BATCHES) + n * CHUNKS * len(BATCHES))
                        load(t * 2 + h + 2, h, t)
                        hold(sp, "sp", scanned[name], t * 2 + h + 1)
                        sp.dma_start(edge_cols(seg_rows, t * 2 + h, 1), OS[h][:, 0:C * F]).then_inc(stored[name][h], 16)

                for h in range(2):
                    load(h, h, 0)
                loop_pairs(sp, pair, end=PAIRS - 1)
                for h in range(2):
                    sp.wait_ge(scanned[name], CHUNKS - 1 + h)
                    sp.dma_start(edge_cols(seg_rows, CHUNKS - 2 + h, 1), OS[h][:, 0:C * F]).then_inc(stored[name][h], 16)

            store_table(5, pair_rows, big[:, 0:NJ * 2 * F])
            load_blocks(5, pair_rows)
            edge_pass("edge1", 0)
            store_table(6, pair_rows, big[:, 0:NJ * 2 * F])
            load_blocks(6, pair_rows)
            edge_pass("edge2", 1)
            store_table(7, h_rows, H[:, :])
            load_blocks(7)
            loop_pairs(sp, store_pass("sum3"))
            sp.wait_ge(out_ready, 1)
            full = N // NJ
            sp.dma_start(out[0:full * NJ, :].rearrange("(p j) f -> p (j f)", p=full), X[0:full, :]).then_inc(out_stored, 16)
            sp.dma_start(out[full * NJ:N, :].rearrange("(a j) f -> a (j f)", a=1),
                         X[full:full + 1, 0:(N - full * NJ) * F]).then_inc(out_stored, 16)
            sp.wait_ge(out_stored, 32)

        @block.gpsimd
        def _(pool):
            nc.gpsimd.memset(EDGES[:, 0:1], -2).then_inc(held["pool"], 1)
            nc.gpsimd.memset(EDGES[:, 1:2], -1).then_inc(held["pool"], 1)
            nc.gpsimd.iota(ROWI[:, :], pattern=[[0, 1]], base=0, channel_multiplier=1).then_inc(held["pool"], 1)
            nc.gpsimd.iota(COLI[:, :], pattern=[[1, P]], base=0, channel_multiplier=0).then_inc(held["pool"], 1)
            pool.wait_ge(held["pool"], 4)
            pool.sem_inc(iota_done, 1)

            def gather(rows, w, slot, c, idx):
                return nc.gpsimd.indirect_dma_start(
                    out=slot[:, c * w:(c + 1) * w], out_offset=None, in_=rows[:, :],
                    in_offset=bass.IndirectOffsetOnAxis(ap=idx, axis=0))

            def scatter(rows, w, slot, c, idx, op=ALU.bypass):
                return nc.gpsimd.indirect_dma_start(
                    out=rows[:, :], out_offset=bass.IndirectOffsetOnAxis(ap=idx, axis=0),
                    in_=slot[:, c * w:(c + 1) * w], in_offset=None, compute_op=op)

            def gather_pass(name, rows, w, freed):
                def pair(t, first):
                    for h in range(2):
                        k = t * 2 + h
                        hold(pool, "pool", idx_ready[name], k + 1)
                        if not first:
                            if freed is None:
                                hold(pool, "pool", stored[name][h], t * 16)
                            else:
                                hold(pool, "pool", freed[0], k - 1)
                        for c in range(gathers(name) // 16):
                            gather(rows, w, GB[h], c, IDX[h][:, c:c + 1]).then_inc(gathered[name][h], 16)
                return pair

            carries = [0]

            def finish_segments(name, rows, w, dest):
                carries[0] += 1
                n = carries[0]
                pool.wait_ge(carry_out, n)
                for h in range(2):
                    pool.wait_ge(types_stored[h] if name == "types" else stored[name][h], 16 * PAIRS)
                scatter(rows, w, CARRY, 0, FIRSTROW[:, 0:1], ALU.add).then_inc(carry_added, 16)
                pool.wait_ge(carry_added, 16 * n)
                for j in range(NJ):
                    gather(rows, w, dest, j, END[:, j:j + 1]).then_inc(ends_in, 16)

            pool.wait_ge(unsorted_known, 1)
            unsorted = nc.gpsimd.value_load(UNSORTED[0:1, 0:1], min_val=0, max_val=1)
            with pool.If(unsorted > 0):
                for run in range(2):
                    with pool.Fori(0, T) as t:
                        hold(pool, "pool", order_keys, t + 1 + run * T)
                        gather(next_rows, 1, NEXT, 0, COLUMN["dst"][:, 0:1]).then_inc(order_got[run], 16)
                        hold(pool, "pool", order_placed, t + 1 + run * T)
                        scatter(next_rows, 1, NEWNEXT, 0, NEXTROW[:, 0:1]).then_inc(order_put[run], 16)
                        if run:
                            for name, a in ordered.items():
                                scatter(a, a.shape[1], COLUMN[name], 0, PLACE[:, 0:1]).then_inc(order_moved[name], 16)
                            for name in ordered:
                                hold(pool, "pool", order_moved[name], t * 16 + 16)
                        hold(pool, "pool", order_put[run], t * 16 + 16)
                        pool.sem_inc(order_turn, 1)

            pool.wait_ge(table_stored, 16)
            loop_pairs(pool, gather_pass("xi", h_rows, F, None))
            finish_segments("types", type_rows, R, type_cnt)
            for h in range(2):
                pool.wait_ge(spread_cleared[h], 16 * PAIRS)
            pool.wait_ge(table_stored, 32)
            gather(node_rows, NE, FIRST, 0, DST0[:, 0:1]).then_inc(first_in, 16)
            for j in range(NJ):
                scatter(spread_rows, NE, big, j, START[:, j:j + 1]).then_inc(starts_out, 16)

            def scatter_pair(t, first):
                for h in range(2):
                    hold(pool, "pool", rows_ready, t * 2 + h + 1)
                    hold(pool, "pool", scat_idx_ready, t * 2 + h + 1)
                    for g in range(SETS):
                        before = (h * SETS + g) // 2
                        if not (first and before == 0):
                            hold(pool, "pool", scattered[g % 2], t * 16 * C + before * 16 * SET)
                        for q in range(SET):
                            c = g * SET + q
                            scatter(accs[(g % 2) * SET + q], ACC, ROWS[h], c, IDX[h][:, c:c + 1], ALU.add)\
                                .then_inc(scattered[g % 2], 16)

            pool.wait_ge(accs_cleared, 16 * 2 * SET)
            loop_pairs(pool, scatter_pair)

            for name in ("conv1", "conv2"):
                for i in range(2):
                    pool.wait_ge(rel_stored[i], 16 * GROUPS // 2 * (1 if name == "conv1" else 2))
                loop_pairs(pool, gather_pass(name, rel_rows, F, [scanned[name]]))
                finish_segments(name, seg_rows, F, AGG)
            for n, name in ((5, "edge1"), (6, "edge2")):
                pool.wait_ge(table_stored, 16 * n)
                loop_pairs(pool, gather_pass(name, pair_rows, 2 * F, [scanned[name]]))
                finish_segments(name, seg_rows, F, AGG)
            pool.wait_ge(table_stored, 16 * 7)
            loop_pairs(pool, gather_pass("sum3", h_rows, F, [scanned["sum3"]]))
            finish_segments("sum3", seg_rows, F, AGG)

        @block.scalar
        def _(act):
            asked = [0]
            lins = [0]

            def function(o, i, f, **kw):
                asked[0] += 1
                act.wait_ge(to_act, asked[0])
                nc.scalar.activation(o, i, f, **kw).then_inc(from_act, 1)

            def index_pass(name, table):
                def pair(t, first):
                    for h in range(2):
                        if not first:
                            hold(act, "act", gathered[name][h], t * gathers(name))
                        nc.scalar.copy(IDX[h][:, :], table[:, bass.ds((t * 2 + h) * C, C)]).then_inc(idx_ready[name], 1)
                return pair

            def linear(dest, staged=None):
                w = {"rel": R * F, "root": F, "b2": F, "ih": 3 * F, "hh": 3 * F}[LIN[lins[0]]]
                def turned(g):
                    act.wait_ge(lin_turned, lins[0] * GROUPS + g + 1)
                    nc.scalar.copy(HT[g % 2][:, :], turn_banks[g % 2][0:G * F, 0:P]).then_inc(lin_copied, 1)

                turned(0)
                for g in range(GROUPS):
                    if g + 1 < GROUPS:
                        turned(g + 1)
                    act.wait_ge(lin_mult, lins[0] * GROUPS + g + 1)
                    if staged is not None and staged * GROUPS // 2 + g // 2 > 0:
                        act.wait_ge(rel_stored[g % 2], 16 * (staged * GROUPS // 2 + g // 2))
                    parts = 2 if G * w > 512 else 1
                    for i in range(parts):
                        o, pw = dest(g), G * w // parts
                        s = lin_banks[g % 2][:, i * 512:i * 512 + pw]
                        if parts == 2:
                            o = o[:, i * pw:(i + 1) * pw]
                        elif len(o.shape) == 3:
                            s = s.rearrange("p (j k) -> p j k", j=G)
                        last = nc.scalar.copy(o, s)
                    last.then_inc(lin_out, 1)
                lins[0] += 1

            function(NB[:, :], NA[:, :], ACT.Sqrt)
            act.wait_ge(edges_in, 32)
            loop_pairs(act, index_pass("xi", SRC))

            def merge_pair(t, first):
                for h in range(2):
                    k = t * 2 + h
                    if not first:
                        for i in range(2):
                            hold(act, "act", scattered[i], t * 16 * C - (1 - h) * 8 * C)
                    for b in range(2):
                        hold(act, "act", merged, k * 2 + b + 1)
                        last = nc.scalar.copy(ROWS[h][:, b * HALF * ACC:(b + 1) * HALF * ACC],
                                              psM[:, b * 512:b * 512 + HALF * ACC])
                        if b == 0:
                            last.then_inc(held["act"], 1)
                    last.then_inc(rows_ready, 1)

            loop_pairs(act, merge_pair)
            function(NB[:, :], NA[:, :], ACT.Sqrt)
            def conv_pass(name, n):
                def typed(t, h, free):
                    at = (n * CHUNKS + h) * TURNS + t * 2 * TURNS
                    for b in range(TURNS):
                        hold(act, "act", typed_turned, at + b + 1)
                        if not (free and b < 2):
                            hold(act, "act", typed_used, at + max(0, b - 1))
                        nc.scalar.copy(by_type_t[b % 2], psM[:, b % 2 * 512:b % 2 * 512 + Q * P]).then_inc(typed_copied, 1)
                    hold(act, "act", typed_used, at + TURNS)
                    w = TURNS * Q * F
                    nc.scalar.copy(GB[h][:, C * F - w:C * F], psH[:, 0:w]).then_inc(typed_out, 1)

                def pair(t, first):
                    for h in range(2):
                        if not first:
                            hold(act, "act", gathered[name][h], t * gathers(name))
                        nc.scalar.copy(IDX[h][:, :], RIDX[:, bass.ds((t * 2 + h) * C, C)]).then_inc(idx_ready[name], 1)
                        if h == 1:
                            typed(t, 0, first and n == 0)
                        elif not first:
                            typed(t - 1, 1, False)

                loop_pairs(act, pair)
                typed(PAIRS - 1, 1, False)

            for n, name in enumerate(("conv1", "conv2")):
                linear(lambda g: stage[g % 2], n)
                linear(lambda g: ROOT[:, g * G * F:(g + 1) * G * F])
                conv_pass(name, n)
            function(TA[:, :], TB[:, :], ACT.Exp)
            function(NB[:, :], NA[:, :], ACT.Ln)
            function(NB[:, :], NA[:, :], ACT.Sqrt)

            def edge_pass(name, n):
                def index(k, h):
                    return nc.scalar.copy(IDX[h][:, :], SRC[:, bass.ds(k * C, C)]).then_inc(idx_ready[name], 1)

                def chunk(t, h):
                    for b, tiles in enumerate(BATCHES):
                        at = ((n * CHUNKS + h) * len(BATCHES) + b + 1) + t * 2 * len(BATCHES)
                        w = len(tiles) * P
                        hold(act, "act", attr_turned, at)
                        nc.scalar.copy(AT[:, 0:w], psT[0:Q * FD, 0:w]).then_inc(attr_copied, 1)
                        hold(act, "act", hid_done, at)
                        nc.scalar.activation(HIDT_OF[b % 2][:, 0:w], psH[:, 0:w], ACT.Relu, bias=FB1[:, 0:1]).then_inc(hid_relu, 1)

                def pair(t, first):
                    for h in range(2):
                        chunk(t, h)
                        hold(act, "act", gathered[name][h], (t + 1) * gathers(name))
                        index(t * 2 + h + 2, h)

                for h in range(2):
                    index(h, h)
                loop_pairs(act, pair, end=PAIRS - 1)
                for h in range(2):
                    chunk(PAIRS - 1, h)

            for n, name in enumerate(("edge1", "edge2")):
                linear(lambda g: pair_tab[:, g * G:(g + 1) * G, F:2 * F])
                edge_pass(name, n)
                linear(lambda g: GI[:, g * G:(g + 1) * G, :])
                linear(lambda g: GH[:, g * G:(g + 1) * G, :])
                function(GI[:, :, 0:2 * F], GI[:, :, 0:2 * F], ACT.Sigmoid)
                function(TA[:, :], TB[:, :], ACT.Tanh)
            function(NB[:, :], NA[:, :], ACT.Sqrt)
            function(NB[:, :], NA[:, :], ACT.Sqrt)
            loop_pairs(act, index_pass("sum3", SRC))
            function(NB[:, :], NA[:, :], ACT.Sqrt)

        @block.tensor
        def _(pe):
            lins = [0]
            ends = [0]
            lin_asked = [0]

            pe.wait_ge(consts_ready, 1)
            nc.tensor.matmul(psH[0:NJ, 0:P], LOWER[:, 0:NJ], NONE_HOT[:, :], start=True, stop=False)

            def spread_keys(slot, c0):
                for i in range(2):
                    c = slot * 16 + c0 + i
                    for part in range(2):
                        mm = nc.tensor.matmul(psT[:, (part * 2 + i) * P:(part * 2 + i + 1) * P],
                                              DK[part][:, c:c + 1].to_broadcast([P, P]), IDENTB[:, :], start=True, stop=True)
                mm.then_inc(dense_keys, 1)

            def half_table(banks, slot, i, half):
                for b in range(2):
                    o = banks[:, b * 512:b * 512 + QB * F]
                    at = slice((2 * half + b) * QB * F, (2 * half + b + 1) * QB * F)
                    for part in range(3):
                        nc.tensor.matmul(o, HOTLO[slot][:, i * P:(i + 1) * P], PART[part][:, at],
                                         start=(part == 0), stop=False)
                    mm = nc.tensor.matmul(o, OFFHI[slot][0:NJ, i * P:(i + 1) * P], PUSH[0:NJ, at],
                                          start=False, stop=True)
                mm.then_inc(dense_sum, 1)

            def dense(name, t, h, start, last, between=None):
                chunk0, pair0, half0 = DENSE[name]
                pairs = BY_PRODUCT[name] // 2
                done = t * 2 * pairs + h * pairs

                def keys(j):
                    slot, c0 = (h + j // pairs) % 2, 2 * (j % pairs)
                    if j % pairs == 0:
                        hold(pe, "pe", dense_cols, t * 2 + h + j // pairs + 1 + chunk0)
                    if not (start and chunk0 == 0 and j == 0):
                        hold(pe, "pe", dense_hot, done + pair0 + j)
                    spread_keys(slot, c0)

                def products(j):
                    slot = (h * pairs + j) % 2
                    hold(pe, "pe", dense_hot, done + pair0 + j + 1)
                    for i in range(2):
                        for half in range(2):
                            n = 4 * j + 2 * i + half
                            if not (start and chunk0 == 0 and n < 2):
                                hold(pe, "pe", dense_read, done * 4 + half0 + n - 1)
                            half_table(psW[half], slot, i, half)

                if start:
                    keys(0)
                for j in range(pairs):
                    if j + 1 < pairs or not last:
                        keys(j + 1)
                    products(j)
                    if between:
                        between(j)

            def hist_pair(t, first, last=False):
                for h in range(2):
                    def between(j):
                        if j not in HIST_PAIRS:
                            return
                        b = HIST_PAIRS.index(j)
                        hold(pe, "pe", hot_ready, t * 4 + (h * 2 + b + 1))
                        for c in range(HALF):
                            mm = nc.tensor.matmul(psH[0:NJ, 0:P], hot_hi[b][:, c, :], hot_lo[b][:, c, :],
                                                  start=False, stop=False, skip_group_check=True)
                        mm.then_inc(hot_used, 1)

                    dense("xi", t, h, first and h == 0, last and h == 1, between)

            def sum3_products(t, first, last=False):
                for h in range(2):
                    dense("sum3", t, h, first and h == 0, last and h == 1)

            pe.wait_ge(unsorted_sum, 1)
            nc.tensor.matmul(psT[0:1, 0:1], SMALL[:, 6:7], ONE[:, :], start=True, stop=True).then_inc(unsorted_sum, 1)
            pe.wait_ge(unsorted_known, 1)
            unsorted = nc.tensor.value_load(UNSORTED[0:1, 0:1], min_val=0, max_val=1)
            with pe.If(unsorted > 0):
                for run in range(2):
                    with pe.Fori(0, T) as t:
                        hold(pe, "pe", order_keys, t + 1 + run * T)
                        nc.tensor.matmul(psT[:, 0:P], COLKEY[:, 0:1].to_broadcast([P, P]), IDENT[:, :],
                                         start=True, stop=True).then_inc(order_spread, 1)
                    if run == 0:
                        pe.wait_ge(order_totals, 1)
                        nc.tensor.matmul(psT[:, 0:1], UPPER[:, :], SMALL[:, 0:1], start=True, stop=True).then_inc(order_offsets, 1)

            pe.wait_ge(cont_ready, 1)
            nc.tensor.matmul(psT[0:F, 0:P], CO16[:, :], IDENT[:, :], start=True, stop=True)
            nc.tensor.matmul(psT[0:F, P:2 * P], A16[:, :], IDENT[:, :], start=True, stop=True).then_inc(cont_turned, 1)
            loop_pairs(pe, hist_pair, end=PAIRS - 1)
            hist_pair(PAIRS - 1, False, last=True)
            nc.tensor.matmul(psH[0:NJ, 0:P], LOWER[:, 0:NJ], NONE_HOT[:, :], start=False, stop=True)\
                .then_inc(hist_done, 1)
            pe.wait_ge(totals_ready, 1)
            nc.tensor.matmul(psH[:, 0:1], UPPER[:, :], SMALL[:, 0:1], start=True, stop=True).then_inc(offsets_ready, 1)

            def finish_segments(w):
                ends[0] += 1
                pe.wait_ge(last_ready, ends[0])
                nc.tensor.transpose(psT[0:w, 0:P], LAST[:, 0:w], IDENT[:, :]).then_inc(last_turned, 1)
                pe.wait_ge(carry_ready, ends[0])
                nc.tensor.transpose(psT[:, P:P + w], CARRY_T[0:w, :], IDENT[0:w, 0:w]).then_inc(carry_turned, 1)

            finish_segments(R)

            def merge_pair(t, first):
                for h in range(2):
                    k = t * 2 + h
                    done = t * (2 * TILES) + h * TILES

                    def merge(g):
                        for c in range(g * Q, (g + 1) * Q):
                            at = c // HALF * 512 + c % HALF * ACC
                            mm = nc.tensor.matmul(psM[:, at:at + ACC], meq[:, c, :], msg[h][:, c, :], start=True, stop=True)
                            if c % HALF == HALF - 1:
                                mm.then_inc(merged, 1)

                    hold(pe, "pe", key_ready, k + 1)
                    for g in range(TILES):
                        if not (first and h == 0 and g < 2):
                            hold(pe, "pe", eq_done, done + g - 1)
                        for q in range(Q):
                            mm = nc.tensor.matmul(psW[(h * TILES + g) % 2][:, q * P:(q + 1) * P],
                                                  KEY[:, g * Q + q:g * Q + q + 1].to_broadcast([P, P]), IDENT[:, :],
                                                  start=True, stop=True)
                        mm.then_inc(key_spread, 1)
                        if g == 2:
                            hold(pe, "pe", msg_ready, k + 1)
                            if not (first and h == 0):
                                hold(pe, "pe", rows_ready, k)
                        if g >= 2 and g % 2 == 0:
                            merge(g // 2 - 1)
                    hold(pe, "pe", eq_done, done + TILES)
                    for g in range(TILES // 2, TILES):
                        merge(g)

            loop_pairs(pe, merge_pair)

            def linear(source):
                name = LIN[lins[0]]
                w = G * {"rel": R * F, "root": F, "b2": F, "ih": 3 * F, "hh": 3 * F}[name]
                before = lins[0] * GROUPS

                def turn(g):
                    if g >= 2:
                        pe.wait_ge(lin_copied, before + g - 1)
                    nc.tensor.transpose(turn_banks[g % 2][0:G * F, 0:P], source[:, g * G * F:(g + 1) * G * F],
                                        IDENT[:, :]).then_inc(lin_turned, 1)

                if before:
                    pe.wait_ge(lin_out, before)
                turn(0)
                for g in range(GROUPS):
                    if g + 1 < GROUPS:
                        turn(g + 1)
                    pe.wait_ge(lin_copied, before + g + 1)
                    if g >= 2:
                        pe.wait_ge(lin_out, before + g - 1)
                    parts = 2 if w > 512 else 1
                    pw = w // parts
                    for i in range(parts):
                        mm = nc.tensor.matmul(lin_banks[g % 2][:, i * 512:i * 512 + pw], HT[g % 2][:, :], BD[name][:, i * pw:(i + 1) * pw],
                                              start=True, stop=True)
                    mm.then_inc(lin_mult, 1)
                lins[0] += 1

            def wait_nodes():
                lin_asked[0] += 1
                pe.wait_ge(lin_in, lin_asked[0])

            pe.wait_ge(weights_in, N_WEIGHTS)
            pe.wait_ge(fw2_ready, 1)
            def conv_pass(name, n):
                def typed(t, h, j, free):
                    at = (n * CHUNKS + h) * TURNS + t * 2 * TURNS
                    if j < TURNS:
                        hold(pe, "pe", typed_ready, at + j + 1)
                        if not (free and j < 2):
                            hold(pe, "pe", typed_copied, at + max(0, j - 1))
                        for i in range(Q):
                            mm = nc.tensor.transpose(psM[:, j % 2 * 512 + i * P:j % 2 * 512 + (i + 1) * P],
                                                     by_type[j % 2][:, i * P:(i + 1) * P], IDENT[:, :])
                        mm.then_inc(typed_turned, 1)
                    if 0 < j <= TURNS:
                        b = j - 1
                        hold(pe, "pe", typed_copied, at + b + 1)
                        if b == 0 and not free:
                            hold(pe, "pe", typed_out, n * CHUNKS + t * 2 + h)
                        for i in range(Q):
                            mm = nc.tensor.matmul(psH[:, (b * Q + i) * F:(b * Q + i + 1) * F],
                                                  by_type_t[b % 2][:, i * P:(i + 1) * P], WREL[n][:, :], start=True, stop=True)
                        mm.then_inc(typed_used, 1)

                def pair(t, first, last=False):
                    dense(name, t, 0, first, False, None if first else lambda j: typed(t - 1, 1, j, False))
                    dense(name, t, 1, False, last, lambda j: typed(t, 0, j, first and n == 0))

                loop_pairs(pe, pair, end=PAIRS - 1)
                pair(PAIRS - 1, False, last=True)
                for j in range(TURNS + 1):
                    typed(PAIRS - 1, 1, j, False)

            for n, name in enumerate(("conv1", "conv2")):
                wait_nodes()
                if name == "conv2":
                    pe.wait_ge(conv2_weights_in, 16 * 2 * G)
                linear(H)
                linear(H)
                pe.wait_ge(lin_out, lins[0] * GROUPS)
                conv_pass(name, n)
                finish_segments(F)

            def edge_pass(name, n):
                chunk0, pair0, half0 = DENSE[name]

                def turn(t, h, b, start=False):
                    at = (n * CHUNKS + h) * len(BATCHES) + b + t * 2 * len(BATCHES)
                    if b == 0:
                        hold(pe, "pe", attr_in[h], t * 16 + (n * PAIRS + 1) * 16)
                    if not (start and n == 0):
                        hold(pe, "pe", attr_copied, at)
                    if b in (1, 2):
                        hold(pe, "pe", dense_hot, t * Q + h * 2 + pair0 + b)
                    for i, g in enumerate(BATCHES[b]):
                        mm = nc.tensor.transpose(psT[0:Q * FD, i * P:(i + 1) * P],
                                                 IN[h][:, g * Q * FD:(g + 1) * Q * FD], IDENT[:, :])
                    mm.then_inc(attr_turned, 1)

                def hidden(t, h, b, start=False):
                    at = (n * CHUNKS + h) * len(BATCHES) + b + t * 2 * len(BATCHES)
                    hold(pe, "pe", attr_copied, at + 1)
                    if not (start and n == 0):
                        hold(pe, "pe", hid_relu, at)
                    w = len(BATCHES[b]) * P
                    nc.tensor.matmul(psH[:, 0:w], FW1[:, :], AT[:, 0:w], start=True, stop=True).then_inc(hid_done, 1)

                def weights(t, h, g, start):
                    at_tile = (n * CHUNKS + h) * TILES + g + t * 2 * TILES
                    b, i = g // 4, g % 4
                    if i == 0:
                        hold(pe, "pe", hid_relu, (n * CHUNKS + h) * len(BATCHES) + b + 1 + t * 2 * len(BATCHES))
                    slot = (h * TILES + g) % 2
                    if not (start and n == 0 and g < 2):
                        hold(pe, "pe", w_used, at_tile - 1)
                    for bank in range(2):
                        o = psW[slot][:, bank * 512:(bank + 1) * 512]
                        mm = nc.tensor.matmul(o, HIDT_OF[b % 2][:, i * P:(i + 1) * P], FW2[:, bank * 512:(bank + 1) * 512],
                                              start=True, stop=(g < TILES - 1))
                        if g == TILES - 1:
                            mm = nc.tensor.matmul(o.rearrange("p (c k) -> p c k", c=2), ONES[:, :],
                                                  FB2[:, :].unsqueeze(1).to_broadcast([1, 2, F * F]),
                                                  start=False, stop=True)
                    mm.then_inc(w_ready, 1)

                def pair(t, first, last=False):
                    for h in range(2):
                        pairs, halves = t * Q + h * 2 + pair0, t * 4 * Q + h * 2 * Q + half0
                        after = (t, 1, 0) if h == 0 else (t + 1, 0, 0)
                        for g in range(TILES):
                            weights(t, h, g, first and h == 0)
                            if g == 0:
                                hold(pe, "pe", dense_cols, t * 2 + h + 1 + chunk0)
                                hold(pe, "pe", dense_hot, pairs)
                                spread_keys(h, 0)
                            elif g == 3:
                                spread_keys(h, 2)
                            if g in (1, 5, 9):
                                turn(t, h, g // 4 + 1)
                            elif g in (2, 6, 10):
                                hidden(t, h, g // 4 + 1)
                            elif g == 11 and not (last and h == 1):
                                turn(*after)
                            elif g == 12 and not (last and h == 1):
                                hidden(*after)
                            if 3 <= g < 3 + 2 * Q:
                                m = g - 3
                                if m % 4 == 0:
                                    hold(pe, "pe", dense_hot, pairs + m // 4 + 1)
                                hold(pe, "pe", dense_read, halves + m)
                                half_table(psM, m // 4, m // 2 % 2, m % 2)

                assert [len(b) for b in BATCHES] == [4, 4, 4, 1]
                turn(0, 0, 0, True)
                hidden(0, 0, 0, True)
                loop_pairs(pe, pair, end=PAIRS - 1)
                pair(PAIRS - 1, False, last=True)

            for n, name in enumerate(("edge1", "edge2")):
                wait_nodes()
                linear(H)
                pe.wait_ge(lin_out, lins[0] * GROUPS)
                edge_pass(name, n)
                finish_segments(F)
                wait_nodes()
                linear(AGG)
                linear(H)
            loop_pairs(pe, sum3_products, end=PAIRS - 1)
            sum3_products(PAIRS - 1, False, last=True)
            finish_segments(F)

        @block.vector
        def _(dve):
            v = nc.vector
            st = Steps(dve, dve_step)
            asked, tables, ends, lin_asked, lin_done = [0], [0], [0], [0], [0]

            def ask():
                dve.wait_ge(dve_step, st.n)
                dve.sem_inc(to_act, 1)
                asked[0] += 1
                dve.wait_ge(from_act, asked[0])

            def signal(s):
                dve.wait_ge(dve_step, st.n)
                dve.sem_inc(s, 1)

            def linear_done(calls):
                lin_done[0] += calls
                dve.wait_ge(lin_out, lin_done[0] * GROUPS)

            X3, H3, TA3, TB3, AGG3 = (node3(t) for t in (X, H, TA, TB, AGG))

            def layer_norm():
                st.do(v.tensor_reduce(NA[:, :], X3, AX.X, ALU.add))
                st.do(v.tensor_scalar(NA[:, :], NA[:, :], 1.0 / F, None, ALU.mult))
                st.do(v.tensor_tensor(TA3, X3, spread(NA[:, :], NJ, F), ALU.subtract))
                st.do(v.tensor_tensor(TB[:, :], TA[:, :], TA[:, :], ALU.mult))
                st.do(v.tensor_reduce(NA[:, :], TB3, AX.X, ALU.add))
                st.do(v.tensor_scalar(NA[:, :], NA[:, :], 1.0 / F, EPS, ALU.mult, ALU.add))
                ask()
                st.do(v.reciprocal(NA[:, :], NB[:, :]))
                st.do(v.tensor_tensor(TA3, TA3, spread(NA[:, :], NJ, F), ALU.mult))
                st.do(v.tensor_scalar(H[:, :], TA[:, :], 0.0, None, ALU.max))

            dve.wait_ge(iota_done, 1)
            for w in BD.values():
                st.did(v.memset(w[:, :], 0.0))
            st.did(v.memset(FW1[:, :], 0.0))
            st.did(v.memset(FW2[:, :], 0.0))
            st.did(v.memset(NONE_HOT[:, :], 0.0))
            st.did(v.memset(ONE[:, :], 1.0))
            st.did(v.memset(ONES[:, :], 1.0))
            st.did(v.tensor_copy(ROWF[:, :], ROWI[:, :]))
            st.did(v.tensor_copy(COLF[:, :], COLI[:, :]))
            st.settle()
            signal(zero_ready)
            st.did(v.tensor_copy(COLB[:, :], COLF[:, :]))
            st.did(v.tensor_scalar(IDENT[:, :], COLF[:, :], ROWF[:, 0:1], None, ALU.is_equal))
            st.did(v.tensor_scalar(LOWER[:, :], COLF[:, :], ROWF[:, 0:1], None, ALU.is_lt))
            st.did(v.tensor_scalar(UPPER[:, :], COLF[:, :], ROWF[:, 0:1], None, ALU.is_gt))
            st.settle()
            signal(consts_ready)
            dve.wait_ge(dst_in, 16 * 3)
            st.did(v.tensor_tensor(NORM[:, 1:T], dst_all[:, 0:T - 1], dst_all[:, 1:T], ALU.is_gt))
            st.did(v.tensor_tensor(NORM[:, 0:1], EDGES[:, 1:2], dst_all[:, 0:1], ALU.is_gt))
            st.settle()
            st.do(v.tensor_reduce(SMALL[:, 6:7], NORM[:, :], AX.X, ALU.max))
            signal(unsorted_sum)
            dve.wait_ge(unsorted_sum, 2)
            st.do(v.tensor_scalar(UNSORTED[:, :], psT[0:1, 0:1], 1.0, None, ALU.min))
            signal(unsorted_known)
            dve.wait_ge(x_in, 16)
            layer_norm()
            signal(table_ready)
            st.do(v.tensor_scalar(TA[:, :], H[:, :], -1.0 / 5.0, 1.0, ALU.mult, ALU.add))
            st.do(v.tensor_tensor(TA[:, :], TA[:, :], H[:, :], ALU.mult))
            st.do(v.scalar_tensor_tensor(out=TA[:, :], in0=H[:, :], scalar=1.0, in1=TA[:, :], op0=ALU.subtract, op1=ALU.mult))
            st.do(v.scalar_tensor_tensor(out=X[:, :], in0=TA[:, :], scalar=0.1, in1=X[:, :], op0=ALU.add, op1=ALU.add))
            st.do(v.memset(TB[:, :], 0.0))
            signal(zero_ready)

            def starts(step, where, asked, answered):
                step.do(v.memset(FULL[:, :], 1.0))
                step.do(v.tensor_tensor_scan(NA[:, :], FULL[:, :], CNT[:, :], 0.0, ALU.mult, ALU.add))
                step.do(v.tensor_copy(SMALL[:, 0:1], NA[:, NJ - 1:NJ]))
                dve.sem_inc(asked, 1)
                dve.wait_ge(answered, 1)
                step.do(v.tensor_copy(SMALL[:, 5:6], where))
                step.do(v.tensor_scalar(NA[:, :], NA[:, :], SMALL[:, 5:6], None, ALU.add))

            dve.wait_ge(unsorted_known, 1)
            unsorted = nc.vector.value_load(UNSORTED[0:1, 0:1], min_val=0, max_val=1)
            with dve.If(unsorted > 0):
                od = Steps(dve, order_step)
                od.peeled = False
                for run in range(2):
                    n0 = od.n
                    od.per = 9
                    with dve.Fori(0, T) as t:
                        od.t = t
                        hold(dve, "dve", order_in, (t * 80 + 80 + 16 * T) if run else (t * 16 + 16))
                        v.tensor_copy(COLKEY[:, :], COLUMN["dst"][:, :]).then_inc(order_key, 1)
                        hold(dve, "dve", order_key, t + 1 + run * T)
                        dve.sem_inc(order_keys, 1)
                        hold(dve, "dve", order_spread, t + 1 + run * T)
                        od.do(v.tensor_scalar(col_eq, psT[:, 0:P], COLKEY[:, 0:1], None, ALU.is_equal))
                        od.did(v.tensor_tensor(col_low, col_eq, LOWER[:, :], ALU.mult))
                        od.did(v.tensor_reduce(SMALL[:, 9:10], col_eq, AX.X, ALU.add))
                        od.settle()
                        od.do(v.tensor_reduce(SMALL[:, 10:11], col_low, AX.X, ALU.add))
                        hold(dve, "dve", order_got[run], t * 16 + 16)
                        od.did(v.tensor_tensor(PLACE[:, :], NEXT[:, :], SMALL[:, 10:11], ALU.add))
                        od.did(v.tensor_tensor(NEWNEXT[:, :], NEXT[:, :], SMALL[:, 9:10], ALU.add))
                        od.did(v.tensor_scalar(SMALL[:, 11:12], SMALL[:, 10:11], 1.0, None, ALU.min))
                        od.did(v.scalar_tensor_tensor(out=SMALL[:, 12:13], in0=ROWF[:, :], scalar=float(NPAD), in1=COLKEY[:, :],
                                                      op0=ALU.add, op1=ALU.subtract))
                        od.settle()
                        od.do(v.tensor_tensor(SMALL[:, 12:13], SMALL[:, 12:13], SMALL[:, 11:12], ALU.mult))
                        v.tensor_tensor(NEXTROW[:, :], SMALL[:, 12:13], COLKEY[:, :], ALU.add).then_inc(order_placed, 1)
                    assert od.n - n0 == od.per
                    od.t = None
                    od.n += (T - 1) * od.per
                    if run == 0:
                        dve.wait_ge(order_next, 32)
                        starts(od, psT[:, 0:1], order_totals, order_offsets)
                        od.do(v.tensor_tensor(NA[:, :], NA[:, :], CNT[:, :], ALU.subtract))
                        dve.sem_inc(order_starts, 1)
                dve.wait_ge(spoiled, 48)

            dve.wait_ge(edges_in, 16 * 2)
            st.did(v.memset(SAME[:, 0:1], 0.0))
            st.did(v.tensor_tensor(SAME[:, 1:T], dst_all[:, 1:T], dst_all[:, 0:T - 1], ALU.is_equal))
            st.did(v.tensor_scalar(RIDX[:, :], SRC[:, :], float(R), None, ALU.mult))
            st.did(v.tensor_tensor(NORM[:, :], dst_all, dst_all[:, 0:1].to_broadcast([P, T]), ALU.is_equal))
            st.did(v.tensor_copy(DST0[:, :], dst_all[:, 0:1]))
            st.settle()
            st.did(v.tensor_tensor(RIDX[:, :], RIDX[:, :], typ_all, ALU.add))
            st.did(v.tensor_tensor(SMALL[:, 1:2], dst_all[:, 0:1], EDGES[:, 1:2], ALU.is_equal))
            st.did(v.tensor_tensor(SMALL[:, 2:3], EDGES[:, 0:1], EDGES[:, 1:2], ALU.is_equal))
            st.did(v.tensor_reduce(SMALL[:, 3:4], NORM[:, :], AX.X, ALU.add))
            st.settle()
            st.did(v.tensor_scalar(SMALL[:, 4:5], ROWF[:, :], float(T), -1.0, ALU.mult, ALU.add))
            st.did(v.tensor_tensor(SMALL[:, 2:3], SMALL[:, 1:2], SMALL[:, 2:3], ALU.mult))
            st.settle()
            st.did(v.tensor_tensor(FIRSTROW[:, :], SMALL[:, 3:4], SMALL[:, 4:5], ALU.add))
            st.did(v.tensor_copy(CO16[:, :], SMALL[:, 1:2].to_broadcast([P, F])))
            st.did(v.tensor_copy(A16[:, :], SMALL[:, 2:3].to_broadcast([P, F])))
            st.settle()
            signal(cont_ready)
            dve.wait_ge(cont_turned, 1)
            st.did(v.tensor_copy(CONT_T[:, :], psT[0:F, 0:P]))
            st.did(v.tensor_copy(A_T[:, :], psT[0:F, P:2 * P]))
            st.settle()

            dve.wait_ge(weights_in, N_WEIGHTS)
            for q in range(Q):
                rows = slice(q * HID, (q + 1) * HID)
                st.did(v.tensor_copy(FW2[rows, q * F * F:(q + 1) * F * F].rearrange("k (o i) -> k o i", o=F),
                                     FW2IO[rows, :].rearrange("k (i o) -> k o i", i=F)))
            st.did(v.tensor_copy(FB2[:, :].rearrange("k (o i) -> k o i", o=F), OTHER[0:1, :].rearrange("k (i o) -> k o i", i=F)))
            st.settle()
            signal(fw2_ready)

            def scans(h, src3, w, k, start, s, features=None):
                o = cols(OS[h], w)
                prev = cols(OS[1 - h], w)
                features = features or range(w)
                for f in features:
                    last = v.tensor_tensor_scan(o[:, :, f], SAME[:, bass.ds(k * C, C)], src3[:, :, f],
                                                0.0 if start else prev[:, C - 1, f:f + 1], ALU.mult, ALU.add)
                if w - 1 in features:
                    last.then_inc(s, 1)

            tables_in = [0]

            def split_table():
                tables_in[0] += 1
                dve.wait_ge(table_in, 16 * tables_in[0])
                w = NJ * F
                for part in range(3):
                    st.do(v.tensor_copy(PART[part][:, 0:w], AGG[:, :]))
                    if part < 2:
                        st.do(v.tensor_tensor(AGG[:, :], AGG[:, :], PART[part][:, 0:w], ALU.subtract))

            def dense_columns(name, t, h):
                n2 = BY_PRODUCT[name]
                src_cols = SRC[:, bass.ds(t * 2 * C + (h * C + C - n2), n2)]
                st.did(v.tensor_scalar(DI[0][:, 0:n2], src_cols, P - 1, None, ALU.bitwise_and))
                st.did(v.tensor_scalar(DI[1][:, 0:n2], src_cols, 7, None, ALU.logical_shift_right))
                st.settle()
                slot = h % 2 * 16
                st.did(v.tensor_copy(DK[0][:, slot:slot + n2], DI[0][:, 0:n2]))
                st.did(v.tensor_copy(DK[1][:, slot:slot + n2], DI[1][:, 0:n2]))
                st.settle()
                dve.sem_inc(dense_cols, 1)

            def hot(slot, keys):
                hold(dve, "dve", dense_keys, keys)
                v.tensor_scalar(HOTLO[slot][:, :], psT[:, 0:2 * P], ROWF[:, 0:1], None, ALU.is_equal)
                v.tensor_scalar(OFFHI[slot][:, :], psT[:, 2 * P:4 * P], ROWF[:, 0:1], None, ALU.not_equal)\
                    .then_inc(dense_hot, 1)

            def dense_start(name):
                dense_columns(name, 0, 0)
                hot(0, DENSE[name][1] + 1)

            def dense(name, t, h, start, last, between):
                chunk0, pair0, half0 = DENSE[name]
                n2 = BY_PRODUCT[name]
                pairs = n2 // 2
                done = t * 2 * pairs + h * pairs
                found = GB[h][:, (C - n2) * F:C * F]

                def read(j):
                    for i in range(2):
                        for half in range(2):
                            hold(dve, "dve", dense_sum, done * 4 + half0 + 4 * j + 2 * i + half + 1)
                            o = (found, OTHER)[half][:, (2 * j + i) * F:(2 * j + i + 1) * F]
                            v.tensor_reduce(o, psW[half][:, :].rearrange("p (b x) -> p b x", b=2)[:, :, 0:QB * F]
                                            .rearrange("p b (q f) -> p f b q", f=F), AX.XY, ALU.max).then_inc(dense_read, 1)
                            between(4 * j + 2 * i + half)

                if not start:
                    hold(dve, "dve", dense_done, t * 2 + h + chunk0)
                for j in range(pairs):
                    if j == pairs - 2 and not last:
                        dense_columns(name, t, h + 1)
                    if j + 1 < pairs or not last:
                        hot((h * pairs + j + 1) % 2, done + pair0 + j + 2)
                    read(j)
                hold(dve, "dve", dense_read, done * 4 + half0 + 4 * pairs)
                v.tensor_tensor(found, found, OTHER[:, 0:n2 * F], ALU.max).then_inc(dense_done, 1)

            st.did(v.tensor_copy(IDENTB[:, :], IDENT[:, :]))
            st.did(v.memset(PUSH[:, NJ * F:BLOCKS * F], -HUGE))
            st.did(v.tensor_scalar(PUSH[:, 0:NJ * F].rearrange("p (b f) -> p b f", f=F), spread(IDENT[:, 0:NJ], NJ, F), -HUGE, None, ALU.mult))
            for part in range(3):
                st.did(v.memset(PART[part][:, NJ * F:BLOCKS * F], 0.0))
            st.settle()
            split_table()

            def hist_pair(t, first, last=False):
                for h in range(2):
                    k = t * 2 + h

                    def hist_columns():
                        hold(dve, "dve", hist_in[h], (t + 1) * 32)
                        st.did(v.tensor_scalar(LOI[:, :], EDST[h][:, :], P - 1, None, ALU.bitwise_and))
                        st.did(v.tensor_scalar(HII[:, :], EDST[h][:, :], 7, None, ALU.logical_shift_right))
                        st.settle()
                        st.did(v.tensor_copy(LOB[:, :], LOI[:, :]))
                        st.did(v.tensor_copy(HIB[:, :], HII[:, :]))
                        st.did(v.tensor_tensor(cols(TH, R), over(COLF[:, 0:R], C, R), spread(ETYP[h][:, :], C, R), ALU.is_equal))
                        st.settle()
                        dve.sem_inc(hist_read, 1)

                    def hist_hot(b, part):
                        if part == 0 and not (first and h == 0):
                            hold(dve, "dve", hot_used, k * 2 + b - 1)
                        a, z = part * HALF // HIST_PARTS, (part + 1) * HALF // HIST_PARTS
                        sl = slice(b * HALF + a, b * HALF + z)
                        st.did(v.tensor_tensor(hot_lo[b][:, a:z, :], over(COLB[:, :], z - a, P), spread(LOB[:, sl], z - a, P), ALU.is_equal))
                        hi = v.tensor_tensor(hot_hi[b][:, a:z, :], over(COLB[:, 0:NJ], z - a, NJ),
                                             spread(HIB[:, sl], z - a, NJ), ALU.is_equal)
                        if part == HIST_PARTS - 1:
                            hi.then_inc(hot_ready, 1)

                    def type_scans(half):
                        if half == 0:
                            if not first:
                                hold(dve, "dve", types_stored[h], t * 16)
                            if not (first and h == 0):
                                hold(dve, "dve", scanned["xi"], k)
                        scans(h, cols(TH, R), R, k, first and h == 0, scanned["xi"],
                              range(half * R // 2, (half + 1) * R // 2))

                    steps = {0: hist_columns, 17: lambda: type_scans(0), 18: lambda: type_scans(1)}
                    for b in range(2):
                        for part in range(HIST_PARTS):
                            steps[2 + (b * HIST_PARTS + part) * 2] = lambda b=b, part=part: hist_hot(b, part)

                    def between(n):
                        if n in steps:
                            steps[n]()

                    if not first:
                        hold(dve, "dve", stored["xi"][h], t * 16)
                    dense("xi", t, h, first and h == 0, last and h == 1, between)

            dense_start("xi")
            loop_pairs(dve, hist_pair, st, end=PAIRS - 1)
            hist_pair(PAIRS - 1, False, last=True)
            dve.wait_ge(hist_done, 1)
            st.do(v.tensor_copy(HIDT[0:NJ, 0:P], psH[0:NJ, 0:P]))
            signal(hist_copied)

            def finish_segments(name, w, dest):
                ends[0] += 1
                n = ends[0]
                dve.wait_ge(scanned["xi" if name == "types" else name], CHUNKS)
                st.do(v.tensor_copy(LAST[:, 0:w], cols(OS[1], w)[:, C - 1, :]))
                signal(last_ready)
                dve.wait_ge(last_turned, n)
                st.did(v.memset(B_T[:, 0:1], 0.0))
                st.did(v.tensor_tensor(B_T[0:w, 1:P], psT[0:w, 0:P - 1], CONT_T[0:w, 1:P], ALU.mult))
                st.settle()
                st.do(v.tensor_tensor_scan(CARRY_T[0:w, :], A_T[0:w, :], B_T[0:w, :], 0.0, ALU.mult, ALU.add))
                signal(carry_ready)
                dve.wait_ge(carry_turned, n)
                st.do(v.tensor_copy(CARRY[:, 0:w], psT[:, P:P + w]))
                signal(carry_out)
                dve.wait_ge(ends_in, 16 * NJ * n)
                st.do(v.tensor_tensor(node3(dest, w), node3(dest, w), spread(FULL[:, :], NJ, w), ALU.mult))

            dve.wait_ge(count_in, 16)
            starts(st, psH[:, 0:1], totals_ready, offsets_ready)
            st.did(v.tensor_scalar(END[:, :], NA[:, :], -1.0, 0.0, ALU.add, ALU.max))
            st.did(v.tensor_tensor(NA[:, :], NA[:, :], CNT[:, :], ALU.subtract))
            st.did(v.tensor_scalar(FULL[:, :], CNT[:, :], 1.0, None, ALU.min))
            st.did(v.tensor_scalar(NB[:, :], ROWF[:, 0:1].to_broadcast([P, NJ]), float(NJ), float(EP), ALU.mult, ALU.add))
            st.settle()
            st.do(v.tensor_tensor(NB[:, :], NB[:, :], COLF[:, 0:NJ], ALU.add))
            st.do(v.tensor_tensor(NA[:, :], NA[:, :], NB[:, :], ALU.subtract))
            st.do(v.tensor_tensor(NA[:, :], NA[:, :], FULL[:, :], ALU.mult))
            st.do(v.tensor_tensor(START[:, :], NA[:, :], NB[:, :], ALU.add))
            finish_segments("types", R, type_cnt)
            st.do(v.tensor_scalar(type_cnt, type_cnt, 1.0, None, ALU.max))
            st.did(v.reciprocal(node_ext[:, :, F:NE], node3(type_cnt, R)))
            st.did(v.tensor_copy(node_ext[:, :, 0:F], H3))
            st.settle()
            signal(table_ready)
            dve.wait_ge(starts_out, 16 * NJ)
            dve.wait_ge(first_in, 16)
            st.did(v.tensor_copy(KT[:, :], ROWF[:, 0:1].to_broadcast([P, C])))
            for h in range(2):
                st.did(v.memset(msg[h][:, :, F:ACC], 1.0))
            st.settle()

            def msg_pair(t, first):
                for h in range(2):
                    k = t * 2 + h
                    st.settle()
                    hold(dve, "dve", msg_in[h], (t + 1) * 64)
                    if first and h == 0:
                        v.tensor_copy(GB[h][:, 0:NE], FIRST[:, :]).then_inc(first_placed, 1)
                        dve.wait_ge(first_placed, 1)
                    if not (first and h == 0):
                        hold(dve, "dve", msg_scanned, k)
                        hold(dve, "dve", key_spread, t * 2 * TILES + h * TILES)
                    st.did(v.tensor_copy(KEY[:, :], SRC[:, bass.ds(k * C, C)]))
                    st.settle()
                    dve.sem_inc(key_ready, 1)
                    scans(h, cols(GB[h], NE), NE, k, first and h == 0, msg_scanned)
                    st.did(v.tensor_tensor(cols(TH, R), over(COLF[:, 0:R], C, R), spread(ETYP[h][:, :], C, R), ALU.is_equal))
                    hold(dve, "dve", msg_scanned, k + 1)
                    st.settle()
                    xj, xi = cols(OS[h], NE)[:, :, 0:F], cols(IN[h], F)
                    dn, mm = cols(GB[h], F), msg[h][:, :, 0:F]
                    st.did(v.tensor_tensor(cols(TH, R), cols(TH, R), cols(OS[h], NE)[:, :, F:NE], ALU.mult))
                    st.did(v.tensor_scalar(dn, xj, 0.1, 5.0, ALU.mult, ALU.add))
                    if not first:
                        hold(dve, "dve", merged, k * 2 - 2)
                    st.did(v.tensor_tensor(mm, xi, xj, ALU.mult))
                    st.settle()
                    st.did(v.tensor_reduce(DUP[:, :], cols(TH, R), AX.X, ALU.add))
                    st.did(v.scalar_tensor_tensor(out=dn, in0=xi, scalar=0.9, in1=dn, op0=ALU.mult, op1=ALU.add))
                    st.did(v.tensor_tensor(mm, mm, spread(EWT[h][:, :], C, F), ALU.mult))
                    st.settle()
                    st.did(v.tensor_copy(NORM[:, bass.ds(k * C, C)], DUP[:, :]))
                    st.do(v.reciprocal(dn, dn))
                    st.do(v.tensor_tensor(mm, mm, dn, ALU.mult))
                    dve.sem_inc(msg_read, 1)
                    dve.sem_inc(msg_ready, 1)
                    if not (first and h == 0):
                        hold(dve, "dve", merged, k * 2)
                    for g in range(TILES):
                        bank = psW[(h * TILES + g) % 2][:, 0:Q * P].rearrange("p (c k) -> p c k", c=Q)
                        gs = slice(g * Q, (g + 1) * Q)
                        hold(dve, "dve", key_spread, t * 2 * TILES + h * TILES + g + 1)
                        v.tensor_tensor(meq[:, gs, :], bank, spread(KEY[:, gs], Q, P), ALU.is_equal).then_inc(eq_done, 1)
                        hold(dve, "dve", eq_done, t * 2 * TILES + h * TILES + g + 1)
                        st.do(v.tensor_tensor(meq_low, meq[:, gs, :], over(LOWER[:, :], Q, P), ALU.mult))
                        st.did(v.tensor_reduce(DUP[:, gs], meq_low, AX.X, ALU.add))
                    st.settle()
                    st.do(v.tensor_scalar(DUP[:, :], DUP[:, :], 1.0, None, ALU.min))
                    st.do(v.scalar_tensor_tensor(out=TH[:, 0:C], in0=KT[:, :], scalar=float(NPAD), in1=KEY[:, :],
                                                 op0=ALU.add, op1=ALU.subtract))
                    st.do(v.tensor_tensor(DUP[:, :], DUP[:, :], TH[:, 0:C], ALU.mult))
                    if not first:
                        for i in range(2):
                            hold(dve, "dve", scattered[i], t * 16 * C - (1 - h) * 8 * C)
                    v.tensor_tensor(IDX[h][:, :], DUP[:, :], KEY[:, :], ALU.add).then_inc(scat_idx_ready, 1)
                    hold(dve, "dve", scat_idx_ready, k + 1)

            loop_pairs(dve, msg_pair, st)
            dve.wait_ge(merged, 2 * CHUNKS)
            st.do(v.memset(acc_sum, 0.0))
            for r in range(2 * SET):
                dve.wait_ge(acc_loaded[r % 4], 16 * (r // 4 + 1))
                st.do(v.tensor_tensor(acc_sum, acc_sum, acc_in[r % 4], ALU.add))
                signal(acc_used)
            sum3 = acc_sum.rearrange("p (j k) -> p j k", j=NJ)
            st.did(v.tensor_tensor(X3, X3, sum3[:, :, 0:F], ALU.add))
            st.did(v.tensor_copy(OUTDEG[:, :], sum3[:, :, F]))
            st.settle()
            layer_norm()
            signal(lin_in)

            def scan_steps(name, t, h, first):
                k = t * 2 + h

                def quarter(i):
                    if i == 0:
                        hold(dve, "dve", gathered[name][h], (t + 1) * gathers(name))
                        hold(dve, "dve", dense_done, DENSE[name][0] + k + 1)
                        if not first:
                            hold(dve, "dve", stored[name][h], t * 16)
                        if not (first and h == 0):
                            hold(dve, "dve", scanned[name], k)
                    scans(h, cols(GB[h], F), F, k, first and h == 0, scanned[name], range(i * F // 4, (i + 1) * F // 4))

                return [lambda i=i: quarter(i) for i in range(4)]

            def sum3_steps(t, h, first):
                return dict(zip((3, 5, 7, 9), scan_steps("sum3", t, h, first)))

            def conv_steps(name, n):
                n2 = BY_PRODUCT[name]

                def steps(t, h, first):
                    k = t * 2 + h
                    at = (n * CHUNKS + h) * TURNS + t * 2 * TURNS
                    free = first and h == 0 and n == 0
                    hots = TH[:, 0:n2 * R].rearrange("p (c r) -> p c r", r=R)
                    found = GB[h][:, (C - n2) * F:C * F].rearrange("p (c f) -> p c f", f=F)

                    def types():
                        if not free:
                            hold(dve, "dve", typed_turned, at)
                        st.do(v.tensor_scalar(TI[:, 0:n2], RIDX[:, bass.ds(k * C + (C - n2), n2)], R - 1, None, ALU.bitwise_and))
                        st.do(v.tensor_tensor(hots, over(COLF[:, 0:R], n2, R), spread(TI[:, 0:n2], n2, R), ALU.is_equal))

                    def by_types(b):
                        if not (free and b < 2):
                            hold(dve, "dve", typed_turned, at + max(0, b - 1))
                        if b == 0:
                            hold(dve, "dve", dense_done, DENSE[name][0] + k + 1)
                        gs = slice(b * Q, (b + 1) * Q)
                        v.tensor_tensor(by_type[b % 2].rearrange("p (c r f) -> p c r f", c=Q, r=R),
                                        hots[:, gs, :].unsqueeze(3).to_broadcast([P, Q, R, F]),
                                        found[:, gs, :].unsqueeze(2).to_broadcast([P, Q, R, F]), ALU.mult).then_inc(typed_ready, 1)

                    def scale():
                        hold(dve, "dve", gathered[name][h], (t + 1) * gathers(name))
                        hold(dve, "dve", typed_out, n * CHUNKS + k + 1)
                        st.do(v.tensor_tensor(cols(GB[h], F), cols(GB[h], F), spread(NORM[:, bass.ds(k * C, C)], C, F), ALU.mult))

                    order = [types] + [lambda b=b: by_types(b) for b in range(TURNS)] + [scale]
                    return dict(zip((0, 1, 5, 9, 17, 18, 19, 20, 21), order + scan_steps(name, t, h, first)))
                return steps

            def product_pass(name, steps):
                def chunk(t, h, first, last=False, before=None):
                    if not first:
                        hold(dve, "dve", scanned[name], t * 2 + h - 1)
                    dense(name, t, h, before is None, last, lambda n: before[n]() if before and n in before else None)

                def pair(t, first, last=False):
                    chunk(t, 1, first, last, steps(t, 0, first))
                    if last:
                        for step in steps(t, 1, first).values():
                            step()
                    else:
                        chunk(t + 1, 0, False, False, steps(t, 1, first))

                dense_start(name)
                chunk(0, 0, True)
                loop_pairs(dve, pair, st, end=PAIRS - 1)
                pair(PAIRS - 1, False, last=True)

            for n, name in enumerate(("conv1", "conv2")):
                signal(table_ready)
                split_table()
                linear_done(2)
                product_pass(name, conv_steps(name, n))
                finish_segments(name, F, AGG)
                st.do(v.tensor_tensor(AGG[:, :], AGG[:, :], ROOT[:, :], ALU.add))
                st.do(v.tensor_tensor(AGG3, AGG3, over((B1, B2)[n][:, :], NJ, F), ALU.add))
                if n == 0:
                    st.do(v.tensor_scalar(H[:, :], AGG[:, :], 0.0, None, ALU.max))
                    signal(lin_in)
            st.do(v.tensor_reduce(NA[:, :], AGG3, AX.X, ALU.max))
            st.do(v.tensor_tensor(TB3, AGG3, spread(NA[:, :], NJ, F), ALU.subtract))
            ask()
            st.do(v.tensor_reduce(NA[:, :], TA3, AX.X, ALU.add))
            ask()
            st.do(v.tensor_tensor(TB3, TB3, spread(NB[:, :], NJ, F), ALU.subtract))
            st.do(v.tensor_tensor(X[:, :], X[:, :], TB[:, :], ALU.add))
            layer_norm()

            def edge_pass(name, n):
                def mult(t, h, g):
                    at = t * 2 * TILES + (n * CHUNKS + h) * TILES + g
                    hold(dve, "dve", w_ready, at + 1)
                    if g >= 3:
                        hold(dve, "dve", m_reduced, at - 2)
                    bank = psW[(h * TILES + g) % 2][:, :].rearrange("p (c o i) -> p c o i", c=Q, o=F)
                    xs = cols(GB[h], 2 * F)[:, g * Q:(g + 1) * Q, 0:F].unsqueeze(2).to_broadcast([P, Q, F, F])
                    v.tensor_tensor(prod[g % 3].rearrange("p (c o i) -> p c o i", c=Q, o=F), bank, xs, ALU.mult).then_inc(w_used, 1)

                def reduce(t, h, g):
                    hold(dve, "dve", w_used, t * 2 * TILES + (n * CHUNKS + h) * TILES + g + 1)
                    v.tensor_reduce(m_edge[:, g * Q:(g + 1) * Q, :], prod[g % 3].rearrange("p (c o i) -> p c o i", c=Q, o=F),
                                    AX.X, ALU.add).then_inc(m_reduced, 1)

                def amid(t, h, g):
                    chunk0, pair0, half0 = DENSE[name]
                    halves = t * 4 * Q + h * 2 * Q + half0
                    found = cols(GB[h], 2 * F)[:, C - Q:C, 0:F]
                    if g == 4:
                        hot(1, t * Q + h * 2 + pair0 + 2)
                    if 3 <= g < 3 + 2 * Q:
                        m = g - 3
                        hold(dve, "dve", dense_sum, halves + m + 1)
                        o = (found[:, m // 2, :], OTHER[:, m // 2 * F:(m // 2 + 1) * F])[m % 2]
                        v.tensor_reduce(o, psM[:, :].rearrange("p (b x) -> p b x", b=2)[:, :, 0:QB * F]
                                        .rearrange("p b (q f) -> p f b q", f=F), AX.XY, ALU.max).then_inc(dense_read, 1)
                    if g == 3 + 2 * Q:
                        hold(dve, "dve", dense_read, halves + 2 * Q)
                        v.tensor_tensor(found, found, OTHER[:, 0:Q * F].rearrange("p (c f) -> p c f", f=F), ALU.max)\
                            .then_inc(dense_done, 1)

                def pair(t, first, last=False):
                    for h in range(2):
                        k = t * 2 + h
                        hot(0, t * Q + h * 2 + DENSE[name][1] + 1)
                        hold(dve, "dve", gathered[name][h], (t + 1) * gathers(name))
                        if not (first and h == 0):
                            hold(dve, "dve", scanned[name], k)
                        for g in range(TILES):
                            if g == TILES - 1:
                                hold(dve, "dve", dense_done, DENSE[name][0] + k + 1)
                            mult(t, h, g)
                            if g == TILES - 1 and not (last and h == 1):
                                dense_columns(name, t, h + 1)
                            amid(t, h, g)
                            if g > 0:
                                reduce(t, h, g - 1)
                        reduce(t, h, TILES - 1)
                        hold(dve, "dve", m_reduced, t * 2 * TILES + (n * CHUNKS + h + 1) * TILES)
                        rest = slice(0, C - Q)
                        st.did(v.tensor_tensor(m_edge[:, rest, :], m_edge[:, rest, :], cols(GB[h], 2 * F)[:, rest, F:2 * F], ALU.add))
                        st.settle()
                        if not first:
                            hold(dve, "dve", stored[name][h], t * 16)
                        scans(h, m_edge, F, k, first and h == 0, scanned[name])

                dense_columns(name, 0, 0)
                loop_pairs(dve, pair, st, end=PAIRS - 1)
                pair(PAIRS - 1, False, last=True)

            for n, name in enumerate(("edge1", "edge2")):
                signal(lin_in)
                st.did(v.tensor_copy(pair_tab[:, :, 0:F], H3))
                st.settle()
                linear_done(1)
                signal(table_ready)
                dve.wait_ge(table_stored, 16 * (5 + n))
                split_table()
                edge_pass(name, n)
                finish_segments(name, F, AGG)
                st.do(v.tensor_scalar(NA[:, :], CNT[:, :], 1.0, None, ALU.max))
                st.do(v.reciprocal(NA[:, :], NA[:, :]))
                st.do(v.tensor_tensor(AGG3, AGG3, spread(NA[:, :], NJ, F), ALU.mult))
                signal(lin_in)
                linear_done(2)
                st.did(v.tensor_tensor(GI, GI, over(BIH[:, :], NJ, 3 * F), ALU.add))
                st.did(v.tensor_tensor(GH, GH, over(BHH[:, :], NJ, 3 * F), ALU.add))
                st.settle()
                st.do(v.tensor_tensor(GI[:, :, 0:2 * F], GI[:, :, 0:2 * F], GH[:, :, 0:2 * F], ALU.add))
                ask()
                st.do(v.tensor_tensor(TB3, GI[:, :, 0:F], GH[:, :, 2 * F:3 * F], ALU.mult))
                st.do(v.tensor_tensor(TB3, TB3, GI[:, :, 2 * F:3 * F], ALU.add))
                ask()
                st.do(v.tensor_tensor(TB[:, :], H[:, :], TA[:, :], ALU.subtract))
                st.do(v.tensor_tensor(TB3, TB3, GI[:, :, F:2 * F], ALU.mult))
                st.do(v.tensor_tensor(H[:, :], TA[:, :], TB[:, :], ALU.add))
            st.do(v.tensor_tensor(X[:, :], X[:, :], H[:, :], ALU.add))
            layer_norm()
            st.do(v.tensor_scalar(NA[:, :], OUTDEG[:, :], 1.0, None, ALU.max))
            ask()
            st.do(v.reciprocal(NA[:, :], NB[:, :]))
            st.do(v.tensor_tensor(H3, H3, spread(NA[:, :], NJ, F), ALU.mult))
            signal(table_ready)
            split_table()

            product_pass("sum3", sum3_steps)
            finish_segments("sum3", F, AGG)
            st.do(v.tensor_scalar(NA[:, :], CNT[:, :], 1.0, None, ALU.max))
            ask()
            st.do(v.reciprocal(NA[:, :], NB[:, :]))
            st.do(v.tensor_tensor(AGG3, AGG3, spread(NA[:, :], NJ, F), ALU.mult))
            st.do(v.tensor_tensor(X[:, :], X[:, :], AGG[:, :], ALU.add))
            signal(out_ready)


_INS = ['x', 'src', 'dst', 'edge_attr_13', 'edge_type_8', 'edge_weight', 'L1_gnn_W1', 'L1_gnn_root1', 'L1_gnn_b1',
        'L1_gnn_W2', 'L1_gnn_root2', 'L1_gnn_b2', 'L2_gnn_fnet_w1', 'L2_gnn_fnet_b1', 'L2_gnn_fnet_w2',
        'L2_gnn_fnet_b2', 'L2_gnn_gru_w_ih', 'L2_gnn_gru_w_hh', 'L2_gnn_gru_b_ih', 'L2_gnn_gru_b_hh']


def kernel(**inputs):
    import numpy as _np
    import concourse.bacc as _bacc
    from concourse import mybir as _mybir
    from concourse.bass_utils import run_bass_kernel_spmd as _run

    nc = _bacc.Bacc("TRN2", target_bir_lowering=False, num_devices=1)
    rows = {'x': (NPAD, 0), 'src': (EP, N), 'dst': (EP, N), 'edge_attr_13': (EP, 0), 'edge_type_8': (EP, 0),
            'edge_weight': (EP, 0)}
    arrays, args = {}, []
    for name in _INS:
        a = _np.ascontiguousarray(inputs[name])
        if name in rows:
            n, fill = rows[name]
            a = _np.concatenate([a, _np.full((n - a.shape[0],) + a.shape[1:], fill, a.dtype)])
        arrays[f"in_{name}_dram"] = a
        args.append(nc.dram_tensor(f"in_{name}_dram", a.shape, _mybir.dt.from_np(a.dtype), kind="ExternalInput").ap())
    out = nc.dram_tensor("out_0_dram", (N, F), F32, kind="ExternalOutput").ap()
    gnn_kernel(nc, *args, out)
    r = _run(nc, [arrays], core_ids=[0])
    return r.results[0]["out_0_dram"]
```
